# Optimizing a Trainium2 kernel written in Bass

```python
import numpy as np
import jax
import jax.numpy as jnp

def _softmax(x, axis=-1):
    return jax.nn.softmax(x, axis=axis)

def _gelu(x):
    return jax.nn.gelu(x, approximate=True)

def _silu(x):
    return jax.nn.silu(x)

def _sigmoid(x):
    return jax.nn.sigmoid(x)

def _layernorm(x, axis=-1, eps=1e-05):
    m = jnp.mean(x, axis=axis, keepdims=True)
    v = jnp.var(x, axis=axis, keepdims=True)
    return (x - m) / jnp.sqrt(v + eps)

def _scatter_add(tgt, idx, src, axis=0):
    return tgt.at[idx].add(src)

def _segment_sum(src, seg, n):
    return jax.ops.segment_sum(src, seg, n)
kernel_name = 'mk_adj_preln_d4_adj_r2_33a170'

def setup_inputs(seed: int=0):
    np.random.seed(seed)
    _w = jnp.asarray

    def _rec_inputs():
        import jax
        import jax.numpy as jnp
        _gk = jax.random.key(seed)
        x = -0.0002928 + 1 * jax.random.normal(jax.random.fold_in(_gk, 1), (16, 512, 256), jnp.float32)
        _a = jax.random.bernoulli(jax.random.fold_in(_gk, 2), 0.015625, (16, 512, 512))
        adj = _a
        return (x, adj)
    x, adj = _rec_inputs()

    def _L0_gnn_setup():
        import jax, jax.numpy as jnp
        import numpy as np
        QUERY_DIM = 256
        HEADS = 4
        DIM_HEAD = 64
        INNER = HEADS * DIM_HEAD
        B, N = (4, 1024)
        key = jax.random.key(seed)
        ks = jax.random.split(key, 6)
        s = 1.0 / np.sqrt(QUERY_DIM)
        x = jax.random.normal(ks[0], (B, N, QUERY_DIM), dtype=jnp.float32)
        adjacency_mask = jax.random.randint(ks[1], (B, N, N), 0, 2) > 0
        Wq = jax.random.normal(ks[2], (QUERY_DIM, INNER), dtype=jnp.float32) * s
        Wk = jax.random.normal(ks[3], (QUERY_DIM, INNER), dtype=jnp.float32) * s
        Wv = jax.random.normal(ks[4], (QUERY_DIM, INNER), dtype=jnp.float32) * s
        Wo = jax.random.normal(ks[5], (INNER, QUERY_DIM), dtype=jnp.float32) * (1.0 / np.sqrt(INNER))
        bo = jnp.zeros((QUERY_DIM,), dtype=jnp.float32)
        return {'x': x, 'adjacency_mask': adjacency_mask, 'Wq': Wq, 'Wk': Wk, 'Wv': Wv, 'Wo': Wo, 'bo': bo}
    _L0_gnn_all = _L0_gnn_setup()
    _L0_gnn_in = {k: v for k, v in _L0_gnn_all.items() if k in ('Wq', 'Wk', 'Wv', 'Wo', 'bo')}
    del _L0_gnn_all

    def _L1_gnn_setup():
        import jax, jax.numpy as jnp
        import numpy as np
        EMB = 256
        HEADS = 8
        HEAD_DIM = 64
        INNER = HEADS * HEAD_DIM
        B, S = (2, 1024)
        SCALE = HEAD_DIM ** (-0.5)
        MIN_SCORE = -1000000000.0
        LN_EPS = 1e-05
        key = jax.random.key(seed)
        ks = jax.random.split(key, 6)
        x = jax.random.normal(ks[0], (B, S, EMB), dtype=jnp.float32)
        graph_mask = jax.random.uniform(ks[1], (B, S, S)) < 0.05
        gamma = jnp.ones((EMB,), jnp.float32)
        beta = jnp.zeros((EMB,), jnp.float32)
        w_qkv = jax.random.normal(ks[2], (3 * INNER, EMB), jnp.float32) * EMB ** (-0.5)
        w_out = jax.random.normal(ks[3], (EMB, INNER), jnp.float32) * INNER ** (-0.5)
        b_out = jnp.zeros((EMB,), jnp.float32)
        return {'x': x, 'graph_mask': graph_mask, 'gamma': gamma, 'beta': beta, 'w_qkv': w_qkv, 'w_out': w_out, 'b_out': b_out}
    _L1_gnn_all = _L1_gnn_setup()
    _L1_gnn_in = {k: v for k, v in _L1_gnn_all.items() if k in ('gamma', 'beta', 'w_qkv', 'w_out', 'b_out')}
    del _L1_gnn_all

    def _L2_gnn_setup():
        import jax, jax.numpy as jnp
        import numpy as np
        B, N, IN, OUT, H = (16, 512, 256, 256, 4)
        key = jax.random.key(seed)
        ks = jax.random.split(key, 10)
        s = 0.03
        return {'h': jax.random.normal(ks[0], (B, N, IN), jnp.float32), 'adj': jax.random.randint(ks[1], (B, N, N), 0, 2) > 0, 'W': jax.random.normal(ks[2], (H, OUT, IN), jnp.float32) * s, 'bW': jax.random.normal(ks[3], (H, OUT), jnp.float32) * s, 'attn': jax.random.normal(ks[4], (H, OUT, OUT), jnp.float32) * s, 'A_w': jax.random.normal(ks[5], (OUT, OUT * H), jnp.float32) * s, 'fc_w': jax.random.normal(ks[6], (OUT, IN), jnp.float32) * s, 'g1_w': jax.random.normal(ks[7], (OUT, OUT), jnp.float32) * s, 'g2_w': jax.random.normal(ks[8], (OUT, OUT), jnp.float32) * s, 'gbias': jax.random.normal(ks[9], (OUT,), jnp.float32) * s}
    _L2_gnn_all = _L2_gnn_setup()
    _L2_gnn_in = {k: v for k, v in _L2_gnn_all.items() if k in ('W', 'bW', 'attn', 'A_w', 'fc_w', 'g1_w', 'g2_w', 'gbias')}
    del _L2_gnn_all

    def _L3_gnn_setup():
        import jax, jax.numpy as jnp
        import numpy as np
        QUERY_DIM = 256
        HEADS = 4
        DIM_HEAD = 64
        INNER = HEADS * DIM_HEAD
        B, N = (4, 1024)
        key = jax.random.key(seed)
        ks = jax.random.split(key, 6)
        s = 1.0 / np.sqrt(QUERY_DIM)
        x = jax.random.normal(ks[0], (B, N, QUERY_DIM), dtype=jnp.float32)
        adjacency_mask = jax.random.randint(ks[1], (B, N, N), 0, 2) > 0
        Wq = jax.random.normal(ks[2], (QUERY_DIM, INNER), dtype=jnp.float32) * s
        Wk = jax.random.normal(ks[3], (QUERY_DIM, INNER), dtype=jnp.float32) * s
        Wv = jax.random.normal(ks[4], (QUERY_DIM, INNER), dtype=jnp.float32) * s
        Wo = jax.random.normal(ks[5], (INNER, QUERY_DIM), dtype=jnp.float32) * (1.0 / np.sqrt(INNER))
        bo = jnp.zeros((QUERY_DIM,), dtype=jnp.float32)
        return {'x': x, 'adjacency_mask': adjacency_mask, 'Wq': Wq, 'Wk': Wk, 'Wv': Wv, 'Wo': Wo, 'bo': bo}
    _L3_gnn_all = _L3_gnn_setup()
    _L3_gnn_in = {k: v for k, v in _L3_gnn_all.items() if k in ('Wq', 'Wk', 'Wv', 'Wo', 'bo')}
    del _L3_gnn_all
    return {'x': x, 'adj': adj, 'L0_gnn_Wq': _L0_gnn_in['Wq'], 'L0_gnn_Wk': _L0_gnn_in['Wk'], 'L0_gnn_Wv': _L0_gnn_in['Wv'], 'L0_gnn_Wo': _L0_gnn_in['Wo'], 'L0_gnn_bo': _L0_gnn_in['bo'], 'L1_gnn_gamma': _L1_gnn_in['gamma'], 'L1_gnn_beta': _L1_gnn_in['beta'], 'L1_gnn_w_qkv': _L1_gnn_in['w_qkv'], 'L1_gnn_w_out': _L1_gnn_in['w_out'], 'L1_gnn_b_out': _L1_gnn_in['b_out'], 'L2_gnn_W': _L2_gnn_in['W'], 'L2_gnn_bW': _L2_gnn_in['bW'], 'L2_gnn_attn': _L2_gnn_in['attn'], 'L2_gnn_A_w': _L2_gnn_in['A_w'], 'L2_gnn_fc_w': _L2_gnn_in['fc_w'], 'L2_gnn_g1_w': _L2_gnn_in['g1_w'], 'L2_gnn_g2_w': _L2_gnn_in['g2_w'], 'L2_gnn_gbias': _L2_gnn_in['gbias'], 'L3_gnn_Wq': _L3_gnn_in['Wq'], 'L3_gnn_Wk': _L3_gnn_in['Wk'], 'L3_gnn_Wv': _L3_gnn_in['Wv'], 'L3_gnn_Wo': _L3_gnn_in['Wo'], 'L3_gnn_bo': _L3_gnn_in['bo']}

def reference(x, adj, L0_gnn_Wq, L0_gnn_Wk, L0_gnn_Wv, L0_gnn_Wo, L0_gnn_bo, L1_gnn_gamma, L1_gnn_beta, L1_gnn_w_qkv, L1_gnn_w_out, L1_gnn_b_out, L2_gnn_W, L2_gnn_bW, L2_gnn_attn, L2_gnn_A_w, L2_gnn_fc_w, L2_gnn_g1_w, L2_gnn_g2_w, L2_gnn_gbias, L3_gnn_Wq, L3_gnn_Wk, L3_gnn_Wv, L3_gnn_Wo, L3_gnn_bo):
    import jax
    import jax.numpy as jnp

    def _L0_gnn_ref(x, adjacency_mask, Wq, Wk, Wv, Wo, bo):
        import jax, jax.numpy as jnp
        import numpy as np
        QUERY_DIM = 256
        HEADS = 4
        DIM_HEAD = 64
        INNER = HEADS * DIM_HEAD
        B, N = (4, 1024)
        scale = DIM_HEAD ** (-0.5)

        def split_heads(t):
            b, n, _ = t.shape
            return t.reshape(b, n, HEADS, DIM_HEAD).transpose(0, 2, 1, 3)
        q = split_heads(x @ Wq)
        k = split_heads(x @ Wk)
        v = split_heads(x @ Wv)
        sim = jnp.einsum('bhid,bhjd->bhij', q, k) * scale
        neg = -jnp.finfo(sim.dtype).max
        sim = jnp.where(adjacency_mask[:, None, :, :], sim, neg)
        attn = jax.nn.softmax(sim, axis=-1)
        out = jnp.einsum('bhij,bhjd->bhid', attn, v)
        out = out.transpose(0, 2, 1, 3).reshape(x.shape[0], x.shape[1], INNER)
        return out @ Wo + bo

    def _L1_gnn_ref(x, graph_mask, gamma, beta, w_qkv, w_out, b_out):
        import jax, jax.numpy as jnp
        import numpy as np
        EMB = 256
        HEADS = 8
        HEAD_DIM = 64
        INNER = HEADS * HEAD_DIM
        B, S = (2, 1024)
        SCALE = HEAD_DIM ** (-0.5)
        MIN_SCORE = -1000000000.0
        LN_EPS = 1e-05
        bsz, seq_len, _ = x.shape
        mu = jnp.mean(x, axis=-1, keepdims=True)
        var = jnp.mean(jnp.square(x - mu), axis=-1, keepdims=True)
        h = (x - mu) * jax.lax.rsqrt(var + LN_EPS) * gamma + beta
        qkv = h @ w_qkv.T
        q, k, v = jnp.split(qkv, 3, axis=-1)
        q = q.reshape(bsz, seq_len, HEADS, HEAD_DIM)
        k = k.reshape(bsz, seq_len, HEADS, HEAD_DIM)
        v = v.reshape(bsz, seq_len, HEADS, HEAD_DIM)
        scores = jnp.einsum('bihd,bjhd->bhij', q, k) * SCALE
        eye = jnp.eye(seq_len, dtype=bool)[None]
        mask = graph_mask | eye
        scores = jnp.where(mask[:, None], scores, MIN_SCORE)
        probs = jax.nn.softmax(scores, axis=-1)
        out = jnp.einsum('bhij,bjhd->bihd', probs, v)
        out = out.reshape(bsz, seq_len, INNER)
        return out @ w_out.T + b_out

    def _L2_gnn_ref(h, adj, W, bW, attn, A_w, fc_w, g1_w, g2_w, gbias):
        import jax, jax.numpy as jnp
        import numpy as np
        B, N, IN, OUT, H = (16, 512, 256, 256, 4)
        Wh = jnp.einsum('bni,hoi->bhno', h, W) + bW[None, :, None, :]
        e = jnp.einsum('bhno,hop->bhnp', Wh, attn)
        scores = jnp.einsum('bhnp,bhmp->bhnm', e, Wh)
        A_mat = jnp.tanh(jnp.where(adj[:, None, :, :], scores, 0.0))
        hp = jax.nn.relu(jnp.einsum('bhnm,bhmo->bhno', A_mat, Wh))
        cat = jnp.transpose(hp, (0, 2, 1, 3)).reshape(hp.shape[0], hp.shape[2], -1)
        ha = cat @ A_w.T
        hf = h @ fc_w.T
        coeff = jax.nn.sigmoid(hf @ g1_w.T + ha @ g2_w.T + gbias)
        return hf * coeff + ha * (1.0 - coeff)

    def _L3_gnn_ref(x, adjacency_mask, Wq, Wk, Wv, Wo, bo):
        import jax, jax.numpy as jnp
        import numpy as np
        QUERY_DIM = 256
        HEADS = 4
        DIM_HEAD = 64
        INNER = HEADS * DIM_HEAD
        B, N = (4, 1024)
        scale = DIM_HEAD ** (-0.5)

        def split_heads(t):
            b, n, _ = t.shape
            return t.reshape(b, n, HEADS, DIM_HEAD).transpose(0, 2, 1, 3)
        q = split_heads(x @ Wq)
        k = split_heads(x @ Wk)
        v = split_heads(x @ Wv)
        sim = jnp.einsum('bhid,bhjd->bhij', q, k) * scale
        neg = -jnp.finfo(sim.dtype).max
        sim = jnp.where(adjacency_mask[:, None, :, :], sim, neg)
        attn = jax.nn.softmax(sim, axis=-1)
        out = jnp.einsum('bhij,bhjd->bhid', attn, v)
        out = out.transpose(0, 2, 1, 3).reshape(x.shape[0], x.shape[1], INNER)
        return out @ Wo + bo
    h = jnp.maximum(_layernorm(x, axis=-1), 0.0)
    x = x + _L0_gnn_ref(h, adj, L0_gnn_Wq, L0_gnn_Wk, L0_gnn_Wv, L0_gnn_Wo, L0_gnn_bo)
    h = jnp.maximum(_layernorm(x, axis=-1), 0.0)
    x = x + _L1_gnn_ref(h, adj, L1_gnn_gamma, L1_gnn_beta, L1_gnn_w_qkv, L1_gnn_w_out, L1_gnn_b_out)
    h = jnp.maximum(_layernorm(x, axis=-1), 0.0)
    x = x + _L2_gnn_ref(h, adj, L2_gnn_W, L2_gnn_bW, L2_gnn_attn, L2_gnn_A_w, L2_gnn_fc_w, L2_gnn_g1_w, L2_gnn_g2_w, L2_gnn_gbias)
    h = jnp.maximum(_layernorm(x, axis=-1), 0.0)
    x = x + _L3_gnn_ref(h, adj, L3_gnn_Wq, L3_gnn_Wk, L3_gnn_Wv, L3_gnn_Wo, L3_gnn_bo)
    return x

_drawn_inputs = setup_inputs


def setup_inputs(seed=0):
    import zlib

    import numpy as np

    out = dict(_drawn_inputs(seed))
    spreads = {'L0_gnn_bo': (0.0, 0.1),
     'L1_gnn_gamma': (1.0, 0.2),
     'L1_gnn_beta': (0.0, 0.1),
     'L1_gnn_b_out': (0.0, 0.1),
     'L3_gnn_bo': (0.0, 0.1)}
    factors = {'L2_gnn_g1_w': 2.999, 'L2_gnn_gbias': 8.0}
    for name, (base, spread) in spreads.items():
        noise = np.random.default_rng([zlib.crc32(name.encode()), seed]).standard_normal(out[name].shape)
        drawn = base * np.exp(spread * noise) if base else spread * noise
        out[name] = jnp.asarray(drawn.astype(out[name].dtype))
    for name, factor in factors.items():
        out[name] = (out[name] * factor).astype(out[name].dtype)
    return out
```

```python
from contextlib import ExitStack

import concourse.bass as bass
from concourse import mybir

ALU = mybir.AluOpType
ACT = mybir.ActivationFunctionType
F32 = mybir.dt.float32
F32R = mybir.dt.float32r
BF16 = mybir.dt.bfloat16
U8 = mybir.dt.uint8

P = 128
BATCHES = 16
ROWS = 512
DIM = 256
RT = ROWS // P
CT = DIM // P
HEAD = 64
GROUP = 4
PER_LOOP = 2
LOOPS = BATCHES // PER_LOOP
SCALE = HEAD**-0.5
EPS = 1e-5
BIG = 2.0**127
LEAST = 3.0e38

PASSES = ((0, 0), (0, 1), (1, 0))
HI, LO = 0, 1


def own_wait(engine, semaphore, value, passed):
    engine.wait_ge(semaphore, value)
    engine.sem_inc(passed, 1)


def exact(tile):
    return tile.bitcast(F32)


def layer_semaphores(nc, ctx, layer):
    given = []

    def sem(name):
        given.append(nc.alloc_semaphore(name=f"{layer}_{name}"))
        return given[-1]

    def give_back():
        nc.clear_and_free_semaphores(given)
        nc.all_engine_barrier()

    ctx.callback(give_back)
    return sem


def split_weights(nc, block, loads, sems):
    staged_in, hi_made, lo_made = sems

    @block.sync
    def _(sync):
        for n, (moves, _, _, _) in enumerate(loads):
            for to, source in moves:
                sync.dma_start(to, source).then_inc(staged_in[n], 16)

    @block.scalar
    def _(act):
        for n, (moves, staged, hi, _) in enumerate(loads):
            act.wait_ge(staged_in[n], 16 * len(moves))
            nc.scalar.activation(hi, staged, ACT.Copy).then_inc(hi_made, 1)

    @block.vector
    def _(dve):
        for n, (_, staged, hi, lo) in enumerate(loads):
            dve.wait_ge(hi_made, n + 1)
            nc.vector.tensor_tensor(lo, staged, exact(hi), ALU.subtract).then_inc(lo_made, 1)


def identity_matrix(nc, block, ident, made):
    @block.gpsimd
    def _(pool):
        nc.gpsimd.memset(ident, 0.0).then_inc(made, 1)
        pool.wait_ge(made, 1)
        nc.gpsimd.affine_select(
            out=ident, in_=ident, compare_op=ALU.not_equal, fill=1.0, base=0,
            pattern=[[-1, P]], channel_multiplier=1,
        ).then_inc(made, 1)


def attention_layer(nc, layer, x_in, x_out, adj, w_qkv, w_out, b_out, heads, gamma=None, beta=None):
    own_norm = gamma is not None
    inner = heads * HEAD
    pair_groups = heads // GROUP
    SLOTS = PER_LOOP * heads
    HEADS_ALL = BATCHES * heads
    norms = 2 if own_norm else 1
    FIRST = 3

    def refreshes(k):
        return (k // GROUP + 1) * GROUP % heads == 0

    def chunks_of(k):
        return 2 if k % 4 != 1 or refreshes(k) else 0

    def chunks_before(k):
        return 6 + sum(chunks_of(j) for j in range(k))

    CHUNKS = chunks_before(SLOTS) - chunks_before(0)

    def chunk(it, k, part):
        return it * CHUNKS + chunks_before(k) + part

    def head(it, k, times=1, more=0):
        return it * (SLOTS * times) + (k * times + more)

    def batch(it, k, times=1, more=0):
        return it * (PER_LOOP * times) + (k // heads * times + more)

    def exists(it, k):
        return not isinstance(it, int) or it * SLOTS + k < HEADS_ALL

    def front_slot(k):
        return k + 2 if k % 2 == 0 else k + (3 if k % 4 == 1 else 1)

    def front_exists(it, k):
        return chunks_of(k) > 0 and exists(it, front_slot(k))

    with ExitStack() as ctx:
        def sb(name, shape, dt):
            return ctx.enter_context(nc.sbuf_tensor(f"{layer}_{name}", shape, dt))

        def psum(name, shape):
            return ctx.enter_context(nc.psum_tensor(f"{layer}_{name}", shape, F32))

        sem = layer_semaphores(nc, ctx, layer)

        wqkv = [sb(f"wqkv{i}", [P, CT, 3, inner], F32R) for i in (HI, LO)]
        wout = [sb(f"wout{i}", [P, heads, DIM], F32R) for i in (HI, LO)]
        bias_row = sb("bias_row", [P, DIM], F32)
        affine = sb("affine", [P, 2, CT], F32)
        ident = sb("ident", [P, P], F32)
        minus_half = sb("minus_half", [P, RT], F32)

        x_sb = sb("x_sb", [P, PER_LOOP, RT, DIM], F32)
        res = sb("res", [P, PER_LOOP, RT, DIM], F32)
        adj_sb = sb("adj_sb", [P, PER_LOOP, RT, ROWS], U8)
        mask = sb("mask", [P, PER_LOOP, RT, ROWS], BF16)
        stats = sb("stats", [P, RT, 6], F32)
        mean_var = sb("mean_var", [P, RT, 2], F32)
        var_eps = sb("var_eps", [P, RT], F32)
        rstd = sb("rstd", [P, RT], F32)
        normed_x = sb("normed_x", [P, RT, DIM], F32)
        hT_full = sb("hT_full", [P, CT, ROWS], F32)
        hT = [sb(f"hT{i}", [P, CT, ROWS], F32R) for i in (HI, LO)]
        qT = [sb(f"qT{i}", [P, 2, ROWS], F32R) for i in (HI, LO)]
        kT = [sb(f"kT{i}", [P, 2, ROWS], F32R) for i in (HI, LO)]
        v_sb = sb("v_sb", [P, 2, RT, GROUP, 2 * HEAD], F32R)
        probs = sb("probs", [P, 2, RT, ROWS], F32)
        row_shift = sb("row_shift", [P, 2, RT], F32)
        row_sum = sb("row_sum", [P, 2, RT], F32)
        row_recip = sb("row_recip", [P, 2, RT], F32)
        pT = [sb(f"pT{i}", [P, RT, ROWS], F32R) for i in (HI, LO)]
        oT = [sb(f"oT{i}", [P, ROWS], F32R) for i in (HI, LO)]

        scores_ps = psum("scores_ps", [P, 2, ROWS])
        pT_ps = psum("pT_ps", [P, 2, ROWS])
        front_ps = psum("front_ps", [P, ROWS])
        oT_ps = psum("oT_ps", [P, ROWS])
        y_ps = psum("y_ps", [P, RT, DIM])

        consts_in = sem("consts_in")
        ident_made = sem("ident_made")
        passed = sem("passed")
        exponent_made = sem("exponent_made")
        staged_in = [sem(f"staged_in{n}") for n in range(2)]
        weights_hi = sem("weights_hi")
        weights_lo = sem("weights_lo")
        x_loaded = [sem(f"x_loaded{i}") for i in range(PER_LOOP)]
        adj_loaded = [sem(f"adj_loaded{i}") for i in range(PER_LOOP)]
        stored = [sem(f"stored{i}") for i in range(PER_LOOP)]
        mask_blank = sem("mask_blank")
        mask_ready = sem("mask_ready")
        stats_done = sem("stats_done")
        mean_var_done = sem("mean_var_done")
        var_eps_done = sem("var_eps_done")
        rstd_done = sem("rstd_done")
        centred = sem("centred")
        rectified = sem("rectified")
        normed_done = sem("normed_done")
        res_ready = sem("res_ready")
        front_done = sem("front_done")
        front_hi = sem("front_hi")
        front_read = sem("front_read")
        hT_ready = sem("hT_ready")
        scores_done = sem("scores_done")
        masked = sem("masked")
        exp_done = sem("exp_done")
        recip_done = sem("recip_done")
        probs_ready = sem("probs_ready")
        pT_done = sem("pT_done")
        pT_hi = sem("pT_hi")
        pT_lo = sem("pT_lo")
        oT_done = sem("oT_done")
        oT_hi = sem("oT_hi")
        oT_lo = sem("oT_lo")
        y_done = sem("y_done")
        y_added = sem("y_added")

        rows = "b (t p) c -> b p t c"
        x_src = x_in.rearrange(rows, p=P)
        x_dst = x_out.rearrange(rows, p=P)
        adj_src = adj.rearrange(rows, p=P)

        with nc.Block() as block:
            w_stage = probs[:].rearrange("p a t r -> p (a t r)")[:, 0:CT * 3 * inner]
            o_stage = res[:].rearrange("p a t c -> p (a t c)")[:, 0:heads * DIM]
            w_view = w_qkv.rearrange("(t p) a n -> p t (a n)", p=P)
            o_view = w_out.rearrange("(h d) c -> d h c", d=HEAD)
            split_weights(nc, block, [
                ([(w_stage.rearrange("p (t n) -> p t n", t=CT), w_view)], w_stage,
                 wqkv[HI][:].rearrange("p t a n -> p (t a n)"), wqkv[LO][:].rearrange("p t a n -> p (t a n)")),
                ([(o_stage[h * HEAD:(h + 1) * HEAD].rearrange("p (h c) -> p h c", h=heads), o_view)
                  for h in range(2)], o_stage,
                 wout[HI][:].rearrange("p h c -> p (h c)"), wout[LO][:].rearrange("p h c -> p (h c)")),
            ], (staged_in, weights_hi, weights_lo))
            identity_matrix(nc, block, ident[:], ident_made)

            @block.sync
            def _(sync):
                sync.dma_start(bias_row[:], b_out.rearrange("(a c) -> a c", a=1).to_broadcast([P, DIM])).then_inc(consts_in, 16)
                if own_norm:
                    with nc.allow_non_contiguous_dma(reason="one column of channels"):
                        for n, v in enumerate((gamma, beta)):
                            sync.dma_start(affine[:, n, :], v.rearrange("(t p) -> p t", p=P)).then_inc(consts_in, 16)

                def load(it, b, source):
                    sync.dma_start(x_sb[:, b], x_src[source]).then_inc(x_loaded[b], 16)
                    sync.dma_start(adj_sb[:, b], adj_src[source]).then_inc(adj_loaded[b], 16)

                def store(it, b, to, count):
                    sync.wait_ge(y_added, count)
                    sync.dma_start(x_dst[to], res[:, b]).then_inc(stored[b], 16)

                for b in range(PER_LOOP):
                    sync.sem_inc(stored[b], 16)
                    load(0, b, b)
                with sync.Fori(0, LOOPS - 1) as it:
                    for b in range(PER_LOOP):
                        sync.wait_ge(res_ready, it * PER_LOOP + (b + 1))
                        sync.wait_ge(mask_ready, it * PER_LOOP + (b + 1))
                        load(it, b, it * PER_LOOP + (b + PER_LOOP))
                        store(it, b, it * PER_LOOP + b, it * (2 * PER_LOOP) + (2 * b + 2))
                for b in range(PER_LOOP):
                    store(0, b, BATCHES - PER_LOOP + b, 2 * (BATCHES - PER_LOOP + b + 1))
                for b in range(PER_LOOP):
                    sync.wait_ge(stored[b], 16 * LOOPS + 16)

            @block.gpsimd
            def _(pool):
                nc.gpsimd.memset(minus_half[:], -0.5).then_inc(exponent_made, 1)

                def make_mask(it, k):
                    b = k // heads % PER_LOOP
                    own_wait(pool, adj_loaded[b], it * 16 + (k // SLOTS * 16 + 16), passed)
                    if not isinstance(it, int) or it * PER_LOOP + k // heads >= PER_LOOP:
                        own_wait(pool, masked, batch(it, k, RT * heads, 1 - RT * heads), passed)
                    convert = nc.gpsimd.tensor_scalar(mask[:, b], adj_sb[:, b], -1.0, BIG, ALU.add, ALU.mult)
                    if own_norm:
                        convert.then_inc(mask_blank, 1)
                        own_wait(pool, mask_blank, batch(it, k, 1, 1), passed)
                        nc.gpsimd.affine_select(
                            out=mask[:, b], in_=mask[:, b], compare_op=ALU.not_equal, fill=0.0, base=0,
                            pattern=[[P, RT], [-1, ROWS]], channel_multiplier=1,
                        ).then_inc(mask_ready, 1)
                    else:
                        convert.then_inc(mask_ready, 1)

                def rstd_step(it, k, n):
                    own_wait(pool, mean_var_done, batch(it, k, norms, n + 1), passed)
                    nc.gpsimd.tensor_scalar(var_eps[:], mean_var[:, :, 1], EPS, 1.0, ALU.add, ALU.mult).then_inc(var_eps_done, 1)
                    pool.wait_ge(var_eps_done, batch(it, k, norms, n + 1))
                    nc.gpsimd.tensor_tensor(rstd[:], var_eps[:], minus_half[:], ALU.pow).then_inc(rstd_done, 1)

                def residual(it, k):
                    b = k // heads % PER_LOOP
                    pool.wait_ge(stored[b], it * 16 + (k // SLOTS * 16 + 16))
                    nc.gpsimd.tensor_tensor(
                        res[:, b], x_sb[:, b], bias_row[:].unsqueeze(1).to_broadcast([P, RT, DIM]), ALU.add,
                    ).then_inc(res_ready, 1)

                def hT_rest(it, k, first):
                    for part in range(CT):
                        pool.wait_ge(front_hi, first + (part + 1))
                        nc.gpsimd.tensor_tensor(
                            hT[LO][:, part], hT_full[:, part], exact(hT[HI][:, part]), ALU.subtract,
                        ).then_inc(hT_ready, 1)

                def normalise(it, k):
                    own_wait(pool, recip_done, head(it, k, 1, 1), passed)
                    for q in range(RT):
                        part = probs[:, k % 2, q]
                        nc.gpsimd.tensor_scalar(
                            part, part, row_recip[:, k % 2, q:q + 1], 1.0, ALU.mult, ALU.mult,
                        ).then_inc(probs_ready, 1)

                def slot(it, k):
                    s, ahead = k % 4, refreshes(k) and exists(it, k + GROUP)
                    nxt = k + GROUP
                    if ahead and s == 0:
                        for n in range(norms):
                            rstd_step(it, nxt, n)
                    if ahead and s == 1:
                        make_mask(it, nxt)
                    if exists(it, k + 1):
                        normalise(it, k + 1)
                    if ahead and s == 1:
                        hT_rest(it, nxt, chunk(it, k, 0))
                    if ahead and s == 3:
                        residual(it, nxt)

                pool.wait_ge(exponent_made, 1)
                pool.wait_ge(consts_in, 48 if own_norm else 16)
                for n in range(norms):
                    rstd_step(0, 0, n)
                make_mask(0, 0)
                hT_rest(0, 0, 0)
                pool.wait_ge(weights_lo, 2)
                residual(0, 0)
                normalise(0, 0)
                for k in range(FIRST):
                    slot(0, k)
                with pool.Fori(0, LOOPS - 1) as it:
                    for k in range(FIRST, SLOTS + FIRST):
                        slot(it, k)
                for k in range(FIRST, SLOTS + 2):
                    slot(LOOPS - 1, k)

            @block.scalar
            def _(act):
                def front(it, k, s, first):
                    for part in range(2):
                        act_front(k, s, part, first)

                def act_front(k, s, part, first):
                    if s == 1:
                        act.wait_ge(front_read, first + (part + 1))
                        nc.scalar.activation(hT[HI][:, part], hT_full[:, part], ACT.Copy).then_inc(front_hi, 1)
                        return
                    act.wait_ge(front_done, first + (part + 1))
                    if s in (0, 2):
                        to, source = (qT, kT)[part][HI][:, k // 2 % 2], front_ps[:]
                    else:
                        to = v_sb[:, k // GROUP % 2, 2 * part:2 * part + 2, :, 0:HEAD]
                        source = front_ps[:].rearrange("p (t h d) -> p t h d", t=2, h=GROUP)
                    nc.scalar.activation(to, source, ACT.Copy).then_inc(front_hi, 1)

                def exps(it, k):
                    for q in range(RT):
                        part = probs[:, k % 2, q]
                        act.wait_ge(masked, head(it, k, RT, q + 1))
                        nc.scalar.activation(
                            part, part, ACT.Exp, bias=row_shift[:, k % 2, q:q + 1], scale=-1.0,
                            accum_out=row_sum[:, k % 2, q:q + 1],
                        ).then_inc(exp_done, 1)

                def slot(it, k):
                    s = k % 4
                    if exists(it, k + 1):
                        exps(it, k + 1)
                    has = front_exists(it, k)
                    target = front_slot(k)
                    first = chunk(it, k, 0)
                    for part in range(2):
                        if has:
                            act_front(target, s, part, first)
                        if exists(it, k):
                            for t in (2 * part, 2 * part + 1):
                                act.wait_ge(pT_done, head(it, k, RT, t + 1))
                                nc.scalar.activation(pT[HI][:, t], pT_ps[:, t % 2], ACT.Copy).then_inc(pT_hi, 1)
                    if k >= 1 and exists(it, k - 1):
                        act.wait_ge(oT_done, head(it, k))
                        nc.scalar.activation(oT[HI][:], oT_ps[:], ACT.Copy).then_inc(oT_hi, 1)

                for n, s in enumerate((1, 0, 3)):
                    front(0, 0, s, 2 * n)
                exps(0, 0)
                for k in range(FIRST):
                    slot(0, k)
                with act.Fori(0, LOOPS - 1) as it:
                    for k in range(FIRST, SLOTS + FIRST):
                        slot(it, k)
                for k in range(FIRST, SLOTS + 2):
                    slot(LOOPS - 1, k)

            @block.vector
            def _(dve):
                def front(it, k, s, part, first):
                    if s == 1:
                        before = batch(it, k, CT)
                        if not isinstance(before, int) or before > 0:
                            dve.wait_ge(hT_ready, before)
                        dve.wait_ge(front_done, first + (part + 1))
                        to, source = hT_full[:, part], front_ps[:]
                        if own_norm:
                            step = nc.vector.tensor_scalar(to, source, affine[:, 0, part:part + 1],
                                                           affine[:, 1, part:part + 1], ALU.mult, ALU.add)
                        else:
                            step = nc.vector.tensor_scalar(to, source, 0.0, None, ALU.max)
                        step.then_inc(front_read, 1)
                        return
                    dve.wait_ge(front_hi, first + (part + 1))
                    if s in (0, 2):
                        half = (qT, kT)[part]
                        to, hi, source = half[LO][:, k // 2 % 2], half[HI][:, k // 2 % 2], front_ps[:]
                    else:
                        both = v_sb[:, k // GROUP % 2, 2 * part:2 * part + 2]
                        to, hi = both[:, :, :, HEAD:], both[:, :, :, 0:HEAD]
                        source = front_ps[:].rearrange("p (t h d) -> p t h d", t=2, h=GROUP)
                    nc.vector.tensor_tensor(to, source, exact(hi), ALU.subtract).then_inc(front_read, 1)

                def mean_and_variance(it, k, n, rows_):
                    for q in range(RT):
                        step = nc.vector.bn_stats(stats[:, q], rows_[:, q])
                    step.then_inc(stats_done, 1)
                    own_wait(dve, stats_done, batch(it, k, norms, n + 1), passed)
                    for q in range(RT):
                        step = nc.vector.bn_aggr(mean_var[:, q], stats[:, q])
                    step.then_inc(mean_var_done, 1)

                def centre(it, k, n, rows_, signal):
                    dve.wait_ge(rstd_done, batch(it, k, norms, n + 1))
                    for q in range(RT):
                        step = nc.vector.tensor_scalar(normed_x[:, q], rows_[:, q], mean_var[:, q, 0:1],
                                                       rstd[:, q:q + 1], ALU.subtract, ALU.mult)
                    step.then_inc(signal, 1)

                def norm_first(it, k):
                    b = k // heads % PER_LOOP
                    dve.wait_ge(x_loaded[b], it * 16 + (k // SLOTS * 16 + 16))
                    mean_and_variance(it, k, 0, x_sb[:, b])

                def norm_middle(it, k):
                    b = k // heads % PER_LOOP
                    if own_norm:
                        centre(it, k, 0, x_sb[:, b], centred)
                        dve.wait_ge(centred, batch(it, k, 1, 1))
                        nc.vector.tensor_scalar(normed_x[:], normed_x[:], 0.0, None, ALU.max).then_inc(rectified, 1)
                        dve.wait_ge(rectified, batch(it, k, 1, 1))
                        mean_and_variance(it, k, 1, normed_x)

                def norm_last(it, k):
                    b = k // heads % PER_LOOP
                    centre(it, k, norms - 1, normed_x if own_norm else x_sb[:, b], normed_done)

                def mask_scores(it, k):
                    b = k // heads % PER_LOOP
                    if k % heads == 0:
                        dve.wait_ge(mask_ready, batch(it, k, 1, 1))
                    for q in range(RT):
                        own_wait(dve, scores_done, head(it, k, RT, q + 1), passed)
                        nc.vector.tensor_tensor_reduce(
                            probs[:, k % 2, q], scores_ps[:, q % 2], mask[:, b, q], -SCALE, LEAST,
                            ALU.add, ALU.min, row_shift[:, k % 2, q:q + 1],
                        ).then_inc(masked, 1)

                def recip(it, k):
                    dve.wait_ge(exp_done, head(it, k, RT, RT))
                    nc.vector.reciprocal(row_recip[:, k % 2], row_sum[:, k % 2]).then_inc(recip_done, 1)

                def add_attention(it, k):
                    b = k // heads % PER_LOOP
                    dve.wait_ge(y_done, batch(it, k, 1, 1))
                    dve.wait_ge(res_ready, batch(it, k, 1, 1))
                    for half in range(2):
                        part = slice(2 * half, 2 * half + 2)
                        nc.vector.tensor_tensor(res[:, b, part], y_ps[:, part], res[:, b, part], ALU.add).then_inc(y_added, 1)

                def slot(it, k):
                    s, ahead = k % 4, refreshes(k) and exists(it, k + GROUP)
                    nxt = k + GROUP
                    if exists(it, k + 1):
                        mask_scores(it, k + 1)
                    if ahead and s == 0:
                        norm_first(it, nxt)
                    has = front_exists(it, k)
                    first = chunk(it, k, 0)
                    for part in range(2):
                        if has:
                            front(it, front_slot(k), s, part, first)
                        if exists(it, k + 1) and part == 0:
                            recip(it, k + 1)
                        if exists(it, k):
                            for t in (2 * part, 2 * part + 1):
                                dve.wait_ge(pT_hi, head(it, k, RT, t + 1))
                                nc.vector.tensor_tensor(pT[LO][:, t], pT_ps[:, t % 2], exact(pT[HI][:, t]), ALU.subtract).then_inc(pT_lo, 1)
                        if ahead and s == 0:
                            (norm_middle if part == 0 else norm_last)(it, nxt)
                    if k >= 2 and (k - 2) % heads == heads - 1:
                        add_attention(it, k - 2)
                    if k >= 1 and exists(it, k - 1):
                        dve.wait_ge(oT_hi, head(it, k))
                        nc.vector.tensor_tensor(oT[LO][:], oT_ps[:], exact(oT[HI][:]), ALU.subtract).then_inc(oT_lo, 1)

                norm_first(0, 0)
                norm_middle(0, 0)
                norm_last(0, 0)
                dve.wait_ge(consts_in, 48 if own_norm else 16)
                for n, s in enumerate((1, 0, 3)):
                    for part in range(2):
                        front(0, 0, s, part, 2 * n)
                mask_scores(0, 0)
                recip(0, 0)
                for k in range(FIRST):
                    slot(0, k)
                with dve.Fori(0, LOOPS - 1) as it:
                    for k in range(FIRST, SLOTS + FIRST):
                        slot(it, k)
                for k in range(FIRST, SLOTS + 2):
                    slot(LOOPS - 1, k)

            @block.tensor
            def _(pe):
                def front_hT(it, k, part, c):
                    if part == 0:
                        pe.wait_ge(normed_done, batch(it, k, 1, 1))
                    for q in range(RT):
                        mm = nc.tensor.transpose(front_ps[:, q * P:(q + 1) * P], normed_x[:, q, part * P:(part + 1) * P], ident[:])
                    return mm

                def front_qk(it, k, part, c):
                    if part == 0:
                        pe.wait_ge(hT_ready, batch(it, k, CT, CT))
                    at = k // 2 * P % inner
                    for n, (i, j) in enumerate(PASSES):
                        for t in range(CT):
                            mm = nc.tensor.matmul(front_ps[:], wqkv[i][:, t, part, at:at + P], hT[j][:, t],
                                                  start=(n + t == 0), stop=(n == 2 and t == CT - 1))
                    return mm

                def front_v(it, k, part, c):
                    at = k // GROUP * GROUP * HEAD % inner
                    for m in range(2):
                        q = 2 * part + m
                        for n, (i, j) in enumerate(PASSES):
                            for t in range(CT):
                                mm = nc.tensor.matmul(
                                    front_ps[:, m * DIM:(m + 1) * DIM], hT[i][:, t, q * P:(q + 1) * P],
                                    wqkv[j][:, t, 2, at:at + GROUP * HEAD],
                                    start=(n + t == 0), stop=(n == 2 and t == CT - 1))
                    return mm

                def front(it, k, s, part, c):
                    if not isinstance(c, int) or c >= 1:
                        pe.wait_ge(front_read, c)
                    mm = {0: front_qk, 1: front_hT, 2: front_qk, 3: front_v}[s](it, k, part, c)
                    mm.then_inc(front_done, 1)

                def scores(it, k, c):
                    if k % 2 == 0:
                        pe.wait_ge(front_read, c)
                    at, pair = k % 2 * HEAD, k // 2 % 2
                    for q in range(RT):
                        tile = head(it, k, RT, q - 1)
                        if not isinstance(tile, int) or tile > 0:
                            pe.wait_ge(masked, tile)
                        for n, (i, j) in enumerate(PASSES):
                            mm = nc.tensor.matmul(
                                scores_ps[:, q % 2], qT[i][at:at + HEAD, pair, q * P:(q + 1) * P],
                                kT[j][at:at + HEAD, pair], start=(n == 0), stop=(n == 2))
                        mm.then_inc(scores_done, 1)

                def transpose(it, k, t):
                    if t == 0:
                        pe.wait_ge(probs_ready, head(it, k, RT, RT))
                    tile = head(it, k, RT, t - 1)
                    if not isinstance(tile, int) or tile > 0:
                        pe.wait_ge(pT_lo, tile)
                    for q in range(RT):
                        mm = nc.tensor.transpose(pT_ps[:, t % 2, q * P:(q + 1) * P],
                                                 probs[:, k % 2, q, t * P:(t + 1) * P], ident[:])
                    mm.then_inc(pT_done, 1)

                def times_values(it, k, t, c):
                    if t == 0:
                        if k % GROUP == 0:
                            pe.wait_ge(front_read, c)
                        before = head(it, k)
                        if not isinstance(before, int) or before > 0:
                            pe.wait_ge(oT_lo, before)
                    pe.wait_ge(pT_lo, head(it, k, RT, t + 1))
                    for i in (HI, LO):
                        mm = nc.tensor.matmul(oT_ps[:], v_sb[:, k // GROUP % 2, t, k % GROUP], pT[i][:, t],
                                              start=(t == 0 and i == HI), stop=(t == RT - 1 and i == LO))
                    if t == RT - 1:
                        mm.then_inc(oT_done, 1)

                def project(it, k):
                    h = k % heads
                    pe.wait_ge(oT_lo, head(it, k, 1, 1))
                    if h == 0:
                        before = batch(it, k, 2, 0)
                        if not isinstance(before, int) or before > 0:
                            pe.wait_ge(y_added, before)
                    for q in range(RT):
                        for n, (i, j) in enumerate(PASSES):
                            mm = nc.tensor.matmul(
                                y_ps[:, q], oT[i][:, q * P:(q + 1) * P], wout[j][:, h],
                                start=(h == 0 and q % 2 == 0 and n == 0), stop=(h == heads - 1 and n == 2),
                                skip_group_check=True)
                    if h == heads - 1:
                        mm.then_inc(y_done, 1)

                def slot(it, k):
                    s = k % 4
                    if exists(it, k + 1):
                        scores(it, k + 1, chunk(it, k - 1, 2) if k % 2 else 0)
                    if k >= 2:
                        project(it, k - 2)
                    has = front_exists(it, k)
                    for part in range(2):
                        if has:
                            front(it, front_slot(k), s, part, chunk(it, k, part))
                        for t in (2 * part, 2 * part + 1):
                            if k >= 1 and exists(it, k - 1):
                                times_values(it, k - 1, t, chunk(it, k - 2, 2) if k >= 2 else 6)
                            if exists(it, k):
                                transpose(it, k, t)

                pe.wait_ge(ident_made, 2)
                for part in range(CT):
                    front(0, 0, 1, part, part)
                pe.wait_ge(weights_lo, 2)
                for n, s in enumerate((0, 3)):
                    for part in range(2):
                        front(0, 0, s, part, 2 * n + 2 + part)
                scores(0, 0, 4)
                for k in range(FIRST):
                    slot(0, k)
                with pe.Fori(0, LOOPS - 1) as it:
                    for k in range(FIRST, SLOTS + FIRST):
                        slot(it, k)
                for k in range(FIRST, SLOTS + 2):
                    slot(LOOPS - 1, k)


def gated_layer(nc, layer, x_in, x_out, adj_t, w_rows, w_cols, attn_t, b_heads, mix, small, gate_bias):
    HEADS = w_rows.shape[1]
    GR = DIM + 1
    SLOTS = PER_LOOP * HEADS
    HEADS_ALL = BATCHES * HEADS
    FIRST = HEADS
    FC, G1, G2 = range(3)

    with ExitStack() as ctx:
        sem = layer_semaphores(nc, ctx, layer)

        def sb(name, shape, dt, to=ctx):
            return to.enter_context(nc.sbuf_tensor(f"{layer}_{name}", shape, dt))

        w_sb = [sb(f"w{i}", [P, CT, HEADS * DIM], F32R) for i in (HI, LO)]
        gw_sb = [sb(f"gw{i}", [P, CT, HEADS, DIM], F32R) for i in (HI, LO)]
        mix_sb = [sb(f"mix{i}", [P, HEADS * CT, DIM], F32R) for i in (HI, LO)]
        small_sb = [sb(f"small{i}", [P, 3, CT, DIM], F32R) for i in (HI, LO)]
        wh_bias = sb("wh_bias", [P, HEADS * DIM], F32)
        s_weights = sb("s_weights", [P, CT, HEADS], F32)
        g_bias = sb("g_bias", [P, CT, HEADS], F32)
        s_bias = sb("s_bias", [P, HEADS], F32)
        half_gate_bias = sb("half_gate_bias", [P, CT], F32)
        ident = sb("ident", [P, P], F32)
        minus_half = sb("minus_half", [P, RT], F32)

        with ExitStack() as pre:
            w_stage = sb("w_stage", [P, CT * HEADS * DIM], F32, pre)
            mix_stage = sb("mix_stage", [P, HEADS * CT * DIM], F32, pre)
            small_stage = sb("small_stage", [P, 3 * CT * DIM], F32, pre)
            wb = sb("wb", [P, CT, HEADS, GR], F32, pre)
            attn_sb = sb("attn_sb", [P, CT, HEADS, DIM], F32, pre)
            aw = sb("aw", [P, CT, HEADS, GR], F32, pre)
            b_attn_b = sb("b_attn_b", [P, CT, HEADS], F32, pre)
            gate_bias_sb = sb("gate_bias_sb", [P, CT], F32, pre)
            ones = sb("ones", [P, P], F32, pre)
            banks = pre.enter_context(nc.psum_tensor(f"{layer}_banks", [P, 2 * HEADS, ROWS], F32))

            staged_in = [sem(f"staged_in{n}") for n in range(3)]
            rows_in = sem("rows_in")
            biases_in = sem("biases_in")
            weights_hi = sem("weights_hi")
            weights_lo = sem("weights_lo")
            ident_made = sem("ident_made")
            ones_made = sem("ones_made")
            aw_done = sem("aw_done")
            aw_kept = sem("aw_kept")
            gw_done = sem("gw_done")
            gw_hi = sem("gw_hi")
            gw_lo = sem("gw_lo")
            b_attn_b_made = sem("b_attn_b_made")
            vectors_done = sem("vectors_done")
            vectors_kept = sem("vectors_kept")

            with nc.Block() as block:
                @block.sync
                def _(sync):
                    with nc.allow_non_contiguous_dma(reason="columns of biases"):
                        for t in range(CT):
                            sync.dma_start(wb[:, t, :, 0:DIM], w_rows[t * P:(t + 1) * P]).then_inc(rows_in, 16)
                            sync.dma_start(wb[:, t, :, DIM], b_heads[:, t * P:(t + 1) * P].rearrange("h p -> p h")).then_inc(rows_in, 16)
                        sync.dma_start(attn_sb[:], attn_t.rearrange("(t p) h o -> p t h o", p=P)).then_inc(rows_in, 16)
                        sync.dma_start(gate_bias_sb[:], gate_bias.rearrange("(t p) -> p t", p=P)).then_inc(biases_in, 16)
                    sync.dma_start(wh_bias[:], b_heads.rearrange("h o -> (h o)").rearrange("(a n) -> a n", a=1).to_broadcast([P, HEADS * DIM])).then_inc(biases_in, 16)

                split_weights(nc, block, [
                    ([(w_stage[:].rearrange("p (t n) -> p t n", t=CT), w_cols.rearrange("(t p) n -> p t n", p=P))],
                     w_stage[:], *(w[:].rearrange("p t n -> p (t n)") for w in w_sb)),
                    ([(mix_stage[:].rearrange("p (t n) -> p t n", t=HEADS * CT), mix.rearrange("(t p) n -> p t n", p=P))],
                     mix_stage[:], *(w[:].rearrange("p t n -> p (t n)") for w in mix_sb)),
                    ([(small_stage[:].rearrange("p (a t n) -> p a t n", a=3, t=CT)[:, a], w.rearrange("(t p) n -> p t n", p=P))
                      for a, w in enumerate(small)],
                     small_stage[:], *(w[:].rearrange("p a t n -> p (a t n)") for w in small_sb)),
                ], (staged_in, weights_hi, weights_lo))
                identity_matrix(nc, block, ident[:], ident_made)

                @block.gpsimd
                def _(pool):
                    nc.gpsimd.memset(ones[:], 1.0).then_inc(ones_made, 1)
                    nc.gpsimd.memset(minus_half[:], -0.5).then_inc(ones_made, 1)

                @block.tensor
                def _(pe):
                    pe.wait_ge(rows_in, 80)
                    for h in range(HEADS):
                        for o in range(CT):
                            for t in range(CT):
                                mm = nc.tensor.matmul(banks[:, h * CT + o, 0:GR], attn_sb[:, t, h, o * P:(o + 1) * P],
                                                      wb[:, t, h], start=(t == 0), stop=(t == CT - 1))
                            mm.then_inc(aw_done, 1)
                    for h in range(HEADS):
                        pe.wait_ge(aw_kept, CT * (h + 1))
                        for i in range(CT):
                            for t in range(CT):
                                mm = nc.tensor.matmul(banks[:, h * CT + i, 0:GR], aw[:, t, h, i * P:(i + 1) * P],
                                                      wb[:, t, h], start=(t == 0), stop=(t == CT - 1))
                            mm.then_inc(gw_done, 1)
                    pe.wait_ge(gw_lo, CT)
                    for i in range(CT):
                        for h in range(HEADS):
                            for t in range(CT):
                                nc.tensor.matmul(banks[:, 0, i * HEADS + h:i * HEADS + h + 1], wb[:, t, h, i * P:(i + 1) * P],
                                                 aw[:, t, h, DIM:GR], start=(t == 0), stop=(t == CT - 1))
                    pe.wait_ge(b_attn_b_made, 1)
                    pe.wait_ge(ones_made, 1)
                    for t in range(CT):
                        mm = nc.tensor.matmul(banks[:, 1, 0:HEADS], ones[:], b_attn_b[:, t], start=(t == 0), stop=(t == CT - 1))
                    mm.then_inc(vectors_done, 1)

                @block.scalar
                def _(act):
                    for h in range(HEADS):
                        for i in range(CT):
                            act.wait_ge(gw_done, h * CT + i + 1)
                            nc.scalar.activation(gw_sb[HI][:, i, h], banks[:, h * CT + i, 0:DIM], ACT.Copy).then_inc(gw_hi, 1)
                    act.wait_ge(biases_in, 32)
                    nc.scalar.activation(half_gate_bias[:], gate_bias_sb[:], ACT.Copy, scale=0.5)

                @block.vector
                def _(dve):
                    for h in range(HEADS):
                        for o in range(CT):
                            dve.wait_ge(aw_done, h * CT + o + 1)
                            nc.vector.tensor_copy(aw[:, o, h], banks[:, h * CT + o, 0:GR]).then_inc(aw_kept, 1)
                    dve.wait_ge(rows_in, 80)
                    dve.wait_ge(aw_kept, HEADS * CT)
                    nc.vector.tensor_tensor(b_attn_b[:], wb[:, :, :, DIM], aw[:, :, :, DIM], ALU.mult).then_inc(b_attn_b_made, 1)
                    for h in range(HEADS):
                        for i in range(CT):
                            bank = banks[:, h * CT + i]
                            dve.wait_ge(gw_hi, h * CT + i + 1)
                            nc.vector.tensor_copy(s_weights[:, i, h:h + 1], bank[:, DIM:GR])
                            nc.vector.tensor_tensor(gw_sb[LO][:, i, h], bank[:, 0:DIM], exact(gw_sb[HI][:, i, h]), ALU.subtract).then_inc(gw_lo, 1)
                    dve.wait_ge(vectors_done, 1)
                    nc.vector.tensor_copy(g_bias[:].rearrange("p i h -> p (i h)"), banks[:, 0, 0:CT * HEADS])
                    nc.vector.tensor_copy(s_bias[:], banks[:, 1, 0:HEADS]).then_inc(vectors_kept, 1)
                    dve.wait_ge(vectors_kept, 1)

        x_sb = sb("x_sb", [P, PER_LOOP, RT, DIM], F32)
        res = sb("res", [P, PER_LOOP, RT, DIM], F32)
        adj_sb = sb("adj_sb", [P, PER_LOOP, RT, ROWS], U8)
        stats = sb("stats", [P, RT, 6], F32)
        mean_var = sb("mean_var", [P, RT, 2], F32)
        var_eps = sb("var_eps", [P, RT], F32)
        rstd = sb("rstd", [P, RT], F32)
        normed_x = sb("normed_x", [P, RT, DIM], F32)
        hT_full = sb("hT_full", [P, CT, ROWS], F32)
        hT = [sb(f"hT{i}", [P, PER_LOOP, CT, ROWS], F32R) for i in (HI, LO)]
        s_sb = sb("s_sb", [P, PER_LOOP, RT, HEADS], F32)
        gT = [sb(f"gT{i}", [P, 2, CT, ROWS], F32R) for i in (HI, LO)]
        wh_full = sb("wh_full", [P, RT, DIM], F32)
        wh = [sb(f"wh{i}", [P, 2, RT, DIM], F32R) for i in (HI, LO)]
        a_full = sb("a_full", [P, RT, ROWS], F32)
        a_sb = [sb(f"a{i}", [P, RT, ROWS], F32R) for i in (HI, LO)]
        hpT = [sb(f"hpT{i}", [P, CT, ROWS], F32R) for i in (HI, LO)]
        ha_full = sb("ha_full", [P, CT, ROWS], F32)
        ha = [sb(f"ha{i}", [P, CT, ROWS], F32R) for i in (HI, LO)]
        hf_full = sb("hf_full", [P, CT, ROWS], F32)
        hf = [sb(f"hf{i}", [P, CT, ROWS], F32R) for i in (HI, LO)]
        gate = sb("gate", [P, CT, ROWS], F32)

        def psum(name, shape):
            return ctx.enter_context(nc.psum_tensor(f"{layer}_{name}", shape, F32))

        scores_ps = psum("scores_ps", [P, 2, ROWS])
        front_ps = psum("front_ps", [P, 2, ROWS])
        hp_ps = psum("hp_ps", [P, CT, ROWS])
        ha_ps = psum("ha_ps", [P, CT, ROWS])

        x_loaded = [sem(f"x_loaded{i}") for i in range(PER_LOOP)]
        adj_loaded = [sem(f"adj_loaded{i}") for i in range(PER_LOOP)]
        res_loaded = [sem(f"res_loaded{i}") for i in range(PER_LOOP)]
        stored = [sem(f"stored{i}") for i in range(PER_LOOP)]
        passed = sem("passed")
        stats_done = sem("stats_done")
        mean_var_done = sem("mean_var_done")
        var_eps_done = sem("var_eps_done")
        rstd_done = sem("rstd_done")
        normed_done = sem("normed_done")
        front_done = sem("front_done")
        front_read = sem("front_read")
        front_full = sem("front_full")
        front_act = sem("front_act")
        hT_ready = sem("hT_ready")
        wh_ready = sem("wh_ready")
        difference_done = sem("difference_done")
        opened = sem("opened")
        mixed = sem("mixed")
        added = sem("added")
        scores_done = sem("scores_done")
        masked = sem("masked")
        tanh_hi = sem("tanh_hi")
        tanh_full = sem("tanh_full")
        tanh_lo = sem("tanh_lo")
        hp_done = sem("hp_done")
        hp_hi = sem("hp_hi")
        hp_lo = sem("hp_lo")
        ha_done = sem("ha_done")
        ha_hi = sem("ha_hi")
        ha_lo = sem("ha_lo")

        def side_work(n):
            b, s = n // HEADS, n % HEADS
            if n == -1:
                at = [[("h", 0, 0), ("h", 1, 0), ("s", 0, 0), ("g", 0, 0), ("g", 1, 0), ("g", 0, 1), ("g", 1, 1),
                       ("w", 0, 0), ("w", 1, 0)], [], [], []]
            else:
                at = [[("g", 0, n + 2), ("g", 1, n + 2)], [("w", 0, n + 1)], [("w", 1, n + 1)], []]
                if s == 1:
                    at[3] = [("gate", 0, b - 1), ("gate", 1, b - 1), ("h", 0, b + 1), ("h", 1, b + 1)]
                elif s == 2:
                    at[3] = [("s", 0, b + 1), ("back", 0, b - 1), ("back", 1, b - 1)]
                elif s == 3:
                    at[3] = [("hf", 0, b), ("hf", 1, b)]

            def there(chunk):
                kind, _, to = chunk
                return 0 <= to < (HEADS_ALL if kind in "gw" else BATCHES)

            return [[c for c in point if there(c)] for point in at]

        LAST = HEADS_ALL + HEADS
        chunks = [(n, c) for n in range(-1, LAST) for point in side_work(n) for c in point]

        def before(kinds, n, c):
            at = chunks.index((n, c))
            return sum(x[0] in kinds for _, x in chunks[:at])

        def through(kinds, n, kind, part):
            at = next(i for i, (_, c) in enumerate(chunks) if c == (kind, part, n))
            return sum(x[0] in kinds for _, x in chunks[:at + 1])

        ALL = ("h", "s", "g", "w", "gate", "back", "hf")
        BY_ACT = ("h", "g", "w", "gate", "hf")

        def per_loop(kinds):
            return sum(c[0] in kinds for n, c in chunks if FIRST <= n < FIRST + SLOTS)

        def times(it, each, value):
            return it * each + value

        def exists(n):
            return n < HEADS_ALL

        def parity(n):
            return n // HEADS % PER_LOOP

        def slots(engine, slot):
            for n in range(FIRST):
                slot(0, n)
            with engine.Fori(0, LOOPS - 1) as it:
                for n in range(FIRST, FIRST + SLOTS):
                    slot(it, n)
            for n in range(FIRST + SLOTS * (LOOPS - 1), LAST):
                slot(0, n)

        rows = "b (t p) c -> b p t c"
        x_src = x_in.rearrange(rows, p=P)
        x_dst = x_out.rearrange(rows, p=P)
        adj_src = adj_t.rearrange(rows, p=P)

        with nc.Block() as block:
            @block.sync
            def _(sync):
                def load(b, source):
                    sync.dma_start(x_sb[:, b], x_src[source]).then_inc(x_loaded[b], 16)
                    sync.dma_start(adj_sb[:, b], adj_src[source]).then_inc(adj_loaded[b], 16)

                for b in range(PER_LOOP):
                    load(b, b)
                    sync.dma_start(res[:, b], x_src[b]).then_inc(res_loaded[b], 16)
                with sync.Fori(0, LOOPS - 1) as it:
                    for b in range(PER_LOOP):
                        own_wait(sync, normed_done, times(it, PER_LOOP, b + 1), passed)
                        own_wait(sync, masked, times(it, PER_LOOP * HEADS * RT, (b + 1) * HEADS * RT), passed)
                        load(b, it * PER_LOOP + (b + PER_LOOP))
                        own_wait(sync, added, times(it, PER_LOOP * 2, 2 * b + 2), passed)
                        sync.dma_start(x_dst[it * PER_LOOP + b], res[:, b]).then_inc(stored[b], 16)
                        own_wait(sync, stored[b], times(it, 16, 16), passed)
                        sync.dma_start(res[:, b], x_src[it * PER_LOOP + (b + PER_LOOP)]).then_inc(res_loaded[b], 16)
                for b in range(PER_LOOP):
                    sync.wait_ge(added, 2 * (BATCHES - PER_LOOP + b + 1))
                    sync.dma_start(x_dst[BATCHES - PER_LOOP + b], res[:, b]).then_inc(stored[b], 16)
                for b in range(PER_LOOP):
                    sync.wait_ge(stored[b], 16 * LOOPS)

            @block.gpsimd
            def _(pool):
                def rstd_step(it, b):
                    own_wait(pool, mean_var_done, times(it, PER_LOOP, b + 1), passed)
                    nc.gpsimd.tensor_scalar(var_eps[:], mean_var[:, :, 1], EPS, 1.0, ALU.add, ALU.mult).then_inc(var_eps_done, 1)
                    pool.wait_ge(var_eps_done, times(it, PER_LOOP, b + 1))
                    nc.gpsimd.tensor_tensor(rstd[:], var_eps[:], minus_half[:], ALU.pow).then_inc(rstd_done, 1)

                def side(it, n, c):
                    kind, part, to = c
                    acted = times(it, per_loop(BY_ACT), before(BY_ACT, n, c) + 1)
                    if kind == "h":
                        pool.wait_ge(front_act, acted)
                        b = to % PER_LOOP
                        nc.gpsimd.tensor_tensor(hT[LO][:, b, part], hT_full[:, part], exact(hT[HI][:, b, part]),
                                                ALU.subtract).then_inc(hT_ready, 1)
                    elif kind == "w":
                        pool.wait_ge(front_act, acted)
                        at = slice(2 * part, 2 * part + 2)
                        nc.gpsimd.tensor_tensor(wh[LO][:, to % 2, at], wh_full[:, at], exact(wh[HI][:, to % 2, at]),
                                                ALU.subtract).then_inc(wh_ready, 1)
                    elif kind == "gate":
                        pool.wait_ge(front_act, acted)
                        nc.gpsimd.tensor_tensor(hf_full[:, part], hf_full[:, part], ha_full[:, part],
                                                ALU.subtract).then_inc(difference_done, 1)

                def tanh_rest(it, n, t):
                    pool.wait_ge(tanh_full, times(it, SLOTS * RT, n * RT + t + 1))
                    nc.gpsimd.tensor_tensor(a_sb[LO][:, t], a_full[:, t], exact(a_sb[HI][:, t]), ALU.subtract).then_inc(tanh_lo, 1)

                def slot(it, n):
                    if n % HEADS == 0 and exists(n + HEADS):
                        rstd_step(it, n // HEADS + 1)
                    work = side_work(n)
                    for t in range(RT):
                        if exists(n + 1):
                            tanh_rest(it, n + 1, t)
                        for c in work[t] if t else []:
                            side(it, n, c)

                rstd_step(0, 0)
                for c in side_work(-1)[0]:
                    side(0, -1, c)
                for t in range(RT):
                    tanh_rest(0, 0, t)
                slots(pool, slot)

            @block.scalar
            def _(act):
                def side(it, n, c):
                    kind, part, to = c
                    bank = front_ps[:, before(ALL, n, c) % 2]
                    done = times(it, per_loop(ALL), before(ALL, n, c) + 1)
                    if kind == "h":
                        act.wait_ge(front_read, done)
                        nc.scalar.activation(hT[HI][:, to % PER_LOOP, part], hT_full[:, part], ACT.Copy).then_inc(front_act, 1)
                    elif kind == "g":
                        act.wait_ge(front_done, done)
                        nc.scalar.activation(gT[HI][:, to % 2, part], bank, ACT.Identity,
                                             bias=g_bias[:, part, to % HEADS:to % HEADS + 1]).then_inc(front_act, 1)
                    elif kind == "w":
                        at = slice(2 * part, 2 * part + 2)
                        act.wait_ge(front_read, done)
                        nc.scalar.activation(wh[HI][:, to % 2, at], wh_full[:, at], ACT.Copy).then_inc(front_act, 1)
                    elif kind == "gate":
                        act.wait_ge(front_done, done)
                        nc.scalar.activation(gate[:, part], bank, ACT.Tanh, scale=0.5,
                                             bias=half_gate_bias[:, part:part + 1]).then_inc(front_act, 1)
                    elif kind == "hf":
                        act.wait_ge(front_done, done)
                        nc.scalar.activation(hf_full[:, part], bank, ACT.Copy)
                        nc.scalar.activation(hf[HI][:, part], bank, ACT.Copy).then_inc(front_act, 1)

                def tanhs(it, n, t):
                    act.wait_ge(masked, times(it, SLOTS * RT, n * RT + t + 1))
                    nc.scalar.activation(a_sb[HI][:, t], a_full[:, t], ACT.Tanh).then_inc(tanh_hi, 1)
                    act.wait_ge(tanh_hi, times(it, SLOTS * RT, n * RT + t + 1))
                    nc.scalar.activation(a_full[:, t], a_full[:, t], ACT.Tanh).then_inc(tanh_full, 1)

                def slot(it, n):
                    work = side_work(n)
                    for c in work[0]:
                        side(it, n, c)
                    for t in range(RT):
                        if t == RT - 1 and exists(n):
                            act.wait_ge(hp_done, times(it, SLOTS, n + 1))
                            for i in range(CT):
                                nc.scalar.activation(hpT[HI][:, i], hp_ps[:, i], ACT.Relu).then_inc(hp_hi, 1)
                        if exists(n + 1):
                            tanhs(it, n + 1, t)
                        if t == 0 and n % HEADS == 0 and 0 < n <= HEADS_ALL:
                            act.wait_ge(ha_done, times(it, PER_LOOP, n // HEADS))
                            for i in range(CT):
                                nc.scalar.activation(ha_full[:, i], ha_ps[:, i], ACT.Copy)
                                nc.scalar.activation(ha[HI][:, i], ha_ps[:, i], ACT.Copy).then_inc(ha_hi, 1)
                        for c in work[t] if t else []:
                            side(it, n, c)

                for c in side_work(-1)[0]:
                    side(0, -1, c)
                for t in range(RT):
                    tanhs(0, 0, t)
                slots(act, slot)

            @block.vector
            def _(dve):
                def norm_first(it, b):
                    p = b % PER_LOOP
                    dve.wait_ge(x_loaded[p], times(it, 16, b // PER_LOOP * 16 + 16))
                    for q in range(RT):
                        step = nc.vector.bn_stats(stats[:, q], x_sb[:, p, q])
                    step.then_inc(stats_done, 1)
                    own_wait(dve, stats_done, times(it, PER_LOOP, b + 1), passed)
                    for q in range(RT):
                        step = nc.vector.bn_aggr(mean_var[:, q], stats[:, q])
                    step.then_inc(mean_var_done, 1)

                def norm_last(it, b):
                    dve.wait_ge(rstd_done, times(it, PER_LOOP, b + 1))
                    for q in range(RT):
                        step = nc.vector.tensor_scalar(normed_x[:, q], x_sb[:, b % PER_LOOP, q], mean_var[:, q, 0:1],
                                                       rstd[:, q:q + 1], ALU.subtract, ALU.mult)
                    step.then_inc(normed_done, 1)

                def side(it, n, c):
                    kind, part, to = c
                    bank = front_ps[:, before(ALL, n, c) % 2]
                    done = times(it, per_loop(ALL), before(ALL, n, c) + 1)
                    acted = times(it, per_loop(BY_ACT), before(BY_ACT, n, c) + 1)
                    if kind == "h":
                        if to > 0:
                            dve.wait_ge(hT_ready, times(it, PER_LOOP * CT, to * CT))
                        dve.wait_ge(front_done, done)
                        nc.vector.tensor_scalar(hT_full[:, part], bank, 0.0, None, ALU.max).then_inc(front_read, 1)
                    elif kind == "s":
                        dve.wait_ge(front_done, done)
                        nc.vector.tensor_tensor(
                            s_sb[:, to % PER_LOOP], bank[:, 0:RT * HEADS].rearrange("p (t h) -> p t h", t=RT),
                            s_bias[:].unsqueeze(1).to_broadcast([P, RT, HEADS]), ALU.add).then_inc(front_read, 1)
                    elif kind == "g":
                        dve.wait_ge(front_act, acted)
                        nc.vector.scalar_tensor_tensor(
                            gT[LO][:, to % 2, part], bank, g_bias[:, part, to % HEADS:to % HEADS + 1],
                            exact(gT[HI][:, to % 2, part]), ALU.add, ALU.subtract).then_inc(front_read, 1)
                    elif kind == "w":
                        if to > 0:
                            dve.wait_ge(wh_ready, times(it, SLOTS * 2, 2 * to))
                        dve.wait_ge(front_done, done)
                        h = to % HEADS
                        bias = wh_bias[:, h * DIM:(h + 1) * DIM].unsqueeze(1).to_broadcast([P, 2, DIM])
                        nc.vector.tensor_tensor(wh_full[:, 2 * part:2 * part + 2], bank.rearrange("p (t o) -> p t o", t=2),
                                                bias, ALU.add).then_inc(front_read, 1)
                    elif kind == "gate":
                        dve.wait_ge(front_act, acted)
                        dve.wait_ge(difference_done, times(it, PER_LOOP * CT, to * CT + part + 1))
                        nc.vector.scalar_tensor_tensor(gate[:, part], gate[:, part], 1.0, hf_full[:, part],
                                                       ALU.add, ALU.mult).then_inc(front_read, 1)
                        dve.wait_ge(front_read, done)
                        nc.vector.scalar_tensor_tensor(gate[:, part], gate[:, part], 0.5, ha_full[:, part],
                                                       ALU.mult, ALU.add).then_inc(mixed, 1)
                    elif kind == "back":
                        p, at = to % PER_LOOP, slice(2 * part, 2 * part + 2)
                        dve.wait_ge(front_done, done)
                        dve.wait_ge(res_loaded[p], times(it, 16, to // PER_LOOP * 16 + 16))
                        nc.vector.tensor_tensor(res[:, p, at], bank.rearrange("p (t o) -> p t o", t=2), res[:, p, at],
                                                ALU.add).then_inc(added, 1)
                        dve.wait_ge(added, times(it, PER_LOOP * 2, to * 2 + part + 1))
                        dve.sem_inc(front_read, 1)
                    elif kind == "hf":
                        dve.wait_ge(front_act, acted)
                        nc.vector.tensor_tensor(hf[LO][:, part], bank, exact(hf[HI][:, part]), ALU.subtract).then_inc(front_read, 1)

                def mask_scores(it, n, t):
                    p, h = parity(n), n % HEADS
                    if h == 0 and t == 0:
                        dve.wait_ge(adj_loaded[p], times(it, 16, n // HEADS // PER_LOOP * 16 + 16))
                    if n > 0:
                        dve.wait_ge(tanh_lo, times(it, SLOTS * RT, (n - 1) * RT + t + 1))
                    dve.wait_ge(scores_done, times(it, SLOTS * RT, n * RT + t + 1))
                    nc.vector.scalar_tensor_tensor(a_full[:, t], scores_ps[:, t % 2], s_sb[:, p, t, h:h + 1], adj_sb[:, p, t],
                                                   ALU.add, ALU.mult).then_inc(masked, 1)

                def slot(it, n):
                    ahead = n % HEADS == 0 and exists(n + HEADS)
                    work = side_work(n)
                    for c in work[0]:
                        side(it, n, c)
                    if ahead:
                        norm_first(it, n // HEADS + 1)
                    for t in range(RT):
                        if t == RT - 1 and exists(n):
                            for i in range(CT):
                                dve.wait_ge(hp_hi, times(it, SLOTS * CT, n * CT + i + 1))
                                nc.vector.scalar_tensor_tensor(hpT[LO][:, i], hp_ps[:, i], 0.0, exact(hpT[HI][:, i]),
                                                               ALU.max, ALU.subtract).then_inc(hp_lo, 1)
                        if exists(n + 1):
                            mask_scores(it, n + 1, t)
                        if t == 1 and ahead:
                            norm_last(it, n // HEADS + 1)
                        if t == 0 and n % HEADS == 0 and 0 < n <= HEADS_ALL:
                            for i in range(CT):
                                dve.wait_ge(ha_hi, times(it, PER_LOOP * CT, (n // HEADS - 1) * CT + i + 1))
                                nc.vector.tensor_tensor(ha[LO][:, i], ha_ps[:, i], exact(ha[HI][:, i]), ALU.subtract).then_inc(ha_lo, 1)
                        for c in work[t] if t else []:
                            side(it, n, c)

                norm_first(0, 0)
                norm_last(0, 0)
                for c in side_work(-1)[0]:
                    side(0, -1, c)
                for t in range(RT):
                    mask_scores(0, 0, t)
                slots(dve, slot)

            @block.tensor
            def _(pe):
                def three_passes(out, pairs):
                    for n, (i, j) in enumerate(PASSES):
                        for m, (left, right) in enumerate(pairs):
                            mm = nc.tensor.matmul(out, left[i], right[j], start=(n + m == 0),
                                                  stop=(n == 2 and m == len(pairs) - 1))
                    return mm

                def halves(pair, *at):
                    return [x[(slice(None), *at)] for x in pair]

                def side(it, n, c):
                    kind, part, to = c
                    number = before(ALL, n, c)
                    bank = front_ps[:, number % 2]
                    if number >= 2:
                        pe.wait_ge(front_read, times(it, per_loop(ALL), number - 1))
                    at = slice(part * P, (part + 1) * P)
                    b = to % PER_LOOP if kind not in "gw" else parity(to)
                    if kind == "h":
                        if part == 0:
                            pe.wait_ge(normed_done, times(it, PER_LOOP, to + 1))
                        for q in range(RT):
                            mm = nc.tensor.transpose(bank[:, q * P:(q + 1) * P], normed_x[:, q, at], ident[:])
                    elif kind == "s":
                        pe.wait_ge(front_read, times(it, per_loop(ALL), through(ALL, to, "h", 1)))
                        for q in range(RT):
                            for t in range(CT):
                                mm = nc.tensor.matmul(bank[:, q * HEADS:(q + 1) * HEADS], hT_full[:, t, q * P:(q + 1) * P],
                                                      s_weights[:, t], start=(t == 0), stop=(t == CT - 1))
                    elif kind == "g":
                        if to % HEADS == 0 and part == 0:
                            pe.wait_ge(hT_ready, times(it, PER_LOOP * CT, (to // HEADS + 1) * CT))
                        mm = three_passes(bank, [(halves(gw_sb, t, to % HEADS, at), halves(hT, b, t)) for t in range(CT)])
                    elif kind == "w":
                        h = to % HEADS
                        for m in range(2):
                            q = 2 * part + m
                            mm = three_passes(bank[:, m * DIM:(m + 1) * DIM], [
                                (halves(hT, b, t, slice(q * P, (q + 1) * P)), halves(w_sb, t, slice(h * DIM, (h + 1) * DIM)))
                                for t in range(CT)])
                    elif kind == "hf":
                        mm = three_passes(bank, [(halves(small_sb, FC, t, at), halves(hT, b, t)) for t in range(CT)])
                    elif kind == "gate":
                        if part == 0:
                            pe.wait_ge(ha_lo, times(it, PER_LOOP * CT, (to + 1) * CT))
                            pe.wait_ge(front_read, times(it, per_loop(ALL), through(ALL, to, "hf", 1)))
                        mm = three_passes(bank, [(halves(small_sb, G1, t, at), halves(hf, t)) for t in range(CT)]
                                          + [(halves(small_sb, G2, t, at), halves(ha, t)) for t in range(CT)])
                    elif kind == "back":
                        pe.wait_ge(mixed, times(it, PER_LOOP * CT, (to + 1) * CT))
                        for m in range(2):
                            q = 2 * part + m
                            for t in range(CT):
                                mm = nc.tensor.transpose(bank[:, m * DIM + t * P:m * DIM + (t + 1) * P],
                                                         gate[:, t, q * P:(q + 1) * P], ident[:])
                    mm.then_inc(front_done, 1)

                def scores(it, n, t):
                    if t == 0:
                        pe.wait_ge(front_read, times(it, per_loop(ALL), through(ALL, n, "g", 1)))
                    tile = n * RT + t
                    if tile >= 2:
                        pe.wait_ge(masked, times(it, SLOTS * RT, tile - 1))
                    three_passes(scores_ps[:, t % 2], [
                        (halves(gT, n % 2, i, slice(t * P, (t + 1) * P)), halves(hT, parity(n), i)) for i in range(CT)
                    ]).then_inc(scores_done, 1)

                def times_wh(it, n, t):
                    if t == 0:
                        pe.wait_ge(wh_ready, times(it, SLOTS * 2, 2 * n + 2))
                        if n > 0:
                            pe.wait_ge(hp_lo, times(it, SLOTS * CT, n * CT))
                    pe.wait_ge(tanh_lo, times(it, SLOTS * RT, n * RT + t + 1))
                    for o in range(CT):
                        for m, (i, j) in enumerate(PASSES):
                            mm = nc.tensor.matmul(hp_ps[:, o], wh[i][:, n % 2, t, o * P:(o + 1) * P], a_sb[j][:, t],
                                                  start=(t == 0 and m == 0), stop=(t == RT - 1 and m == 2))
                    if t == RT - 1:
                        mm.then_inc(hp_done, 1)

                def mix_head(it, n):
                    h = n % HEADS
                    pe.wait_ge(hp_lo, times(it, SLOTS * CT, (n + 1) * CT))
                    if h == 0 and n > 0:
                        pe.wait_ge(ha_lo, times(it, PER_LOOP * CT, n // HEADS * CT))
                    for o in range(CT):
                        for m, (i, j) in enumerate(PASSES):
                            for t in range(CT):
                                mm = nc.tensor.matmul(
                                    ha_ps[:, o], mix_sb[i][:, h * CT + t, o * P:(o + 1) * P], hpT[j][:, t],
                                    start=(h == 0 and m + t == 0), stop=(h == HEADS - 1 and m == 2 and t == CT - 1))
                    if h == HEADS - 1:
                        mm.then_inc(ha_done, 1)

                def slot(it, n):
                    work = side_work(n)
                    for c in work[0]:
                        side(it, n, c)
                    for t in range(RT):
                        if exists(n):
                            times_wh(it, n, t)
                        if exists(n + 1):
                            scores(it, n + 1, t)
                        if t == 0 and n > 0 and exists(n - 1):
                            mix_head(it, n - 1)
                        for c in work[t] if t else []:
                            side(it, n, c)

                for c in side_work(-1)[0]:
                    side(0, -1, c)
                for t in range(RT):
                    scores(0, 0, t)
                slots(pe, slot)


def network(nc, x, adj, adj_t, l0, l1, l2, l3, out):
    x1, x2, x3 = (nc.dram_tensor(f"x{n}", x.shape, F32).ap() for n in (1, 2, 3))
    attention_layer(nc, "L0", x, x1, adj, *l0, heads=4)
    attention_layer(nc, "L1", x1, x2, adj, *l1[:3], heads=8, gamma=l1[3], beta=l1[4])
    gated_layer(nc, "L2", x2, x3, adj_t, *l2)
    attention_layer(nc, "L3", x3, out, adj, *l3, heads=4)


def kernel(**inputs):
    import numpy as _np
    import concourse.bacc as _bacc
    from concourse import mybir as _mybir
    from concourse.bass_utils import run_bass_kernel_spmd as _run

    nc = _bacc.Bacc("TRN2", target_bir_lowering=False, num_devices=1)
    arrays = {}
    inputs = {name: _np.asarray(a) for name, a in inputs.items()}

    def given(name, array):
        arrays[name] = _np.ascontiguousarray(array)
        dtype = _mybir.dt.from_np(arrays[name].dtype)
        return nc.dram_tensor(name, arrays[name].shape, dtype, kind="ExternalInput").ap()

    x = given("x", inputs["x"])
    adj = given("adj", inputs["adj"])
    adj_t = given("adj_t", inputs["adj"].transpose(0, 2, 1))

    def square_layer(n):
        w = _np.stack([inputs[f"L{n}_gnn_W{c}"] for c in "qkv"], axis=1)
        return given(f"L{n}_qkv", w), given(f"L{n}_Wo", inputs[f"L{n}_gnn_Wo"]), given(f"L{n}_bo", inputs[f"L{n}_gnn_bo"])

    w_qkv = inputs["L1_gnn_w_qkv"]
    l1 = (
        given("L1_qkv", w_qkv.reshape(3, -1, w_qkv.shape[1]).transpose(2, 0, 1)),
        given("L1_w_out", inputs["L1_gnn_w_out"].T), given("L1_b_out", inputs["L1_gnn_b_out"]),
        given("L1_gamma", inputs["L1_gnn_gamma"]), given("L1_beta", inputs["L1_gnn_beta"]),
    )
    w = inputs["L2_gnn_W"]
    l2 = (
        given("L2_W_rows", w.transpose(1, 0, 2)), given("L2_W_cols", w.transpose(2, 0, 1).reshape(w.shape[2], -1)),
        given("L2_attn_t", inputs["L2_gnn_attn"].transpose(2, 0, 1)), given("L2_bW", inputs["L2_gnn_bW"]),
        given("L2_A_w_t", inputs["L2_gnn_A_w"].T),
        tuple(given(f"L2_{c}_t", inputs[f"L2_gnn_{c}_w"].T) for c in ("fc", "g1", "g2")),
        given("L2_gbias", inputs["L2_gnn_gbias"]),
    )
    out = nc.dram_tensor("out", x.shape, _mybir.dt.float32, kind="ExternalOutput").ap()
    network(nc, x, adj, adj_t, square_layer(0), l1, l2, square_layer(3), out)
    r = _run(nc, [arrays], core_ids=[0])
    return r.results[0]["out"]
```

```python
from contextlib import ExitStack

import concourse.bass as bass
from concourse import mybir

ALU = mybir.AluOpType
ACT = mybir.ActivationFunctionType
F32 = mybir.dt.float32
F32R = mybir.dt.float32r
BF16 = mybir.dt.bfloat16
U8 = mybir.dt.uint8

P = 128
BATCHES = 16
ROWS = 512
DIM = 256
RT = ROWS // P
CT = DIM // P
HEAD = 64
GROUP = 4
PER_LOOP = 2
LOOPS = BATCHES // PER_LOOP
SCALE = HEAD**-0.5
EPS = 1e-5
BIG = 2.0**127
LEAST = 3.0e38

PASSES = ((0, 0), (0, 1), (1, 0))
HI, LO = 0, 1


def own_wait(engine, semaphore, value, passed):
    engine.wait_ge(semaphore, value)
    engine.sem_inc(passed, 1)


def exact(tile):
    return tile.bitcast(F32)


def layer_semaphores(nc, ctx, layer):
    given = []

    def sem(name):
        given.append(nc.alloc_semaphore(name=f"{layer}_{name}"))
        return given[-1]

    def give_back():
        nc.clear_and_free_semaphores(given)
        nc.all_engine_barrier()

    ctx.callback(give_back)
    return sem


def split_weights(nc, block, loads, sems):
    staged_in, hi_made, lo_made = sems

    @block.sync
    def _(sync):
        for n, (moves, _, _, _) in enumerate(loads):
            for to, source in moves:
                sync.dma_start(to, source).then_inc(staged_in[n], 16)

    @block.scalar
    def _(act):
        for n, (moves, staged, hi, _) in enumerate(loads):
            act.wait_ge(staged_in[n], 16 * len(moves))
            nc.scalar.activation(hi, staged, ACT.Copy).then_inc(hi_made, 1)

    @block.vector
    def _(dve):
        for n, (_, staged, hi, lo) in enumerate(loads):
            dve.wait_ge(hi_made, n + 1)
            nc.vector.tensor_tensor(lo, staged, exact(hi), ALU.subtract).then_inc(lo_made, 1)


def identity_matrix(nc, block, ident, made):
    @block.gpsimd
    def _(pool):
        nc.gpsimd.memset(ident, 0.0).then_inc(made, 1)
        pool.wait_ge(made, 1)
        nc.gpsimd.affine_select(
            out=ident, in_=ident, compare_op=ALU.not_equal, fill=1.0, base=0,
            pattern=[[-1, P]], channel_multiplier=1,
        ).then_inc(made, 1)


def attention_layer(nc, layer, x_in, x_out, adj, w_qkv, w_out, b_out, heads, gamma=None, beta=None):
    own_norm = gamma is not None
    inner = heads * HEAD
    pair_groups = heads // GROUP
    SLOTS = PER_LOOP * heads
    HEADS_ALL = BATCHES * heads
    norms = 2 if own_norm else 1
    FIRST = 3

    LEAD = 2
    BEFORE = ((0, 0), (1, 0), (3, 2), (2, 0))
    PROJECTED = ((0,), (1,), (2, 3), ())

    def refreshes(k):
        return (k // GROUP + 1) * GROUP % heads == 0

    def chunks_of(k):
        return 2 if k % 4 != 0 or refreshes(k) else 0

    def chunks_before(k):
        return 8 + sum(chunks_of(j) for j in range(k))

    CHUNKS = chunks_before(SLOTS) - chunks_before(0)

    def chunk(it, k, part):
        return it * CHUNKS + chunks_before(k) + part

    def head(it, k, times=1, more=0):
        return it * (SLOTS * times) + (k * times + more)

    def batch(it, k, times=1, more=0):
        return it * (PER_LOOP * times) + (k // heads * times + more)

    def exists(it, k):
        return not isinstance(it, int) or it * SLOTS + k < HEADS_ALL

    def front_slot(k):
        return k + (4, 3, 2, 3)[k % 4]

    def front_exists(it, k):
        return chunks_of(k) > 0 and exists(it, front_slot(k))

    def norms_ahead(it, k):
        return k % 4 == 3 and refreshes(k + 1) and exists(it, k + 1 + GROUP)

    with ExitStack() as ctx:
        def sb(name, shape, dt):
            return ctx.enter_context(nc.sbuf_tensor(f"{layer}_{name}", shape, dt))

        def psum(name, shape):
            return ctx.enter_context(nc.psum_tensor(f"{layer}_{name}", shape, F32))

        sem = layer_semaphores(nc, ctx, layer)

        wqkv = [sb(f"wqkv{i}", [P, CT, 3, inner], F32R) for i in (HI, LO)]
        wout = [sb(f"wout{i}", [P, heads, DIM], F32R) for i in (HI, LO)]
        bias_row = sb("bias_row", [P, DIM], F32)
        affine = sb("affine", [P, 2, CT], F32)
        ident = sb("ident", [P, P], F32)
        minus_half = sb("minus_half", [P, RT], F32)

        x_sb = sb("x_sb", [P, PER_LOOP, RT, DIM], F32)
        res = sb("res", [P, PER_LOOP, RT, DIM], F32)
        adj_sb = sb("adj_sb", [P, PER_LOOP, RT, ROWS], U8)
        mask = sb("mask", [P, PER_LOOP, RT, ROWS], BF16)
        stats = sb("stats", [P, RT, 6], F32)
        mean_var = sb("mean_var", [P, RT, 2], F32)
        var_eps = sb("var_eps", [P, RT], F32)
        rstd = sb("rstd", [P, RT], F32)
        normed_x = sb("normed_x", [P, RT, DIM], F32)
        hT_full = sb("hT_full", [P, CT, ROWS], F32)
        hT = [sb(f"hT{i}", [P, CT, ROWS], F32R) for i in (HI, LO)]
        qT = [sb(f"qT{i}", [P, 2, ROWS], F32R) for i in (HI, LO)]
        kT = [sb(f"kT{i}", [P, 2, ROWS], F32R) for i in (HI, LO)]
        v_sb = sb("v_sb", [P, 2, RT, GROUP, 2 * HEAD], F32R)
        probs = sb("probs", [P, 4, RT, ROWS], F32)
        row_shift = sb("row_shift", [P, 4, RT], F32)
        row_sum = sb("row_sum", [P, 4, RT], F32)
        row_recip = sb("row_recip", [P, 4, RT], F32)
        pT = [sb(f"pT{i}", [P, RT, ROWS], F32R) for i in (HI, LO)]
        oT = [sb(f"oT{i}", [P, ROWS], F32R) for i in (HI, LO)]

        scores_ps = psum("scores_ps", [P, 2, ROWS])
        pT_ps = psum("pT_ps", [P, 2, ROWS])
        front_ps = psum("front_ps", [P, ROWS])
        oT_ps = psum("oT_ps", [P, ROWS])
        y_ps = psum("y_ps", [P, RT, DIM])

        consts_in = sem("consts_in")
        ident_made = sem("ident_made")
        passed = sem("passed")
        exponent_made = sem("exponent_made")
        staged_in = [sem(f"staged_in{n}") for n in range(2)]
        weights_hi = sem("weights_hi")
        weights_lo = sem("weights_lo")
        x_loaded = [sem(f"x_loaded{i}") for i in range(PER_LOOP)]
        adj_loaded = [sem(f"adj_loaded{i}") for i in range(PER_LOOP)]
        stored = [sem(f"stored{i}") for i in range(PER_LOOP)]
        mask_blank = sem("mask_blank")
        mask_ready = sem("mask_ready")
        stats_done = sem("stats_done")
        mean_var_done = sem("mean_var_done")
        var_eps_done = sem("var_eps_done")
        rstd_done = sem("rstd_done")
        centred = sem("centred")
        rectified = sem("rectified")
        normed_done = sem("normed_done")
        res_ready = sem("res_ready")
        front_done = sem("front_done")
        front_hi = sem("front_hi")
        front_read = sem("front_read")
        hT_ready = sem("hT_ready")
        scores_done = sem("scores_done")
        masked = sem("masked")
        exp_done = sem("exp_done")
        recip_done = sem("recip_done")
        probs_ready = sem("probs_ready")
        pT_done = sem("pT_done")
        pT_hi = sem("pT_hi")
        pT_lo = sem("pT_lo")
        oT_done = sem("oT_done")
        oT_hi = sem("oT_hi")
        oT_lo = sem("oT_lo")
        y_done = sem("y_done")
        y_added = sem("y_added")

        rows = "b (t p) c -> b p t c"
        x_src = x_in.rearrange(rows, p=P)
        x_dst = x_out.rearrange(rows, p=P)
        adj_src = adj.rearrange(rows, p=P)

        with nc.Block() as block:
            w_stage = probs[:].rearrange("p a t r -> p (a t r)")[:, 0:CT * 3 * inner]
            o_stage = res[:].rearrange("p a t c -> p (a t c)")[:, 0:heads * DIM]
            w_view = w_qkv.rearrange("(t p) a n -> p t (a n)", p=P)
            o_view = w_out.rearrange("(h d) c -> d h c", d=HEAD)
            split_weights(nc, block, [
                ([(w_stage.rearrange("p (t n) -> p t n", t=CT), w_view)], w_stage,
                 wqkv[HI][:].rearrange("p t a n -> p (t a n)"), wqkv[LO][:].rearrange("p t a n -> p (t a n)")),
                ([(o_stage[h * HEAD:(h + 1) * HEAD].rearrange("p (h c) -> p h c", h=heads), o_view)
                  for h in range(2)], o_stage,
                 wout[HI][:].rearrange("p h c -> p (h c)"), wout[LO][:].rearrange("p h c -> p (h c)")),
            ], (staged_in, weights_hi, weights_lo))
            identity_matrix(nc, block, ident[:], ident_made)

            @block.sync
            def _(sync):
                sync.dma_start(bias_row[:], b_out.rearrange("(a c) -> a c", a=1).to_broadcast([P, DIM])).then_inc(consts_in, 16)
                if own_norm:
                    with nc.allow_non_contiguous_dma(reason="one column of channels"):
                        for n, v in enumerate((gamma, beta)):
                            sync.dma_start(affine[:, n, :], v.rearrange("(t p) -> p t", p=P)).then_inc(consts_in, 16)

                def load(it, b, source):
                    sync.dma_start(x_sb[:, b], x_src[source]).then_inc(x_loaded[b], 16)
                    sync.dma_start(adj_sb[:, b], adj_src[source]).then_inc(adj_loaded[b], 16)

                def store(it, b, to, count):
                    sync.wait_ge(y_added, count)
                    sync.dma_start(x_dst[to], res[:, b]).then_inc(stored[b], 16)

                for b in range(PER_LOOP):
                    sync.sem_inc(stored[b], 16)
                    load(0, b, b)
                with sync.Fori(0, LOOPS - 1) as it:
                    for b in range(PER_LOOP):
                        sync.wait_ge(normed_done, it * PER_LOOP + (b + 1))
                        sync.wait_ge(res_ready, it * PER_LOOP + (b + 1))
                        sync.wait_ge(mask_ready, it * PER_LOOP + (b + 1))
                        load(it, b, it * PER_LOOP + (b + PER_LOOP))
                        store(it, b, it * PER_LOOP + b, it * (2 * PER_LOOP) + (2 * b + 2))
                for b in range(PER_LOOP):
                    store(0, b, BATCHES - PER_LOOP + b, 2 * (BATCHES - PER_LOOP + b + 1))
                for b in range(PER_LOOP):
                    sync.wait_ge(stored[b], 16 * LOOPS + 16)

            @block.gpsimd
            def _(pool):
                nc.gpsimd.memset(minus_half[:], -0.5).then_inc(exponent_made, 1)

                def make_mask(it, k):
                    b = k // heads % PER_LOOP
                    own_wait(pool, adj_loaded[b], it * 16 + (k // SLOTS * 16 + 16), passed)
                    if not isinstance(it, int) or it * PER_LOOP + k // heads >= PER_LOOP:
                        own_wait(pool, masked, batch(it, k, RT * heads, 1 - RT * heads), passed)
                    convert = nc.gpsimd.tensor_scalar(mask[:, b], adj_sb[:, b], -1.0, BIG, ALU.add, ALU.mult)
                    if own_norm:
                        convert.then_inc(mask_blank, 1)
                        own_wait(pool, mask_blank, batch(it, k, 1, 1), passed)
                        nc.gpsimd.affine_select(
                            out=mask[:, b], in_=mask[:, b], compare_op=ALU.not_equal, fill=0.0, base=0,
                            pattern=[[P, RT], [-1, ROWS]], channel_multiplier=1,
                        ).then_inc(mask_ready, 1)
                    else:
                        convert.then_inc(mask_ready, 1)

                def rstd_step(it, k, n):
                    own_wait(pool, mean_var_done, batch(it, k, norms, n + 1), passed)
                    nc.gpsimd.tensor_scalar(var_eps[:], mean_var[:, :, 1], EPS, 1.0, ALU.add, ALU.mult).then_inc(var_eps_done, 1)
                    pool.wait_ge(var_eps_done, batch(it, k, norms, n + 1))
                    nc.gpsimd.tensor_tensor(rstd[:], var_eps[:], minus_half[:], ALU.pow).then_inc(rstd_done, 1)

                def residual(it, k):
                    b = k // heads % PER_LOOP
                    pool.wait_ge(stored[b], it * 16 + (k // SLOTS * 16 + 16))
                    nc.gpsimd.tensor_tensor(
                        res[:, b], x_sb[:, b], bias_row[:].unsqueeze(1).to_broadcast([P, RT, DIM]), ALU.add,
                    ).then_inc(res_ready, 1)

                def hT_rest(it, k, first):
                    for part in range(CT):
                        pool.wait_ge(front_read, first + (part + 1))
                        nc.gpsimd.tensor_tensor(
                            hT[LO][:, part], hT_full[:, part], exact(hT[HI][:, part]), ALU.subtract,
                        ).then_inc(hT_ready, 1)

                def normalise(it, k):
                    own_wait(pool, recip_done, head(it, k, 1, 1), passed)
                    for q in range(RT):
                        part = probs[:, k % 4, q]
                        nc.gpsimd.tensor_scalar(
                            part, part, row_recip[:, k % 4, q:q + 1], 1.0, ALU.mult, ALU.mult,
                        ).then_inc(probs_ready, 1)

                def slot(it, k):
                    s, ahead = k % 4, refreshes(k) and exists(it, k + GROUP)
                    if norms_ahead(it, k):
                        for n in range(norms):
                            rstd_step(it, k + 1 + GROUP, n)
                    if exists(it, k + 1):
                        normalise(it, k + 1)
                    if ahead and s == 0:
                        if own_norm:
                            hT_rest(it, k + GROUP, chunk(it, k, 0))
                        make_mask(it, k + GROUP)
                    if ahead and s == 3:
                        residual(it, k + GROUP)

                pool.wait_ge(exponent_made, 1)
                pool.wait_ge(consts_in, 48 if own_norm else 16)
                for n in range(norms):
                    rstd_step(0, 0, n)
                make_mask(0, 0)
                if own_norm:
                    hT_rest(0, 0, 0)
                pool.wait_ge(weights_lo, 2)
                residual(0, 0)
                normalise(0, 0)
                if refreshes(0):
                    for n in range(norms):
                        rstd_step(0, GROUP, n)
                for k in range(FIRST):
                    slot(0, k)
                with pool.Fori(0, LOOPS - 1) as it:
                    for k in range(FIRST, SLOTS + FIRST):
                        slot(it, k)
                for k in range(FIRST, SLOTS + 2):
                    slot(LOOPS - 1, k)

            @block.scalar
            def _(act):
                def act_front(k, s, part, first):
                    act.wait_ge(front_done, first + (part + 1))
                    if s == 0:
                        if own_norm:
                            step = nc.scalar.activation(hT[HI][:, part], front_ps[:], ACT.Identity,
                                                        bias=affine[:, 1, part:part + 1], scale=affine[:, 0, part:part + 1])
                        else:
                            step = nc.scalar.activation(hT[HI][:, part], front_ps[:], ACT.Relu)
                        step.then_inc(front_hi, 1)
                        return
                    if s in (1, 3):
                        to, source = (qT, kT)[part][HI][:, k // 2 % 2], front_ps[:]
                    else:
                        to = v_sb[:, k // GROUP % 2, 2 * part:2 * part + 2, :, 0:HEAD]
                        source = front_ps[:].rearrange("p (t h d) -> p t h d", t=2, h=GROUP)
                    nc.scalar.activation(to, source, ACT.Copy).then_inc(front_hi, 1)

                def exps(it, k, q):
                    part = probs[:, k % 4, q]
                    act.wait_ge(masked, head(it, k, RT, q + 1))
                    nc.scalar.activation(
                        part, part, ACT.Exp, bias=row_shift[:, k % 4, q:q + 1], scale=-1.0,
                        accum_out=row_sum[:, k % 4, q:q + 1],
                    ).then_inc(exp_done, 1)

                def slot(it, k):
                    for q in range(RT):
                        if exists(it, k):
                            act.wait_ge(pT_done, head(it, k, RT, q + 1))
                            nc.scalar.activation(pT[HI][:, q], pT_ps[:, q % 2], ACT.Copy).then_inc(pT_hi, 1)
                        if k >= 1 and exists(it, k - 1) and q == RT - 2:
                            act.wait_ge(oT_done, head(it, k))
                            nc.scalar.activation(oT[HI][:], oT_ps[:], ACT.Copy).then_inc(oT_hi, 1)
                        if q % 2 and front_exists(it, k):
                            act_front(front_slot(k), k % 4, q // 2, chunk(it, k, 0))
                        if q > 0:
                            if exists(it, k + LEAD):
                                exps(it, k + LEAD, q - 1)
                        elif exists(it, k + LEAD - 1):
                            exps(it, k + LEAD - 1, RT - 1)

                for n, (s, k) in enumerate(BEFORE):
                    for part in range(2):
                        act_front(k, s, part, 2 * n)
                for k in range(LEAD):
                    for q in range(RT - (k == LEAD - 1)):
                        exps(0, k, q)
                for k in range(FIRST):
                    slot(0, k)
                with act.Fori(0, LOOPS - 1) as it:
                    for k in range(FIRST, SLOTS + FIRST):
                        slot(it, k)
                for k in range(FIRST, SLOTS + 2):
                    slot(LOOPS - 1, k)

            @block.vector
            def _(dve):
                def front(it, k, s, part, first):
                    dve.wait_ge(front_hi, first + (part + 1))
                    if s == 0 and own_norm:
                        before = batch(it, k, CT)
                        if not isinstance(before, int) or before > 0:
                            dve.wait_ge(hT_ready, before)
                        nc.vector.tensor_scalar(
                            hT_full[:, part], front_ps[:], affine[:, 0, part:part + 1], affine[:, 1, part:part + 1],
                            ALU.mult, ALU.add,
                        ).then_inc(front_read, 1)
                        return
                    if s == 0:
                        nc.vector.scalar_tensor_tensor(
                            hT[LO][:, part], front_ps[:], 0.0, exact(hT[HI][:, part]), ALU.max, ALU.subtract,
                        ).then_inc(front_read, 1)
                        return
                    if s in (1, 3):
                        half = (qT, kT)[part]
                        to, hi, source = half[LO][:, k // 2 % 2], half[HI][:, k // 2 % 2], front_ps[:]
                    else:
                        both = v_sb[:, k // GROUP % 2, 2 * part:2 * part + 2]
                        to, hi = both[:, :, :, HEAD:], both[:, :, :, 0:HEAD]
                        source = front_ps[:].rearrange("p (t h d) -> p t h d", t=2, h=GROUP)
                    nc.vector.tensor_tensor(to, source, exact(hi), ALU.subtract).then_inc(front_read, 1)

                def mean_and_variance(it, k, n, rows_):
                    for q in range(RT):
                        step = nc.vector.bn_stats(stats[:, q], rows_[:, q])
                    step.then_inc(stats_done, 1)
                    own_wait(dve, stats_done, batch(it, k, norms, n + 1), passed)
                    for q in range(RT):
                        step = nc.vector.bn_aggr(mean_var[:, q], stats[:, q])
                    step.then_inc(mean_var_done, 1)

                def centre(it, k, n, rows_, signal):
                    dve.wait_ge(rstd_done, batch(it, k, norms, n + 1))
                    for q in range(RT):
                        step = nc.vector.tensor_scalar(normed_x[:, q], rows_[:, q], mean_var[:, q, 0:1],
                                                       rstd[:, q:q + 1], ALU.subtract, ALU.mult)
                    step.then_inc(signal, 1)

                def norm_first(it, k):
                    b = k // heads % PER_LOOP
                    dve.wait_ge(x_loaded[b], it * 16 + (k // SLOTS * 16 + 16))
                    mean_and_variance(it, k, 0, x_sb[:, b])

                def norm_middle(it, k):
                    b = k // heads % PER_LOOP
                    if own_norm:
                        centre(it, k, 0, x_sb[:, b], centred)
                        dve.wait_ge(centred, batch(it, k, 1, 1))
                        nc.vector.tensor_scalar(normed_x[:], normed_x[:], 0.0, None, ALU.max).then_inc(rectified, 1)
                        dve.wait_ge(rectified, batch(it, k, 1, 1))
                        mean_and_variance(it, k, 1, normed_x)

                def norm_last(it, k):
                    b = k // heads % PER_LOOP
                    centre(it, k, norms - 1, normed_x if own_norm else x_sb[:, b], normed_done)

                def mask_scores(it, k, q):
                    b = k // heads % PER_LOOP
                    if k % heads == 0 and q == 0:
                        dve.wait_ge(mask_ready, batch(it, k, 1, 1))
                    own_wait(dve, scores_done, head(it, k, RT, q + 1), passed)
                    nc.vector.tensor_tensor_reduce(
                        probs[:, k % 4, q], scores_ps[:, q % 2], mask[:, b, q], -SCALE, LEAST,
                        ALU.add, ALU.min, row_shift[:, k % 4, q:q + 1],
                    ).then_inc(masked, 1)

                def recip(it, k):
                    dve.wait_ge(exp_done, head(it, k, RT, RT))
                    nc.vector.reciprocal(row_recip[:, k % 4], row_sum[:, k % 4]).then_inc(recip_done, 1)

                def add_attention(it, k):
                    b = k // heads % PER_LOOP
                    dve.wait_ge(y_done, batch(it, k, 1, 1))
                    dve.wait_ge(res_ready, batch(it, k, 1, 1))
                    for half in range(2):
                        part = slice(2 * half, 2 * half + 2)
                        nc.vector.tensor_tensor(res[:, b, part], y_ps[:, part], res[:, b, part], ALU.add).then_inc(y_added, 1)

                def slot(it, k):
                    norming = norms_ahead(it, k)
                    if norming:
                        norm_first(it, k + 1 + GROUP)
                    for q in range(RT):
                        if q == RT - 1 and k >= 2 and (k - 2) % heads == heads - 1:
                            add_attention(it, k - 2)
                        if q == 1 and exists(it, k + 1):
                            recip(it, k + 1)
                        if exists(it, k):
                            dve.wait_ge(pT_hi, head(it, k, RT, q + 1))
                            nc.vector.tensor_tensor(pT[LO][:, q], pT_ps[:, q % 2], exact(pT[HI][:, q]), ALU.subtract).then_inc(pT_lo, 1)
                        if k >= 1 and exists(it, k - 1) and q == RT - 2:
                            dve.wait_ge(oT_hi, head(it, k))
                            nc.vector.tensor_tensor(oT[LO][:], oT_ps[:], exact(oT[HI][:]), ALU.subtract).then_inc(oT_lo, 1)
                        if q % 2 and front_exists(it, k):
                            front(it, front_slot(k), k % 4, q // 2, chunk(it, k, 0))
                        if exists(it, k + LEAD):
                            mask_scores(it, k + LEAD, q)
                        if q % 2 and norming:
                            (norm_last if q > 1 else norm_middle)(it, k + 1 + GROUP)

                def norm(k):
                    for stage in (norm_first, norm_middle, norm_last):
                        stage(0, k)

                norm(0)
                dve.wait_ge(consts_in, 48 if own_norm else 16)
                for n, (s, k) in enumerate(BEFORE):
                    for part in range(2):
                        front(0, k, s, part, 2 * n)
                for k in range(LEAD):
                    for q in range(RT):
                        mask_scores(0, k, q)
                    if k == 0:
                        recip(0, 0)
                if refreshes(0):
                    norm(GROUP)
                for k in range(FIRST):
                    slot(0, k)
                with dve.Fori(0, LOOPS - 1) as it:
                    for k in range(FIRST, SLOTS + FIRST):
                        slot(it, k)
                for k in range(FIRST, SLOTS + 2):
                    slot(LOOPS - 1, k)

            @block.tensor
            def _(pe):
                def front_hT(it, k, part, c):
                    if part == 0:
                        pe.wait_ge(normed_done, batch(it, k, 1, 1))
                    for q in range(RT):
                        mm = nc.tensor.transpose(front_ps[:, q * P:(q + 1) * P], normed_x[:, q, part * P:(part + 1) * P], ident[:])
                    return mm

                def front_qk(it, k, part, c):
                    if own_norm and part == 0:
                        pe.wait_ge(hT_ready, batch(it, k, CT, CT))
                    at = k // 2 * P % inner
                    for n, (i, j) in enumerate(PASSES):
                        for t in range(CT):
                            mm = nc.tensor.matmul(front_ps[:], wqkv[i][:, t, part, at:at + P], hT[j][:, t],
                                                  start=(n + t == 0), stop=(n == 2 and t == CT - 1))
                    return mm

                def front_v(it, k, part, c):
                    at = k // GROUP * GROUP * HEAD % inner
                    for m in range(2):
                        q = 2 * part + m
                        for n, (i, j) in enumerate(PASSES):
                            for t in range(CT):
                                mm = nc.tensor.matmul(
                                    front_ps[:, m * DIM:(m + 1) * DIM], hT[i][:, t, q * P:(q + 1) * P],
                                    wqkv[j][:, t, 2, at:at + GROUP * HEAD],
                                    start=(n + t == 0), stop=(n == 2 and t == CT - 1))
                    return mm

                def front(it, k, s, part, c):
                    if not isinstance(c, int) or c >= 1:
                        pe.wait_ge(front_read, c)
                    mm = (front_hT, front_qk, front_v, front_qk)[s](it, k, part, c)
                    mm.then_inc(front_done, 1)

                def scores(it, k, q, c):
                    if k % 2 == 0 and q == 0:
                        pe.wait_ge(front_read, c)
                    at, pair = k % 2 * HEAD, k // 2 % 2
                    tile = head(it, k, RT, q - 1)
                    if not isinstance(tile, int) or tile > 0:
                        pe.wait_ge(masked, tile)
                    for n, (i, j) in enumerate(PASSES):
                        mm = nc.tensor.matmul(
                            scores_ps[:, q % 2], qT[i][at:at + HEAD, pair, q * P:(q + 1) * P],
                            kT[j][at:at + HEAD, pair], start=(n == 0), stop=(n == 2))
                    mm.then_inc(scores_done, 1)

                def transpose(it, k, t):
                    if t == 0:
                        pe.wait_ge(probs_ready, head(it, k, RT, RT))
                    tile = head(it, k, RT, t - 1)
                    if not isinstance(tile, int) or tile > 0:
                        pe.wait_ge(pT_lo, tile)
                    for q in range(RT):
                        mm = nc.tensor.transpose(pT_ps[:, t % 2, q * P:(q + 1) * P],
                                                 probs[:, k % 4, q, t * P:(t + 1) * P], ident[:])
                    mm.then_inc(pT_done, 1)

                def times_values(it, k, t, c):
                    if t == 0:
                        if k % GROUP == 0:
                            pe.wait_ge(front_read, c)
                        before = head(it, k)
                        if not isinstance(before, int) or before > 0:
                            pe.wait_ge(oT_lo, before)
                    pe.wait_ge(pT_lo, head(it, k, RT, t + 1))
                    for i in (HI, LO):
                        mm = nc.tensor.matmul(oT_ps[:], v_sb[:, k // GROUP % 2, t, k % GROUP], pT[i][:, t],
                                              start=(t == 0 and i == HI), stop=(t == RT - 1 and i == LO))
                    if t == RT - 1:
                        mm.then_inc(oT_done, 1)

                def project(it, k, q):
                    h = k % heads
                    if q == 0:
                        pe.wait_ge(oT_lo, head(it, k, 1, 1))
                        before = batch(it, k, 2, 0)
                        if h == 0 and (not isinstance(before, int) or before > 0):
                            pe.wait_ge(y_added, before)
                    for n, (i, j) in enumerate(PASSES):
                        mm = nc.tensor.matmul(
                            y_ps[:, q], oT[i][:, q * P:(q + 1) * P], wout[j][:, h],
                            start=(h == 0 and q % 2 == 0 and n == 0), stop=(h == heads - 1 and n == 2),
                            skip_group_check=True)
                    if h == heads - 1 and q == RT - 1:
                        mm.then_inc(y_done, 1)

                def slot(it, k):
                    for q in range(RT):
                        weighs = k >= 1 and exists(it, k - 1)
                        if weighs and q < RT - 1:
                            times_values(it, k - 1, q, 8 if k == 1 else chunk(it, k - 3, 2))
                        if exists(it, k):
                            transpose(it, k, q)
                        if k >= 2:
                            for tile in PROJECTED[q]:
                                project(it, k - 2, tile)
                        if weighs and q == RT - 2:
                            times_values(it, k - 1, RT - 1, 0)
                        if q % 2 and front_exists(it, k):
                            front(it, front_slot(k), k % 4, q // 2, chunk(it, k, q // 2))
                        if exists(it, k + LEAD):
                            scores(it, k + LEAD, q, 6 if k == 0 else chunk(it, k - 1, 2))

                pe.wait_ge(ident_made, 2)
                for n, (s, k) in enumerate(BEFORE):
                    if n == 1:
                        pe.wait_ge(weights_lo, 2)
                    for part in range(2):
                        front(0, k, s, part, 2 * n + part)
                for k in range(LEAD):
                    for q in range(RT):
                        scores(0, k, q, 4)
                for k in range(FIRST):
                    slot(0, k)
                with pe.Fori(0, LOOPS - 1) as it:
                    for k in range(FIRST, SLOTS + FIRST):
                        slot(it, k)
                for k in range(FIRST, SLOTS + 2):
                    slot(LOOPS - 1, k)


def gated_layer(nc, layer, x_in, x_out, adj_t, w_rows, w_cols, attn_t, b_heads, mix, small, gate_bias):
    HEADS = w_rows.shape[1]
    GR = DIM + 1
    SLOTS = PER_LOOP * HEADS
    HEADS_ALL = BATCHES * HEADS
    FIRST = HEADS
    FC, G1, G2 = range(3)

    with ExitStack() as ctx:
        sem = layer_semaphores(nc, ctx, layer)

        def sb(name, shape, dt, to=ctx):
            return to.enter_context(nc.sbuf_tensor(f"{layer}_{name}", shape, dt))

        w_sb = [sb(f"w{i}", [P, CT, HEADS * DIM], F32R) for i in (HI, LO)]
        gw_sb = [sb(f"gw{i}", [P, CT, HEADS, DIM], F32R) for i in (HI, LO)]
        mix_sb = [sb(f"mix{i}", [P, HEADS * CT, DIM], F32R) for i in (HI, LO)]
        small_sb = [sb(f"small{i}", [P, 3, CT, DIM], F32R) for i in (HI, LO)]
        wh_bias = sb("wh_bias", [P, HEADS * DIM], F32)
        s_weights = sb("s_weights", [P, CT, HEADS], F32)
        g_bias = sb("g_bias", [P, CT, HEADS], F32)
        s_bias = sb("s_bias", [P, HEADS], F32)
        half_gate_bias = sb("half_gate_bias", [P, CT], F32)
        ident = sb("ident", [P, P], F32)
        minus_half = sb("minus_half", [P, RT], F32)

        with ExitStack() as pre:
            w_stage = sb("w_stage", [P, CT * HEADS * DIM], F32, pre)
            mix_stage = sb("mix_stage", [P, HEADS * CT * DIM], F32, pre)
            small_stage = sb("small_stage", [P, 3 * CT * DIM], F32, pre)
            wb = sb("wb", [P, CT, HEADS, GR], F32, pre)
            attn_sb = sb("attn_sb", [P, CT, HEADS, DIM], F32, pre)
            aw = sb("aw", [P, CT, HEADS, GR], F32, pre)
            b_attn_b = sb("b_attn_b", [P, CT, HEADS], F32, pre)
            gate_bias_sb = sb("gate_bias_sb", [P, CT], F32, pre)
            ones = sb("ones", [P, P], F32, pre)
            banks = pre.enter_context(nc.psum_tensor(f"{layer}_banks", [P, 2 * HEADS, ROWS], F32))

            staged_in = [sem(f"staged_in{n}") for n in range(3)]
            rows_in = sem("rows_in")
            biases_in = sem("biases_in")
            weights_hi = sem("weights_hi")
            weights_lo = sem("weights_lo")
            ident_made = sem("ident_made")
            ones_made = sem("ones_made")
            aw_done = sem("aw_done")
            aw_kept = sem("aw_kept")
            gw_done = sem("gw_done")
            gw_hi = sem("gw_hi")
            gw_lo = sem("gw_lo")
            b_attn_b_made = sem("b_attn_b_made")
            vectors_done = sem("vectors_done")
            vectors_kept = sem("vectors_kept")

            with nc.Block() as block:
                @block.sync
                def _(sync):
                    with nc.allow_non_contiguous_dma(reason="columns of biases"):
                        for t in range(CT):
                            sync.dma_start(wb[:, t, :, 0:DIM], w_rows[t * P:(t + 1) * P]).then_inc(rows_in, 16)
                            sync.dma_start(wb[:, t, :, DIM], b_heads[:, t * P:(t + 1) * P].rearrange("h p -> p h")).then_inc(rows_in, 16)
                        sync.dma_start(attn_sb[:], attn_t.rearrange("(t p) h o -> p t h o", p=P)).then_inc(rows_in, 16)
                        sync.dma_start(gate_bias_sb[:], gate_bias.rearrange("(t p) -> p t", p=P)).then_inc(biases_in, 16)
                    sync.dma_start(wh_bias[:], b_heads.rearrange("h o -> (h o)").rearrange("(a n) -> a n", a=1).to_broadcast([P, HEADS * DIM])).then_inc(biases_in, 16)

                split_weights(nc, block, [
                    ([(w_stage[:].rearrange("p (t n) -> p t n", t=CT), w_cols.rearrange("(t p) n -> p t n", p=P))],
                     w_stage[:], *(w[:].rearrange("p t n -> p (t n)") for w in w_sb)),
                    ([(mix_stage[:].rearrange("p (t n) -> p t n", t=HEADS * CT), mix.rearrange("(t p) n -> p t n", p=P))],
                     mix_stage[:], *(w[:].rearrange("p t n -> p (t n)") for w in mix_sb)),
                    ([(small_stage[:].rearrange("p (a t n) -> p a t n", a=3, t=CT)[:, a], w.rearrange("(t p) n -> p t n", p=P))
                      for a, w in enumerate(small)],
                     small_stage[:], *(w[:].rearrange("p a t n -> p (a t n)") for w in small_sb)),
                ], (staged_in, weights_hi, weights_lo))
                identity_matrix(nc, block, ident[:], ident_made)

                @block.gpsimd
                def _(pool):
                    nc.gpsimd.memset(ones[:], 1.0).then_inc(ones_made, 1)
                    nc.gpsimd.memset(minus_half[:], -0.5).then_inc(ones_made, 1)

                @block.tensor
                def _(pe):
                    pe.wait_ge(rows_in, 80)
                    for h in range(HEADS):
                        for o in range(CT):
                            for t in range(CT):
                                mm = nc.tensor.matmul(banks[:, h * CT + o, 0:GR], attn_sb[:, t, h, o * P:(o + 1) * P],
                                                      wb[:, t, h], start=(t == 0), stop=(t == CT - 1))
                            mm.then_inc(aw_done, 1)
                    for h in range(HEADS):
                        pe.wait_ge(aw_kept, CT * (h + 1))
                        for i in range(CT):
                            for t in range(CT):
                                mm = nc.tensor.matmul(banks[:, h * CT + i, 0:GR], aw[:, t, h, i * P:(i + 1) * P],
                                                      wb[:, t, h], start=(t == 0), stop=(t == CT - 1))
                            mm.then_inc(gw_done, 1)
                    pe.wait_ge(gw_lo, CT)
                    for i in range(CT):
                        for h in range(HEADS):
                            for t in range(CT):
                                nc.tensor.matmul(banks[:, 0, i * HEADS + h:i * HEADS + h + 1], wb[:, t, h, i * P:(i + 1) * P],
                                                 aw[:, t, h, DIM:GR], start=(t == 0), stop=(t == CT - 1))
                    pe.wait_ge(b_attn_b_made, 1)
                    pe.wait_ge(ones_made, 1)
                    for t in range(CT):
                        mm = nc.tensor.matmul(banks[:, 1, 0:HEADS], ones[:], b_attn_b[:, t], start=(t == 0), stop=(t == CT - 1))
                    mm.then_inc(vectors_done, 1)

                @block.scalar
                def _(act):
                    for h in range(HEADS):
                        for i in range(CT):
                            act.wait_ge(gw_done, h * CT + i + 1)
                            nc.scalar.activation(gw_sb[HI][:, i, h], banks[:, h * CT + i, 0:DIM], ACT.Copy).then_inc(gw_hi, 1)
                    act.wait_ge(biases_in, 32)
                    nc.scalar.activation(half_gate_bias[:], gate_bias_sb[:], ACT.Copy, scale=0.5)

                @block.vector
                def _(dve):
                    for h in range(HEADS):
                        for o in range(CT):
                            dve.wait_ge(aw_done, h * CT + o + 1)
                            nc.vector.tensor_copy(aw[:, o, h], banks[:, h * CT + o, 0:GR]).then_inc(aw_kept, 1)
                    dve.wait_ge(rows_in, 80)
                    dve.wait_ge(aw_kept, HEADS * CT)
                    nc.vector.tensor_tensor(b_attn_b[:], wb[:, :, :, DIM], aw[:, :, :, DIM], ALU.mult).then_inc(b_attn_b_made, 1)
                    for h in range(HEADS):
                        for i in range(CT):
                            bank = banks[:, h * CT + i]
                            dve.wait_ge(gw_hi, h * CT + i + 1)
                            nc.vector.tensor_copy(s_weights[:, i, h:h + 1], bank[:, DIM:GR])
                            nc.vector.tensor_tensor(gw_sb[LO][:, i, h], bank[:, 0:DIM], exact(gw_sb[HI][:, i, h]), ALU.subtract).then_inc(gw_lo, 1)
                    dve.wait_ge(vectors_done, 1)
                    nc.vector.tensor_copy(g_bias[:].rearrange("p i h -> p (i h)"), banks[:, 0, 0:CT * HEADS])
                    nc.vector.tensor_copy(s_bias[:], banks[:, 1, 0:HEADS]).then_inc(vectors_kept, 1)
                    dve.wait_ge(vectors_kept, 1)

        x_sb = sb("x_sb", [P, PER_LOOP, RT, DIM], F32)
        res = sb("res", [P, PER_LOOP, RT, DIM], F32)
        adj_sb = sb("adj_sb", [P, PER_LOOP, RT, ROWS], U8)
        stats = sb("stats", [P, RT, 6], F32)
        mean_var = sb("mean_var", [P, RT, 2], F32)
        var_eps = sb("var_eps", [P, RT], F32)
        rstd = sb("rstd", [P, RT], F32)
        normed_x = sb("normed_x", [P, RT, DIM], F32)
        hT_full = sb("hT_full", [P, CT, ROWS], F32)
        hT = [sb(f"hT{i}", [P, PER_LOOP, CT, ROWS], F32R) for i in (HI, LO)]
        s_sb = sb("s_sb", [P, PER_LOOP, RT, HEADS], F32)
        gT = [sb(f"gT{i}", [P, 2, CT, ROWS], F32R) for i in (HI, LO)]
        wh_full = sb("wh_full", [P, RT, DIM], F32)
        wh = [sb(f"wh{i}", [P, 2, RT, DIM], F32R) for i in (HI, LO)]
        a_full = sb("a_full", [P, RT, ROWS], F32)
        a_sb = [sb(f"a{i}", [P, RT, ROWS], F32R) for i in (HI, LO)]
        hpT = [sb(f"hpT{i}", [P, CT, ROWS], F32R) for i in (HI, LO)]
        ha_full = sb("ha_full", [P, CT, ROWS], F32)
        ha = [sb(f"ha{i}", [P, CT, ROWS], F32R) for i in (HI, LO)]
        hf_full = sb("hf_full", [P, CT, ROWS], F32)
        hf = [sb(f"hf{i}", [P, CT, ROWS], F32R) for i in (HI, LO)]
        gate = sb("gate", [P, CT, ROWS], F32)

        def psum(name, shape):
            return ctx.enter_context(nc.psum_tensor(f"{layer}_{name}", shape, F32))

        scores_ps = psum("scores_ps", [P, 2, ROWS])
        front_ps = psum("front_ps", [P, 2, ROWS])
        hp_ps = psum("hp_ps", [P, CT, ROWS])
        ha_ps = psum("ha_ps", [P, CT, ROWS])

        x_loaded = [sem(f"x_loaded{i}") for i in range(PER_LOOP)]
        adj_loaded = [sem(f"adj_loaded{i}") for i in range(PER_LOOP)]
        res_loaded = [sem(f"res_loaded{i}") for i in range(PER_LOOP)]
        stored = [sem(f"stored{i}") for i in range(PER_LOOP)]
        passed = sem("passed")
        stats_done = sem("stats_done")
        mean_var_done = sem("mean_var_done")
        var_eps_done = sem("var_eps_done")
        rstd_done = sem("rstd_done")
        normed_done = sem("normed_done")
        front_done = sem("front_done")
        front_read = sem("front_read")
        front_full = sem("front_full")
        front_act = sem("front_act")
        wh_ready = sem("wh_ready")
        difference_done = sem("difference_done")
        opened = sem("opened")
        mixed = sem("mixed")
        added = sem("added")
        scores_done = sem("scores_done")
        masked = sem("masked")
        tanh_hi = sem("tanh_hi")
        tanh_full = sem("tanh_full")
        tanh_lo = sem("tanh_lo")
        hp_done = sem("hp_done")
        hp_hi = sem("hp_hi")
        hp_lo = sem("hp_lo")
        ha_done = sem("ha_done")
        ha_hi = sem("ha_hi")
        ha_lo = sem("ha_lo")

        def side_work(n):
            b, s = n // HEADS, n % HEADS
            if n == -1:
                at = [[("h", 0, 0), ("h", 1, 0), ("s", 0, 0), ("g", 0, 0), ("g", 1, 0), ("g", 0, 1), ("g", 1, 1),
                       ("w", 0, 0), ("w", 1, 0)], [], [], []]
            else:
                at = [[("g", 0, n + 2), ("g", 1, n + 2)], [("w", 0, n + 1)], [("w", 1, n + 1)], []]
                if s == 0:
                    at[1] += [("gate", 0, b - 1)]
                    at[2] += [("gate", 1, b - 1)]
                elif s == 1:
                    at[1] += [("h", 0, b + 1)]
                    at[2] += [("h", 1, b + 1)]
                    at[3] += [("s", 0, b + 1), ("back", 0, b - 1)]
                elif s == 2:
                    at[1] += [("back", 1, b - 1)]
                    at[2] += [("hf", 0, b)]
                elif s == 3:
                    at[2] += [("hf", 1, b)]

            def there(chunk):
                kind, _, to = chunk
                return 0 <= to < (HEADS_ALL if kind in "gw" else BATCHES)

            return [[c for c in point if there(c)] for point in at]

        LAST = HEADS_ALL + HEADS
        chunks = [(n, c) for n in range(-1, LAST) for point in side_work(n) for c in point]

        def before(kinds, n, c):
            at = chunks.index((n, c))
            return sum(x[0] in kinds for _, x in chunks[:at])

        def through(kinds, n, kind, part):
            at = next(i for i, (_, c) in enumerate(chunks) if c == (kind, part, n))
            return sum(x[0] in kinds for _, x in chunks[:at + 1])

        ALL = ("h", "s", "g", "w", "gate", "back", "hf")
        BY_ACT = ("h", "g", "w", "gate", "hf")

        def per_loop(kinds):
            return sum(c[0] in kinds for n, c in chunks if FIRST <= n < FIRST + SLOTS)

        def times(it, each, value):
            return it * each + value

        def exists(n):
            return n < HEADS_ALL

        def parity(n):
            return n // HEADS % PER_LOOP

        def slots(engine, slot):
            for n in range(FIRST):
                slot(0, n)
            with engine.Fori(0, LOOPS - 1) as it:
                for n in range(FIRST, FIRST + SLOTS):
                    slot(it, n)
            for n in range(FIRST + SLOTS * (LOOPS - 1), LAST):
                slot(0, n)

        rows = "b (t p) c -> b p t c"
        x_src = x_in.rearrange(rows, p=P)
        x_dst = x_out.rearrange(rows, p=P)
        adj_src = adj_t.rearrange(rows, p=P)

        with nc.Block() as block:
            @block.sync
            def _(sync):
                def load(b, source):
                    sync.dma_start(x_sb[:, b], x_src[source]).then_inc(x_loaded[b], 16)
                    sync.dma_start(adj_sb[:, b], adj_src[source]).then_inc(adj_loaded[b], 16)

                for b in range(PER_LOOP):
                    load(b, b)
                    sync.dma_start(res[:, b], x_src[b]).then_inc(res_loaded[b], 16)
                with sync.Fori(0, LOOPS - 1) as it:
                    for b in range(PER_LOOP):
                        own_wait(sync, normed_done, times(it, PER_LOOP, b + 1), passed)
                        own_wait(sync, masked, times(it, PER_LOOP * HEADS * RT, (b + 1) * HEADS * RT), passed)
                        load(b, it * PER_LOOP + (b + PER_LOOP))
                        own_wait(sync, added, times(it, PER_LOOP * 2, 2 * b + 2), passed)
                        sync.dma_start(x_dst[it * PER_LOOP + b], res[:, b]).then_inc(stored[b], 16)
                        own_wait(sync, stored[b], times(it, 16, 16), passed)
                        sync.dma_start(res[:, b], x_src[it * PER_LOOP + (b + PER_LOOP)]).then_inc(res_loaded[b], 16)
                for b in range(PER_LOOP):
                    sync.wait_ge(added, 2 * (BATCHES - PER_LOOP + b + 1))
                    sync.dma_start(x_dst[BATCHES - PER_LOOP + b], res[:, b]).then_inc(stored[b], 16)
                for b in range(PER_LOOP):
                    sync.wait_ge(stored[b], 16 * LOOPS)

            @block.gpsimd
            def _(pool):
                def rstd_step(it, b):
                    own_wait(pool, mean_var_done, times(it, PER_LOOP, b + 1), passed)
                    nc.gpsimd.tensor_scalar(var_eps[:], mean_var[:, :, 1], EPS, 1.0, ALU.add, ALU.mult).then_inc(var_eps_done, 1)
                    pool.wait_ge(var_eps_done, times(it, PER_LOOP, b + 1))
                    nc.gpsimd.tensor_tensor(rstd[:], var_eps[:], minus_half[:], ALU.pow).then_inc(rstd_done, 1)

                def side(it, n, c):
                    kind, part, to = c
                    acted = times(it, per_loop(BY_ACT), before(BY_ACT, n, c) + 1)
                    if kind == "w":
                        pool.wait_ge(front_act, acted)
                        at = slice(2 * part, 2 * part + 2)
                        nc.gpsimd.tensor_tensor(wh[LO][:, to % 2, at], wh_full[:, at], exact(wh[HI][:, to % 2, at]),
                                                ALU.subtract).then_inc(wh_ready, 1)
                    elif kind == "gate":
                        pool.wait_ge(front_act, acted)
                        nc.gpsimd.tensor_tensor(hf_full[:, part], hf_full[:, part], ha_full[:, part],
                                                ALU.subtract).then_inc(difference_done, 1)

                def tanh_rest(it, n, t):
                    pool.wait_ge(tanh_full, times(it, SLOTS * RT, n * RT + t + 1))
                    nc.gpsimd.tensor_tensor(a_sb[LO][:, t], a_full[:, t], exact(a_sb[HI][:, t]), ALU.subtract).then_inc(tanh_lo, 1)

                def slot(it, n):
                    if n % HEADS == 0 and exists(n + HEADS):
                        rstd_step(it, n // HEADS + 1)
                    work = side_work(n)
                    for t in range(RT):
                        if exists(n + 1):
                            tanh_rest(it, n + 1, t)
                        for c in work[t] if t else []:
                            side(it, n, c)

                rstd_step(0, 0)
                for c in side_work(-1)[0]:
                    side(0, -1, c)
                for t in range(RT):
                    tanh_rest(0, 0, t)
                slots(pool, slot)

            @block.scalar
            def _(act):
                def side(it, n, c):
                    kind, part, to = c
                    bank = front_ps[:, before(ALL, n, c) % 2]
                    done = times(it, per_loop(ALL), before(ALL, n, c) + 1)
                    if kind == "h":
                        act.wait_ge(front_done, done)
                        nc.scalar.activation(hT[HI][:, to % PER_LOOP, part], bank, ACT.Relu).then_inc(front_act, 1)
                    elif kind == "g":
                        act.wait_ge(front_done, done)
                        nc.scalar.activation(gT[HI][:, to % 2, part], bank, ACT.Identity,
                                             bias=g_bias[:, part, to % HEADS:to % HEADS + 1]).then_inc(front_act, 1)
                    elif kind == "w":
                        at = slice(2 * part, 2 * part + 2)
                        act.wait_ge(front_read, done)
                        nc.scalar.activation(wh[HI][:, to % 2, at], wh_full[:, at], ACT.Copy).then_inc(front_act, 1)
                    elif kind == "gate":
                        act.wait_ge(front_done, done)
                        nc.scalar.activation(gate[:, part], bank, ACT.Tanh, scale=0.5,
                                             bias=half_gate_bias[:, part:part + 1]).then_inc(front_act, 1)
                    elif kind == "hf":
                        act.wait_ge(front_done, done)
                        nc.scalar.activation(hf[HI][:, part], bank, ACT.Copy).then_inc(front_act, 1)

                def tanhs(it, n, t):
                    act.wait_ge(masked, times(it, SLOTS * RT, n * RT + t + 1))
                    nc.scalar.activation(a_sb[HI][:, t], a_full[:, t], ACT.Tanh).then_inc(tanh_hi, 1)
                    act.wait_ge(tanh_hi, times(it, SLOTS * RT, n * RT + t + 1))
                    nc.scalar.activation(a_full[:, t], a_full[:, t], ACT.Tanh).then_inc(tanh_full, 1)

                def slot(it, n):
                    work = side_work(n)
                    for c in work[0]:
                        side(it, n, c)
                    for t in range(RT):
                        if t == RT - 1 and exists(n):
                            act.wait_ge(hp_done, times(it, SLOTS, n + 1))
                            for i in range(CT):
                                nc.scalar.activation(hpT[HI][:, i], hp_ps[:, i], ACT.Relu).then_inc(hp_hi, 1)
                        if exists(n + 1):
                            tanhs(it, n + 1, t)
                        if t == 0 and n % HEADS == 0 and 0 < n <= HEADS_ALL:
                            act.wait_ge(ha_done, times(it, PER_LOOP, n // HEADS))
                            for i in range(CT):
                                nc.scalar.activation(ha_full[:, i], ha_ps[:, i], ACT.Copy)
                                nc.scalar.activation(ha[HI][:, i], ha_ps[:, i], ACT.Copy).then_inc(ha_hi, 1)
                        for c in work[t] if t else []:
                            side(it, n, c)

                for c in side_work(-1)[0]:
                    side(0, -1, c)
                for t in range(RT):
                    tanhs(0, 0, t)
                slots(act, slot)

            @block.vector
            def _(dve):
                def norm_first(it, b):
                    p = b % PER_LOOP
                    dve.wait_ge(x_loaded[p], times(it, 16, b // PER_LOOP * 16 + 16))
                    for q in range(RT):
                        step = nc.vector.bn_stats(stats[:, q], x_sb[:, p, q])
                    step.then_inc(stats_done, 1)
                    own_wait(dve, stats_done, times(it, PER_LOOP, b + 1), passed)
                    for q in range(RT):
                        step = nc.vector.bn_aggr(mean_var[:, q], stats[:, q])
                    step.then_inc(mean_var_done, 1)

                def norm_last(it, b):
                    dve.wait_ge(rstd_done, times(it, PER_LOOP, b + 1))
                    for q in range(RT):
                        step = nc.vector.tensor_scalar(normed_x[:, q], x_sb[:, b % PER_LOOP, q], mean_var[:, q, 0:1],
                                                       rstd[:, q:q + 1], ALU.subtract, ALU.mult)
                    step.then_inc(normed_done, 1)

                def side(it, n, c):
                    kind, part, to = c
                    bank = front_ps[:, before(ALL, n, c) % 2]
                    done = times(it, per_loop(ALL), before(ALL, n, c) + 1)
                    acted = times(it, per_loop(BY_ACT), before(BY_ACT, n, c) + 1)
                    if kind == "h":
                        dve.wait_ge(front_act, acted)
                        nc.vector.tensor_scalar(hT_full[:, part], bank, 0.0, None, ALU.max)
                        nc.vector.scalar_tensor_tensor(hT[LO][:, to % PER_LOOP, part], bank, 0.0,
                                                       exact(hT[HI][:, to % PER_LOOP, part]),
                                                       ALU.max, ALU.subtract).then_inc(front_read, 1)
                    elif kind == "s":
                        dve.wait_ge(front_done, done)
                        nc.vector.tensor_tensor(
                            s_sb[:, to % PER_LOOP], bank[:, 0:RT * HEADS].rearrange("p (t h) -> p t h", t=RT),
                            s_bias[:].unsqueeze(1).to_broadcast([P, RT, HEADS]), ALU.add).then_inc(front_read, 1)
                    elif kind == "g":
                        dve.wait_ge(front_act, acted)
                        nc.vector.scalar_tensor_tensor(
                            gT[LO][:, to % 2, part], bank, g_bias[:, part, to % HEADS:to % HEADS + 1],
                            exact(gT[HI][:, to % 2, part]), ALU.add, ALU.subtract).then_inc(front_read, 1)
                    elif kind == "w":
                        if to > 0:
                            dve.wait_ge(wh_ready, times(it, SLOTS * 2, 2 * to))
                        dve.wait_ge(front_done, done)
                        h = to % HEADS
                        bias = wh_bias[:, h * DIM:(h + 1) * DIM].unsqueeze(1).to_broadcast([P, 2, DIM])
                        nc.vector.tensor_tensor(wh_full[:, 2 * part:2 * part + 2], bank.rearrange("p (t o) -> p t o", t=2),
                                                bias, ALU.add).then_inc(front_read, 1)
                    elif kind == "gate":
                        dve.wait_ge(front_act, acted)
                        dve.sem_inc(front_read, 1)
                    elif kind == "back":
                        p, at = to % PER_LOOP, slice(2 * part, 2 * part + 2)
                        dve.wait_ge(front_done, done)
                        dve.wait_ge(res_loaded[p], times(it, 16, to // PER_LOOP * 16 + 16))
                        nc.vector.tensor_tensor(res[:, p, at], bank.rearrange("p (t o) -> p t o", t=2), res[:, p, at],
                                                ALU.add).then_inc(added, 1)
                        dve.wait_ge(added, times(it, PER_LOOP * 2, to * 2 + part + 1))
                        dve.sem_inc(front_read, 1)
                    elif kind == "hf":
                        dve.wait_ge(front_act, acted)
                        nc.vector.tensor_tensor(hf[LO][:, part], bank, exact(hf[HI][:, part]), ALU.subtract)
                        nc.vector.tensor_copy(hf_full[:, part], bank).then_inc(front_read, 1)

                def mix_gate(it, b):
                    for part in range(CT):
                        dve.wait_ge(difference_done, times(it, PER_LOOP * CT, b * CT + part + 1))
                        nc.vector.scalar_tensor_tensor(gate[:, part], gate[:, part], 1.0, hf_full[:, part],
                                                       ALU.add, ALU.mult).then_inc(opened, 1)
                    for part in range(CT):
                        dve.wait_ge(opened, times(it, PER_LOOP * CT, b * CT + part + 1))
                        nc.vector.scalar_tensor_tensor(gate[:, part], gate[:, part], 0.5, ha_full[:, part],
                                                       ALU.mult, ALU.add).then_inc(mixed, 1)

                def mask_scores(it, n, t):
                    p, h = parity(n), n % HEADS
                    if h == 0 and t == 0:
                        dve.wait_ge(adj_loaded[p], times(it, 16, n // HEADS // PER_LOOP * 16 + 16))
                    if n > 0:
                        dve.wait_ge(tanh_lo, times(it, SLOTS * RT, (n - 1) * RT + t + 1))
                    dve.wait_ge(scores_done, times(it, SLOTS * RT, n * RT + t + 1))
                    nc.vector.scalar_tensor_tensor(a_full[:, t], scores_ps[:, t % 2], s_sb[:, p, t, h:h + 1], adj_sb[:, p, t],
                                                   ALU.add, ALU.mult).then_inc(masked, 1)

                def slot(it, n):
                    ahead = n % HEADS == 0 and exists(n + HEADS)
                    work = side_work(n)
                    for c in work[0]:
                        side(it, n, c)
                    if ahead:
                        norm_first(it, n // HEADS + 1)
                    for t in range(RT):
                        if t == RT - 1 and exists(n):
                            for i in range(CT):
                                dve.wait_ge(hp_hi, times(it, SLOTS * CT, n * CT + i + 1))
                                nc.vector.scalar_tensor_tensor(hpT[LO][:, i], hp_ps[:, i], 0.0, exact(hpT[HI][:, i]),
                                                               ALU.max, ALU.subtract).then_inc(hp_lo, 1)
                        if exists(n + 1):
                            mask_scores(it, n + 1, t)
                        if t == 1 and ahead:
                            norm_last(it, n // HEADS + 1)
                        if t == 0 and n % HEADS == 0 and 0 < n <= HEADS_ALL:
                            for i in range(CT):
                                dve.wait_ge(ha_hi, times(it, PER_LOOP * CT, (n // HEADS - 1) * CT + i + 1))
                                nc.vector.tensor_tensor(ha[LO][:, i], ha_ps[:, i], exact(ha[HI][:, i]), ALU.subtract).then_inc(ha_lo, 1)
                        if t == 0 and n % HEADS == 1 and n > HEADS:
                            mix_gate(it, n // HEADS - 1)
                        for c in work[t] if t else []:
                            side(it, n, c)

                norm_first(0, 0)
                norm_last(0, 0)
                for c in side_work(-1)[0]:
                    side(0, -1, c)
                for t in range(RT):
                    mask_scores(0, 0, t)
                slots(dve, slot)

            @block.tensor
            def _(pe):
                def three_passes(out, pairs):
                    for n, (i, j) in enumerate(PASSES):
                        for m, (left, right) in enumerate(pairs):
                            mm = nc.tensor.matmul(out, left[i], right[j], start=(n + m == 0),
                                                  stop=(n == 2 and m == len(pairs) - 1))
                    return mm

                def halves(pair, *at):
                    return [x[(slice(None), *at)] for x in pair]

                def side(it, n, c):
                    kind, part, to = c
                    number = before(ALL, n, c)
                    bank = front_ps[:, number % 2]
                    if number >= 2:
                        pe.wait_ge(front_read, times(it, per_loop(ALL), number - 1))
                    at = slice(part * P, (part + 1) * P)
                    b = to % PER_LOOP if kind not in "gw" else parity(to)
                    if kind == "h":
                        if part == 0:
                            pe.wait_ge(normed_done, times(it, PER_LOOP, to + 1))
                        for q in range(RT):
                            mm = nc.tensor.transpose(bank[:, q * P:(q + 1) * P], normed_x[:, q, at], ident[:])
                    elif kind == "s":
                        pe.wait_ge(front_read, times(it, per_loop(ALL), through(ALL, to, "h", 1)))
                        for q in range(RT):
                            for t in range(CT):
                                mm = nc.tensor.matmul(bank[:, q * HEADS:(q + 1) * HEADS], hT_full[:, t, q * P:(q + 1) * P],
                                                      s_weights[:, t], start=(t == 0), stop=(t == CT - 1))
                    elif kind == "g":
                        if to % HEADS == 0 and part == 0:
                            pe.wait_ge(front_read, times(it, per_loop(ALL), through(ALL, to // HEADS, "h", 1)))
                        mm = three_passes(bank, [(halves(gw_sb, t, to % HEADS, at), halves(hT, b, t)) for t in range(CT)])
                    elif kind == "w":
                        h = to % HEADS
                        for m in range(2):
                            q = 2 * part + m
                            mm = three_passes(bank[:, m * DIM:(m + 1) * DIM], [
                                (halves(hT, b, t, slice(q * P, (q + 1) * P)), halves(w_sb, t, slice(h * DIM, (h + 1) * DIM)))
                                for t in range(CT)])
                    elif kind == "hf":
                        mm = three_passes(bank, [(halves(small_sb, FC, t, at), halves(hT, b, t)) for t in range(CT)])
                    elif kind == "gate":
                        if part == 0:
                            pe.wait_ge(ha_lo, times(it, PER_LOOP * CT, (to + 1) * CT))
                            pe.wait_ge(front_read, times(it, per_loop(ALL), through(ALL, to, "hf", 1)))
                        mm = three_passes(bank, [(halves(small_sb, G1, t, at), halves(hf, t)) for t in range(CT)]
                                          + [(halves(small_sb, G2, t, at), halves(ha, t)) for t in range(CT)])
                    elif kind == "back":
                        pe.wait_ge(mixed, times(it, PER_LOOP * CT, (to + 1) * CT))
                        for m in range(2):
                            q = 2 * part + m
                            for t in range(CT):
                                mm = nc.tensor.transpose(bank[:, m * DIM + t * P:m * DIM + (t + 1) * P],
                                                         gate[:, t, q * P:(q + 1) * P], ident[:])
                    mm.then_inc(front_done, 1)

                def scores(it, n, t):
                    if t == 0:
                        pe.wait_ge(front_read, times(it, per_loop(ALL), through(ALL, n, "g", 1)))
                    tile = n * RT + t
                    if tile >= 2:
                        pe.wait_ge(masked, times(it, SLOTS * RT, tile - 1))
                    three_passes(scores_ps[:, t % 2], [
                        (halves(gT, n % 2, i, slice(t * P, (t + 1) * P)), halves(hT, parity(n), i)) for i in range(CT)
                    ]).then_inc(scores_done, 1)

                def times_wh(it, n, t):
                    if t == 0:
                        pe.wait_ge(wh_ready, times(it, SLOTS * 2, 2 * n + 2))
                        if n > 0:
                            pe.wait_ge(hp_lo, times(it, SLOTS * CT, n * CT))
                    pe.wait_ge(tanh_lo, times(it, SLOTS * RT, n * RT + t + 1))
                    for o in range(CT):
                        for m, (i, j) in enumerate(PASSES):
                            mm = nc.tensor.matmul(hp_ps[:, o], wh[i][:, n % 2, t, o * P:(o + 1) * P], a_sb[j][:, t],
                                                  start=(t == 0 and m == 0), stop=(t == RT - 1 and m == 2))
                    if t == RT - 1:
                        mm.then_inc(hp_done, 1)

                def mix_head(it, n):
                    h = n % HEADS
                    pe.wait_ge(hp_lo, times(it, SLOTS * CT, (n + 1) * CT))
                    if h == 0 and n > 0:
                        pe.wait_ge(ha_lo, times(it, PER_LOOP * CT, n // HEADS * CT))
                    for o in range(CT):
                        for m, (i, j) in enumerate(PASSES):
                            for t in range(CT):
                                mm = nc.tensor.matmul(
                                    ha_ps[:, o], mix_sb[i][:, h * CT + t, o * P:(o + 1) * P], hpT[j][:, t],
                                    start=(h == 0 and m + t == 0), stop=(h == HEADS - 1 and m == 2 and t == CT - 1))
                    if h == HEADS - 1:
                        mm.then_inc(ha_done, 1)

                def slot(it, n):
                    work = side_work(n)
                    for c in work[0]:
                        side(it, n, c)
                    for t in range(RT):
                        if exists(n):
                            times_wh(it, n, t)
                        if exists(n + 1):
                            scores(it, n + 1, t)
                        if t == 0 and n > 0 and exists(n - 1):
                            mix_head(it, n - 1)
                        for c in work[t] if t else []:
                            side(it, n, c)

                for c in side_work(-1)[0]:
                    side(0, -1, c)
                for t in range(RT):
                    scores(0, 0, t)
                slots(pe, slot)


def network(nc, x, adj, adj_t, l0, l1, l2, l3, out):
    x1, x2, x3 = (nc.dram_tensor(f"x{n}", x.shape, F32).ap() for n in (1, 2, 3))
    attention_layer(nc, "L0", x, x1, adj, *l0, heads=4)
    attention_layer(nc, "L1", x1, x2, adj, *l1[:3], heads=8, gamma=l1[3], beta=l1[4])
    gated_layer(nc, "L2", x2, x3, adj_t, *l2)
    attention_layer(nc, "L3", x3, out, adj, *l3, heads=4)


def kernel(**inputs):
    import numpy as _np
    import concourse.bacc as _bacc
    from concourse import mybir as _mybir
    from concourse.bass_utils import run_bass_kernel_spmd as _run

    nc = _bacc.Bacc("TRN2", target_bir_lowering=False, num_devices=1)
    arrays = {}
    inputs = {name: _np.asarray(a) for name, a in inputs.items()}

    def given(name, array):
        arrays[name] = _np.ascontiguousarray(array)
        dtype = _mybir.dt.from_np(arrays[name].dtype)
        return nc.dram_tensor(name, arrays[name].shape, dtype, kind="ExternalInput").ap()

    x = given("x", inputs["x"])
    adj = given("adj", inputs["adj"])
    adj_t = given("adj_t", inputs["adj"].transpose(0, 2, 1))

    def square_layer(n):
        w = _np.stack([inputs[f"L{n}_gnn_W{c}"] for c in "qkv"], axis=1)
        return given(f"L{n}_qkv", w), given(f"L{n}_Wo", inputs[f"L{n}_gnn_Wo"]), given(f"L{n}_bo", inputs[f"L{n}_gnn_bo"])

    w_qkv = inputs["L1_gnn_w_qkv"]
    l1 = (
        given("L1_qkv", w_qkv.reshape(3, -1, w_qkv.shape[1]).transpose(2, 0, 1)),
        given("L1_w_out", inputs["L1_gnn_w_out"].T), given("L1_b_out", inputs["L1_gnn_b_out"]),
        given("L1_gamma", inputs["L1_gnn_gamma"]), given("L1_beta", inputs["L1_gnn_beta"]),
    )
    w = inputs["L2_gnn_W"]
    l2 = (
        given("L2_W_rows", w.transpose(1, 0, 2)), given("L2_W_cols", w.transpose(2, 0, 1).reshape(w.shape[2], -1)),
        given("L2_attn_t", inputs["L2_gnn_attn"].transpose(2, 0, 1)), given("L2_bW", inputs["L2_gnn_bW"]),
        given("L2_A_w_t", inputs["L2_gnn_A_w"].T),
        tuple(given(f"L2_{c}_t", inputs[f"L2_gnn_{c}_w"].T) for c in ("fc", "g1", "g2")),
        given("L2_gbias", inputs["L2_gnn_gbias"]),
    )
    out = nc.dram_tensor("out", x.shape, _mybir.dt.float32, kind="ExternalOutput").ap()
    network(nc, x, adj, adj_t, square_layer(0), l1, l2, square_layer(3), out)
    r = _run(nc, [arrays], core_ids=[0])
    return r.results[0]["out"]
```

```python
from contextlib import ExitStack

import concourse.bass as bass
from concourse import mybir

ALU = mybir.AluOpType
ACT = mybir.ActivationFunctionType
F32 = mybir.dt.float32
F32R = mybir.dt.float32r
BF16 = mybir.dt.bfloat16
U8 = mybir.dt.uint8

P = 128
BATCHES = 16
ROWS = 512
DIM = 256
RT = ROWS // P
CT = DIM // P
HEAD = 64
GROUP = 4
PER_LOOP = 2
LOOPS = BATCHES // PER_LOOP
SCALE = HEAD**-0.5
EPS = 1e-5
BIG = 2.0**127
LEAST = 3.0e38

PASSES = ((0, 0), (0, 1), (1, 0))
HI, LO = 0, 1


def own_wait(engine, semaphore, value, passed):
    engine.wait_ge(semaphore, value)
    engine.sem_inc(passed, 1)


def exact(tile):
    return tile.bitcast(F32)


def layer_semaphores(nc, ctx, layer):
    given = []

    def sem(name):
        given.append(nc.alloc_semaphore(name=f"{layer}_{name}"))
        return given[-1]

    def give_back():
        nc.clear_and_free_semaphores(given)
        nc.all_engine_barrier()

    ctx.callback(give_back)
    return sem


def split_weights(nc, loads, sems):
    staged_in, hi_made, lo_made = sems

    def stage(sync):
        for n, (moves, _, _, _) in enumerate(loads):
            for to, source in moves:
                sync.dma_start(to, source).then_inc(staged_in[n], 16)

    def make_hi(act):
        for n, (moves, staged, hi, _) in enumerate(loads):
            act.wait_ge(staged_in[n], 16 * len(moves))
            nc.scalar.activation(hi, staged, ACT.Copy).then_inc(hi_made, 1)

    def make_lo(dve):
        for n, (_, staged, hi, lo) in enumerate(loads):
            dve.wait_ge(hi_made, n + 1)
            nc.vector.tensor_tensor(lo, staged, exact(hi), ALU.subtract).then_inc(lo_made, 1)

    return stage, make_hi, make_lo


def identity_matrix(nc, block, ident, made):
    @block.gpsimd
    def _(pool):
        nc.gpsimd.memset(ident, 0.0).then_inc(made, 1)
        pool.wait_ge(made, 1)
        nc.gpsimd.affine_select(
            out=ident, in_=ident, compare_op=ALU.not_equal, fill=1.0, base=0,
            pattern=[[-1, P]], channel_multiplier=1,
        ).then_inc(made, 1)


def attention_layer(nc, layer, x_in, x_out, adj, w_qkv, w_out, b_out, heads, gamma=None, beta=None):
    own_norm = gamma is not None
    inner = heads * HEAD
    SLOTS = PER_LOOP * heads
    HEADS_ALL = BATCHES * heads
    ROUNDS = LOOPS - 1 - (2 * GROUP >= SLOTS)
    FIRST = 5

    LEAD = 2
    CHUNK_AT = {0: 0, 2: 1}
    KEYS, QUERIES = 0, 1
    BEFORE = ((0, 0), (1, 0), (3, 2), (2, 0))
    BESIDE = 2

    def refreshes(k):
        return (k // GROUP + 1) * GROUP % heads == 0

    def chunks_of(k):
        return 2 if k % 4 != 0 or refreshes(k) else 0

    def chunks_before(k):
        return 8 + sum(chunks_of(j) for j in range(k))

    CHUNKS = chunks_before(SLOTS) - chunks_before(0)

    def chunk(it, k, part):
        return it * CHUNKS + chunks_before(k) + part

    def head(it, k, times=1, more=0):
        return it * (SLOTS * times) + (k * times + more)

    def pair(it, k, more=0):
        return it * (SLOTS // 2) + (k // 2 + more)

    def projects(k):
        return k % 2 == 0 and k >= 4

    def batch(it, k, times=1, more=0):
        return it * (PER_LOOP * times) + (k // heads * times + more)

    def exists(it, k):
        return not isinstance(it, int) or it * SLOTS + k < HEADS_ALL

    def front_slot(k):
        return k + (4, 3, 2, 3)[k % 4]

    def front_exists(it, k):
        return chunks_of(k) > 0 and exists(it, front_slot(k))

    def next_rows(k):
        return k // GROUP * GROUP + 2 * GROUP

    def norms_ahead(it, k):
        return refreshes(k // GROUP * GROUP + GROUP) and exists(it, next_rows(k))

    with ExitStack() as ctx:
        def sb(name, shape, dt):
            return ctx.enter_context(nc.sbuf_tensor(f"{layer}_{name}", shape, dt))

        def psum(name, shape):
            return ctx.enter_context(nc.psum_tensor(f"{layer}_{name}", shape, F32))

        sem = layer_semaphores(nc, ctx, layer)

        wqkv = [sb(f"wqkv{i}", [P, CT, 3, inner], F32R) for i in (HI, LO)]
        wout = [sb(f"wout{i}", [P, heads // 2, DIM], F32R) for i in (HI, LO)]
        bias_row = sb("bias_row", [P, DIM], F32)
        affine = sb("affine", [P, 2, CT], F32)
        ident = sb("ident", [P, P], F32)
        minus_half = sb("minus_half", [P, RT], F32)

        x_sb = sb("x_sb", [P, PER_LOOP, RT, DIM], F32)
        res = sb("res", [P, PER_LOOP, RT, DIM], F32)
        adj_sb = sb("adj_sb", [P, PER_LOOP, RT, ROWS], U8)
        mask = sb("mask", [P, PER_LOOP, RT, ROWS], BF16)
        stats = sb("stats", [P, RT, 6], F32)
        mean_var = [sb(f"mean_var{i}", [P, RT, 2], F32) for i in range(1 + own_norm)]
        var_eps = sb("var_eps", [P, RT], F32)
        rstd = sb("rstd", [P, RT], F32)
        normed_x = sb("normed_x", [P, RT, DIM], F32)
        hT_full = sb("hT_full", [P, CT, ROWS], F32)
        hT = [sb(f"hT{i}", [P, CT, ROWS], F32R) for i in (HI, LO)]
        qT = sb("qT", [P, 2, 2, ROWS], F32R)
        kT_twice = sb("kT_twice", [P, 2, 2, ROWS], F32R)
        kT_hi = sb("kT_hi", [P, 2, ROWS], F32R)
        kT_lo = sb("kT_lo", [P, 2, ROWS], F32R)
        v_sb = sb("v_sb", [P, 2, RT, GROUP, 2 * HEAD], F32R)
        probs = sb("probs", [P, 4, RT, ROWS], F32)
        row_shift = sb("row_shift", [P, 4, RT], F32)
        row_sum = sb("row_sum", [P, 4, RT], F32)
        row_recip = sb("row_recip", [P, 4, RT], F32)
        pT = [sb(f"pT{i}", [P, RT, ROWS], F32R) for i in (HI, LO)]
        oT_parts = [sb(f"oT_part{i}", [P, ROWS], F32) for i in (HI, LO)]
        oT_sum = sb("oT_sum", [P, ROWS], F32)
        oT = [sb(f"oT{i}", [P, ROWS], F32R) for i in (HI, LO)]

        scores_ps = psum("scores_ps", [P, 2, ROWS])
        pT_ps = psum("pT_ps", [P, 2, ROWS])
        front_ps = psum("front_ps", [P, ROWS])
        oT_ps = psum("oT_ps", [P, ROWS])
        y_ps = psum("y_ps", [P, RT, DIM])

        consts_in = sem("consts_in")
        ident_made = sem("ident_made")
        passed = sem("passed")
        exponent_made = sem("exponent_made")
        staged_in = [sem(f"staged_in{n}") for n in range(2)]
        weights_hi = sem("weights_hi")
        weights_lo = sem("weights_lo")
        x_loaded = [sem(f"x_loaded{i}") for i in range(PER_LOOP)]
        adj_loaded = [sem(f"adj_loaded{i}") for i in range(PER_LOOP)]
        stored = [sem(f"stored{i}") for i in range(PER_LOOP)]
        mask_blank = sem("mask_blank")
        mask_ready = sem("mask_ready")
        stats_done = sem("stats_done")
        mean_var_done = sem("mean_var_done")
        var_eps_done = sem("var_eps_done")
        rstd_done = sem("rstd_done")
        centred = sem("centred")
        first_mean_done = sem("first_mean_done")
        eps_scaled = sem("eps_scaled")
        normed_done = sem("normed_done")
        res_ready = sem("res_ready")
        front_done = sem("front_done")
        front_hi = sem("front_hi")
        front_read = sem("front_read")
        hT_ready = sem("hT_ready")
        keys_ready = sem("keys_ready")
        keys_crossed = sem("keys_crossed")
        scores_done = sem("scores_done")
        masked = sem("masked")
        exp_done = sem("exp_done")
        recip_done = sem("recip_done")
        probs_ready = sem("probs_ready")
        pT_done = sem("pT_done")
        pT_hi = sem("pT_hi")
        pT_lo = sem("pT_lo")
        oT_done = sem("oT_done")
        oT_copied = sem("oT_copied")
        oT_summed = sem("oT_summed")
        oT_hi = sem("oT_hi")
        oT_lo = sem("oT_lo")
        projected = sem("projected")
        y_added = sem("y_added")

        def front_bank(c):
            turn = c % len(BANKS) if isinstance(c, int) and c < chunks_before(0) else 0
            return BANKS[turn]

        BANKS = [front_ps[:], *(y_ps[:, 2 * i:2 * i + 2].rearrange("p t c -> p (t c)") for i in range(2))]
        rows = "b (t p) c -> b p t c"
        x_src = x_in.rearrange(rows, p=P)
        x_dst = x_out.rearrange(rows, p=P)
        adj_src = adj.rearrange(rows, p=P)

        with nc.Block() as block:
            w_stage = probs[:].rearrange("p a t r -> p (a t r)")[:, 0:CT * 3 * inner]
            o_stage = res[:].rearrange("p a t c -> p (a t c)")[:, 0:heads // 2 * DIM]
            w_view = w_qkv.rearrange("(t p) a n -> p t (a n)", p=P)
            o_view = w_out.rearrange("(h p) c -> p h c", p=P)
            stage, make_hi, make_lo = split_weights(nc, [
                ([(w_stage.rearrange("p (t n) -> p t n", t=CT), w_view)], w_stage,
                 wqkv[HI][:].rearrange("p t a n -> p (t a n)"), wqkv[LO][:].rearrange("p t a n -> p (t a n)")),
                ([(o_stage.rearrange("p (h c) -> p h c", h=heads // 2), o_view)], o_stage,
                 wout[HI][:].rearrange("p h c -> p (h c)"), wout[LO][:].rearrange("p h c -> p (h c)")),
            ], (staged_in, weights_hi, weights_lo))
            identity_matrix(nc, block, ident[:], ident_made)

            @block.sync
            def _(sync):
                def load(it, b, source):
                    sync.dma_start(x_sb[:, b], x_src[source]).then_inc(x_loaded[b], 16)
                    sync.dma_start(adj_sb[:, b], adj_src[source]).then_inc(adj_loaded[b], 16)

                load(0, 0, 0)
                stage(sync)
                sync.dma_start(bias_row[:], b_out.rearrange("(a c) -> a c", a=1).to_broadcast([P, DIM])).then_inc(consts_in, 16)
                if own_norm:
                    with nc.allow_non_contiguous_dma(reason="one column of channels"):
                        for n, v in enumerate((gamma, beta)):
                            sync.dma_start(affine[:, n, :], v.rearrange("(t p) -> p t", p=P)).then_inc(consts_in, 16)

                def store(it, b, to, count):
                    sync.wait_ge(y_added, count)
                    sync.dma_start(x_dst[to], res[:, b]).then_inc(stored[b], 16)

                def reload(it, n):
                    for used, each in ((normed_done, 1), (res_ready, 1), (mask_ready, 2)):
                        own_wait(sync, used, it * (PER_LOOP * each) + (n - PER_LOOP + 1) * each, passed)
                    load(it, n % PER_LOOP, it * PER_LOOP + n)

                for b in range(PER_LOOP):
                    sync.sem_inc(stored[b], 16)
                for b in range(1, PER_LOOP):
                    load(0, b, b)
                reload(0, PER_LOOP)
                with sync.Fori(0, LOOPS - 2) as it:
                    for b in range(PER_LOOP):
                        reload(it, PER_LOOP + 1 + b)
                        store(it, b, it * PER_LOOP + b, it * (2 * PER_LOOP) + (2 * b + 2))
                reload(0, BATCHES - 1)
                for n in range(BATCHES - 2 * PER_LOOP, BATCHES):
                    store(0, n % PER_LOOP, n, 2 * (n + 1))
                for b in range(PER_LOOP):
                    sync.wait_ge(stored[b], 16 * LOOPS + 16)

            @block.gpsimd
            def _(pool):
                nc.gpsimd.memset(minus_half[:], -0.5).then_inc(exponent_made, 1)

                def make_mask(it, k, half):
                    b, part = k // heads % PER_LOOP, slice(2 * half, 2 * half + 2)
                    own_wait(pool, adj_loaded[b], it * 16 + (k // SLOTS * 16 + 16), passed)
                    if not isinstance(it, int) or it * PER_LOOP + k // heads >= PER_LOOP:
                        own_wait(pool, masked, batch(it, k, RT * heads, -RT * heads), passed)
                    convert = nc.gpsimd.tensor_scalar(mask[:, b, part], adj_sb[:, b, part], -1.0, BIG, ALU.add, ALU.mult)
                    if own_norm:
                        convert.then_inc(mask_blank, 1)
                        own_wait(pool, mask_blank, batch(it, k, 2, half + 1), passed)
                        nc.gpsimd.affine_select(
                            out=mask[:, b, part], in_=mask[:, b, part], compare_op=ALU.not_equal, fill=0.0,
                            base=2 * half * P, pattern=[[P, 2], [-1, ROWS]], channel_multiplier=1,
                        ).then_inc(mask_ready, 1)
                    else:
                        convert.then_inc(mask_ready, 1)

                def rstd_step(it, k):
                    own_wait(pool, mean_var_done, batch(it, k, 1, 1), passed)
                    if own_norm:
                        nc.gpsimd.tensor_scalar(var_eps[:], mean_var[0][:, :, 1], EPS, EPS, ALU.add, ALU.mult).then_inc(eps_scaled, 1)
                        pool.wait_ge(eps_scaled, batch(it, k, 1, 1))
                        nc.gpsimd.tensor_tensor(var_eps[:], mean_var[1][:, :, 1], var_eps[:], ALU.add).then_inc(var_eps_done, 1)
                    else:
                        nc.gpsimd.tensor_scalar(var_eps[:], mean_var[0][:, :, 1], EPS, 1.0, ALU.add, ALU.mult).then_inc(var_eps_done, 1)
                    pool.wait_ge(var_eps_done, batch(it, k, 1, 1))
                    nc.gpsimd.tensor_tensor(rstd[:], var_eps[:], minus_half[:], ALU.pow).then_inc(rstd_done, 1)

                def residual(it, k):
                    b = k // heads % PER_LOOP
                    pool.wait_ge(stored[b], it * 16 + (k // SLOTS * 16 + 16))
                    nc.gpsimd.tensor_tensor(
                        res[:, b], x_sb[:, b], bias_row[:].unsqueeze(1).to_broadcast([P, RT, DIM]), ALU.add,
                    ).then_inc(res_ready, 1)

                def hT_rest(it, k, first):
                    for part in range(CT):
                        pool.wait_ge(front_read, first + (part + 1))
                        nc.gpsimd.tensor_tensor(
                            hT[LO][:, part], hT_full[:, part], exact(hT[HI][:, part]), ALU.subtract,
                        ).then_inc(hT_ready, 1)

                def repeat_keys(it, k, first):
                    own_wait(pool, front_hi, first + 1, passed)
                    nc.gpsimd.tensor_scalar(
                        kT_twice[0:HEAD, k // 2 % 2, 0], exact(kT_hi[0:HEAD, k // 2 % 2]), 1.0, 1.0, ALU.mult, ALU.mult,
                    ).then_inc(keys_ready, 1)

                def normalise(it, k):
                    own_wait(pool, recip_done, head(it, k, 1, 1), passed)
                    for q in range(RT):
                        part = probs[:, k % 4, q]
                        nc.gpsimd.tensor_scalar(
                            part, part, row_recip[:, k % 4, q:q + 1], 1.0, ALU.mult, ALU.mult,
                        ).then_inc(probs_ready, 1)

                def slot(it, k):
                    s, ahead = k % 4, refreshes(k) and exists(it, k + GROUP)
                    if k % 2 and k >= 3 and exists(it, k - 2):
                        pool.wait_ge(oT_hi, pair(it, k - 1))
                        nc.gpsimd.tensor_tensor(oT[LO][:], oT_sum[:], exact(oT[HI][:]), ALU.subtract).then_inc(oT_lo, 1)
                    if exists(it, k + 1):
                        normalise(it, k + 1)
                    if s % 2 and front_exists(it, k):
                        repeat_keys(it, front_slot(k), chunk(it, k, 0))
                    if own_norm and ahead and s == 0:
                        hT_rest(it, k + GROUP, chunk(it, k, 0))
                    if s == 2 and norms_ahead(it, k):
                        rstd_step(it, next_rows(k))
                    if k % 2 == 0 and k >= 2 and exists(it, k - 1):
                        pool.wait_ge(oT_copied, head(it, k))
                        nc.gpsimd.tensor_tensor(oT_sum[:], oT_parts[HI][:], oT_parts[LO][:], ALU.add).then_inc(oT_summed, 1)
                    if norms_ahead(it, k):
                        if s >= 2:
                            make_mask(it, next_rows(k), s - 2)
                    if ahead and s == 3:
                        residual(it, k + GROUP)

                pool.wait_ge(exponent_made, 1)
                rstd_step(0, 0)
                for half in range(2):
                    make_mask(0, 0, half)
                if own_norm:
                    hT_rest(0, 0, 0)
                for n, (s, k) in enumerate(BEFORE):
                    if s % 2:
                        repeat_keys(0, k, 2 * n)
                pool.wait_ge(weights_lo, 2)
                pool.wait_ge(consts_in, 48 if own_norm else 16)
                residual(0, 0)
                normalise(0, 0)
                if refreshes(0):
                    rstd_step(0, GROUP)
                    for half in range(2):
                        make_mask(0, GROUP, half)
                for k in range(FIRST):
                    slot(0, k)
                with pool.Fori(0, ROUNDS) as it:
                    for k in range(FIRST, SLOTS + FIRST):
                        slot(it, k)
                for k in range(FIRST, (LOOPS - ROUNDS) * SLOTS + 4):
                    slot(ROUNDS, k)

            @block.scalar
            def _(act):
                def act_front(k, s, part, first):
                    bank = front_bank(first + part)
                    act.wait_ge(front_done, first + (part + 1))
                    if s == 0:
                        if own_norm:
                            step = nc.scalar.activation(hT[HI][:, part], bank, ACT.Identity,
                                                        bias=affine[:, 1, part:part + 1], scale=affine[:, 0, part:part + 1])
                        else:
                            step = nc.scalar.activation(hT[HI][:, part], bank, ACT.Relu)
                        step.then_inc(front_hi, 1)
                        return
                    if s % 2 and part == QUERIES:
                        for of in range(2):
                            own = slice(of * HEAD, (of + 1) * HEAD)
                            step = nc.scalar.activation(qT[own, k // 2 % 2, of], bank[own], ACT.Copy)
                        step.then_inc(front_hi, 1)
                        return
                    if s % 2:
                        to, source = kT_hi[:, k // 2 % 2], bank
                    else:
                        to = v_sb[:, k // GROUP % 2, 2 * part:2 * part + 2, :, 0:HEAD]
                        source = bank.rearrange("p (t h d) -> p t h d", t=2, h=GROUP)
                    nc.scalar.activation(to, source, ACT.Copy).then_inc(front_hi, 1)

                def cross_keys(it, k, first):
                    act.wait_ge(front_hi, first + 1)
                    for of in range(2):
                        own, other = (slice(h * HEAD, (h + 1) * HEAD) for h in (of, 1 - of))
                        step = nc.scalar.activation(kT_twice[other, k // 2 % 2, of], exact(kT_hi[own, k // 2 % 2]), ACT.Copy)
                    step.then_inc(keys_crossed, 1)

                def copy_output(it, k):
                    before = pair(it, k)
                    if k % 2 == 0 and (not isinstance(before, int) or before > 0):
                        act.wait_ge(oT_summed, before)
                    act.wait_ge(oT_done, head(it, k, 1, 1))
                    at = slice(k % 2 * HEAD, (k % 2 + 1) * HEAD)
                    nc.scalar.activation(oT_parts[HI][at], oT_ps[0:HEAD], ACT.Copy)
                    nc.scalar.activation(oT_parts[LO][at], oT_ps[HEAD:P], ACT.Copy).then_inc(oT_copied, 1)

                def output_hi(it, k):
                    before = pair(it, k)
                    if not isinstance(before, int) or before > 0:
                        act.wait_ge(projected, before)
                    act.wait_ge(oT_summed, pair(it, k, 1))
                    nc.scalar.activation(oT[HI][:], oT_sum[:], ACT.Copy).then_inc(oT_hi, 1)

                def exps(it, k, q):
                    part = probs[:, k % 4, q]
                    act.wait_ge(masked, head(it, k, RT, q + 1))
                    nc.scalar.activation(
                        part, part, ACT.Exp, bias=row_shift[:, k % 4, q:q + 1], scale=-1.0,
                        accum_out=row_sum[:, k % 4, q:q + 1],
                    ).then_inc(exp_done, 1)

                def slot(it, k):
                    for q in range(RT):
                        if exists(it, k):
                            act.wait_ge(pT_done, head(it, k, RT, q + 1))
                            nc.scalar.activation(pT[HI][:, q], pT_ps[:, q % 2], ACT.Copy).then_inc(pT_hi, 1)
                        if k >= 1 and exists(it, k - 1) and q == RT - 2:
                            copy_output(it, k - 1)
                        if q in CHUNK_AT and front_exists(it, k):
                            act_front(front_slot(k), k % 4, CHUNK_AT[q], chunk(it, k, 0))
                        if q == 0 and k % 2 and k >= 3 and exists(it, k - 2):
                            output_hi(it, k - 3)
                        if q > 0:
                            if exists(it, k + LEAD):
                                exps(it, k + LEAD, q - 1)
                        elif exists(it, k + LEAD - 1):
                            exps(it, k + LEAD - 1, RT - 1)
                        if k % 2 and q == 2 and front_exists(it, k):
                            cross_keys(it, front_slot(k), chunk(it, k, 0))

                make_hi(act)
                if own_norm:
                    act.wait_ge(consts_in, 48)
                for n, (s, k) in enumerate(BEFORE):
                    for part in range(2):
                        act_front(k, s, part, 2 * n)
                        if n >= BESIDE:
                            exps(0, 0, 2 * (n - BESIDE) + part)
                    if s % 2:
                        cross_keys(0, k, 2 * n)
                for q in range(RT - 1):
                    exps(0, LEAD - 1, q)
                for k in range(FIRST):
                    slot(0, k)
                with act.Fori(0, ROUNDS) as it:
                    for k in range(FIRST, SLOTS + FIRST):
                        slot(it, k)
                for k in range(FIRST, (LOOPS - ROUNDS) * SLOTS + 4):
                    slot(ROUNDS, k)

            @block.vector
            def _(dve):
                def front(it, k, s, part, first):
                    bank = front_bank(first + part)
                    dve.wait_ge(front_hi, first + (part + 1))
                    if s == 0 and own_norm:
                        before = batch(it, k, CT)
                        if not isinstance(before, int) or before > 0:
                            dve.wait_ge(hT_ready, before)
                        nc.vector.tensor_scalar(
                            hT_full[:, part], bank, affine[:, 0, part:part + 1], affine[:, 1, part:part + 1],
                            ALU.mult, ALU.add,
                        ).then_inc(front_read, 1)
                        return
                    if s == 0:
                        nc.vector.scalar_tensor_tensor(
                            hT[LO][:, part], bank, 0.0, exact(hT[HI][:, part]), ALU.max, ALU.subtract,
                        ).then_inc(front_read, 1)
                        return
                    if s % 2 and part == QUERIES:
                        for of in range(2):
                            own, other = (slice(h * HEAD, (h + 1) * HEAD) for h in (of, 1 - of))
                            step = nc.vector.tensor_tensor(qT[other, k // 2 % 2, of], bank[own],
                                                           exact(qT[own, k // 2 % 2, of]), ALU.subtract)
                        step.then_inc(front_read, 1)
                        return
                    if s % 2:
                        to, hi, source = kT_lo[:, k // 2 % 2], kT_hi[:, k // 2 % 2], bank
                    else:
                        both = v_sb[:, k // GROUP % 2, 2 * part:2 * part + 2]
                        to, hi = both[:, :, :, HEAD:], both[:, :, :, 0:HEAD]
                        source = bank.rearrange("p (t h d) -> p t h d", t=2, h=GROUP)
                    nc.vector.tensor_tensor(to, source, exact(hi), ALU.subtract).then_inc(front_read, 1)
                    if s % 2:
                        nc.vector.tensor_copy(kT_twice[HEAD:P, k // 2 % 2, 1], exact(kT_hi[HEAD:P, k // 2 % 2]))

                def mean_and_variance(it, k, n, rows_, signal):
                    for q in range(RT):
                        step = nc.vector.bn_stats(stats[:, q], rows_[:, q])
                    step.then_inc(stats_done, 1)
                    own_wait(dve, stats_done, batch(it, k, 1 + own_norm, n + 1), passed)
                    for q in range(RT):
                        step = nc.vector.bn_aggr(mean_var[n][:, q], stats[:, q])
                    if signal:
                        step.then_inc(signal, 1)

                def norm_first(it, k):
                    b = k // heads % PER_LOOP
                    dve.wait_ge(x_loaded[b], it * 16 + (k // SLOTS * 16 + 16))
                    mean_and_variance(it, k, 0, x_sb[:, b], first_mean_done if own_norm else mean_var_done)

                def norm_middle(it, k):
                    b = k // heads % PER_LOOP
                    dve.wait_ge(first_mean_done, batch(it, k, 1, 1))
                    for q in range(RT):
                        step = nc.vector.tensor_scalar(normed_x[:, q], x_sb[:, b, q], mean_var[0][:, q, 0:1], 0.0,
                                                       ALU.subtract, ALU.max)
                    step.then_inc(centred, 1)

                def norm_again(it, k):
                    dve.wait_ge(centred, batch(it, k, 1, 1))
                    mean_and_variance(it, k, 1, normed_x, mean_var_done)

                def norm_last(it, k):
                    dve.wait_ge(rstd_done, batch(it, k, 1, 1))
                    rows_ = normed_x if own_norm else x_sb[:, k // heads % PER_LOOP]
                    for q in range(RT):
                        step = nc.vector.tensor_scalar(normed_x[:, q], rows_[:, q], mean_var[-1][:, q, 0:1],
                                                       rstd[:, q:q + 1], ALU.subtract, ALU.mult)
                    step.then_inc(normed_done, 1)

                if own_norm:
                    NORM_STEPS = {(1, 0): norm_first, (2, 0): norm_middle, (2, 1): norm_again, (3, 1): norm_last}
                else:
                    NORM_STEPS = {(2, 0): norm_first, (3, 1): norm_last}

                def mask_scores(it, k, q):
                    b = k // heads % PER_LOOP
                    if k % heads == 0 and q == 0:
                        dve.wait_ge(mask_ready, batch(it, k, 2, 2))
                    own_wait(dve, scores_done, head(it, k, RT, q + 1), passed)
                    nc.vector.tensor_tensor_reduce(
                        probs[:, k % 4, q], scores_ps[:, q % 2], mask[:, b, q], -SCALE, LEAST,
                        ALU.add, ALU.min, row_shift[:, k % 4, q:q + 1],
                    ).then_inc(masked, 1)

                def recip(it, k):
                    dve.wait_ge(exp_done, head(it, k, RT, RT))
                    nc.vector.reciprocal(row_recip[:, k % 4], row_sum[:, k % 4]).then_inc(recip_done, 1)

                def add_attention(it, k):
                    b = k // heads % PER_LOOP
                    dve.wait_ge(projected, pair(it, k, 1))
                    dve.wait_ge(res_ready, batch(it, k, 1, 1))
                    for half in range(2):
                        part = slice(2 * half, 2 * half + 2)
                        nc.vector.tensor_tensor(res[:, b, part], y_ps[:, part], res[:, b, part], ALU.add).then_inc(y_added, 1)

                def slot(it, k):
                    for q in range(RT):
                        if q == 0 and projects(k - 1) and (k - 4) % heads == heads - 1:
                            add_attention(it, k - 5)
                        if q == 1 and exists(it, k + 1):
                            recip(it, k + 1)
                        if exists(it, k):
                            dve.wait_ge(pT_hi, head(it, k, RT, q + 1))
                            nc.vector.tensor_tensor(pT[LO][:, q], pT_ps[:, q % 2], exact(pT[HI][:, q]), ALU.subtract).then_inc(pT_lo, 1)
                        if exists(it, k + LEAD):
                            mask_scores(it, k + LEAD, q)
                        if q in CHUNK_AT and front_exists(it, k):
                            front(it, front_slot(k), k % 4, CHUNK_AT[q], chunk(it, k, 0))
                        if (k % 4, q) in NORM_STEPS and norms_ahead(it, k):
                            NORM_STEPS[k % 4, q](it, next_rows(k))

                def norm(k):
                    for step in NORM_STEPS.values():
                        step(0, k)

                norm(0)
                make_lo(dve)
                if own_norm:
                    dve.wait_ge(consts_in, 48)
                for n, (s, k) in enumerate(BEFORE):
                    for part in range(2):
                        if n >= BESIDE:
                            mask_scores(0, 0, 2 * (n - BESIDE) + part)
                        front(0, k, s, part, 2 * n)
                for q in range(RT):
                    mask_scores(0, LEAD - 1, q)
                    if q == 0:
                        recip(0, 0)
                if refreshes(0):
                    norm(GROUP)
                for k in range(FIRST):
                    slot(0, k)
                with dve.Fori(0, ROUNDS) as it:
                    for k in range(FIRST, SLOTS + FIRST):
                        slot(it, k)
                for k in range(FIRST, (LOOPS - ROUNDS) * SLOTS + 4):
                    slot(ROUNDS, k)

            @block.tensor
            def _(pe):
                def front_hT(it, k, part, bank):
                    if part == 0:
                        pe.wait_ge(normed_done, batch(it, k, 1, 1))
                    for q in range(RT):
                        mm = nc.tensor.transpose(bank[:, q * P:(q + 1) * P], normed_x[:, q, part * P:(part + 1) * P], ident[:])
                    return mm

                def front_qk(it, k, part, bank):
                    if own_norm and part == 0:
                        pe.wait_ge(hT_ready, batch(it, k, CT, CT))
                    elif part == 0 and isinstance(it, int) and k == 0:
                        pe.wait_ge(front_read, CT)
                    at = k // 2 * P % inner
                    for n, (i, j) in enumerate(PASSES):
                        for t in range(CT):
                            mm = nc.tensor.matmul(bank, wqkv[i][:, t, 1 if part == KEYS else 0, at:at + P], hT[j][:, t],
                                                  start=(n + t == 0), stop=(n == 2 and t == CT - 1))
                    return mm

                def front_v(it, k, part, bank):
                    at = k // GROUP * GROUP * HEAD % inner
                    for m in range(2):
                        q = 2 * part + m
                        for n, (i, j) in enumerate(PASSES):
                            for t in range(CT):
                                mm = nc.tensor.matmul(
                                    bank[:, m * DIM:(m + 1) * DIM], hT[i][:, t, q * P:(q + 1) * P],
                                    wqkv[j][:, t, 2, at:at + GROUP * HEAD],
                                    start=(n + t == 0), stop=(n == 2 and t == CT - 1))
                    return mm

                def front(it, k, s, part, c):
                    if not isinstance(c, int) or c >= chunks_before(0):
                        pe.wait_ge(front_read, c)
                    elif c >= len(BANKS):
                        pe.wait_ge(front_read, c - len(BANKS) + 1)
                    bank = front_bank(c)
                    mm = (front_hT, front_qk, front_v, front_qk)[s](it, k, part, bank)
                    mm.then_inc(front_done, 1)

                def scores(it, k, q, c):
                    if k % 2 == 0 and q == 0:
                        pe.wait_ge(front_read, c)
                        pe.wait_ge(keys_ready, pair(it, k, 1))
                        pe.wait_ge(keys_crossed, pair(it, k, 1))
                    own = slice(k % 2 * HEAD, (k % 2 + 1) * HEAD)
                    rows_, at = slice(q * P, (q + 1) * P), (k // 2 % 2, k % 2)
                    tile = head(it, k, RT, q - 1)
                    if not isinstance(tile, int) or tile > 0:
                        pe.wait_ge(masked, tile)
                    nc.tensor.matmul(scores_ps[:, q % 2], qT[:, *at, rows_], kT_twice[:, *at], start=True, stop=False)
                    nc.tensor.matmul(scores_ps[:, q % 2], qT[own, *at, rows_], kT_lo[own, k // 2 % 2],
                                     start=False, stop=True).then_inc(scores_done, 1)

                def transpose(it, k, t):
                    if t == 0:
                        pe.wait_ge(probs_ready, head(it, k, RT, RT))
                    tile = head(it, k, RT, t - 1)
                    if not isinstance(tile, int) or tile > 0:
                        pe.wait_ge(pT_lo, tile)
                    for q in range(RT):
                        mm = nc.tensor.transpose(pT_ps[:, t % 2, q * P:(q + 1) * P],
                                                 probs[:, k % 4, q, t * P:(t + 1) * P], ident[:])
                    mm.then_inc(pT_done, 1)

                def times_values(it, k, t, c):
                    if t == 0:
                        if k % GROUP == 0:
                            pe.wait_ge(front_read, c)
                        before = head(it, k)
                        if not isinstance(before, int) or before > 0:
                            pe.wait_ge(oT_copied, before)
                    pe.wait_ge(pT_lo, head(it, k, RT, t + 1))
                    for i in (HI, LO):
                        mm = nc.tensor.matmul(oT_ps[:], v_sb[:, k // GROUP % 2, t, k % GROUP], pT[i][:, t],
                                              start=(t == 0 and i == HI), stop=(t == RT - 1 and i == LO))
                    if t == RT - 1:
                        mm.then_inc(oT_done, 1)

                def project(it, k, q):
                    h = k % heads
                    if q == 0:
                        pe.wait_ge(oT_lo, pair(it, k, 1))
                        before = batch(it, k, 2, 0)
                        if h == 0 and (not isinstance(before, int) or before > 0):
                            pe.wait_ge(y_added, before)
                    for n, (i, j) in enumerate(PASSES):
                        mm = nc.tensor.matmul(
                            y_ps[:, q], oT[i][:, q * P:(q + 1) * P], wout[j][:, h // 2],
                            start=(h == 0 and q % 2 == 0 and n == 0), stop=(h == heads - 2 and n == 2),
                            skip_group_check=True)
                    if q == RT - 1:
                        mm.then_inc(projected, 1)

                def slot(it, k):
                    for q in range(RT):
                        weighs = k >= 1 and exists(it, k - 1)
                        if weighs and q < RT - 1:
                            times_values(it, k - 1, q, 8 if k == 1 else chunk(it, k - 3, 2))
                        if exists(it, k):
                            transpose(it, k, q)
                        if projects(k):
                            project(it, k - 4, q)
                        if weighs and q == RT - 2:
                            times_values(it, k - 1, RT - 1, 0)
                        if q in CHUNK_AT and front_exists(it, k):
                            front(it, front_slot(k), k % 4, CHUNK_AT[q], chunk(it, k, CHUNK_AT[q]))
                        if exists(it, k + LEAD):
                            scores(it, k + LEAD, q, 6 if k == 0 else chunk(it, k - 1, 2))

                pe.wait_ge(ident_made, 2)
                for n, (s, k) in enumerate(BEFORE):
                    if n == 1:
                        pe.wait_ge(weights_lo, 2)
                    for part in range(2):
                        if n >= BESIDE:
                            scores(0, 0, 2 * (n - BESIDE) + part, 2 * BESIDE)
                        front(0, k, s, part, 2 * n + part)
                for q in range(RT):
                    scores(0, LEAD - 1, q, 0)
                for k in range(FIRST):
                    slot(0, k)
                with pe.Fori(0, ROUNDS) as it:
                    for k in range(FIRST, SLOTS + FIRST):
                        slot(it, k)
                for k in range(FIRST, (LOOPS - ROUNDS) * SLOTS + 4):
                    slot(ROUNDS, k)


def gated_layer(nc, layer, x_in, x_out, adj_t, w_rows, w_cols, attn_t, b_heads, mix, small, gate_bias):
    HEADS = w_rows.shape[1]
    GR = DIM + 1
    SLOTS = PER_LOOP * HEADS
    HEADS_ALL = BATCHES * HEADS
    FIRST = HEADS
    FC, G1, G2 = range(3)

    with ExitStack() as ctx:
        sem = layer_semaphores(nc, ctx, layer)

        def sb(name, shape, dt, to=ctx):
            return to.enter_context(nc.sbuf_tensor(f"{layer}_{name}", shape, dt))

        w_sb = [sb(f"w{i}", [P, CT, HEADS * DIM], F32R) for i in (HI, LO)]
        gw_sb = [sb(f"gw{i}", [P, CT, HEADS, DIM], F32R) for i in (HI, LO)]
        mix_sb = [sb(f"mix{i}", [P, HEADS * CT, DIM], F32R) for i in (HI, LO)]
        small_sb = [sb(f"small{i}", [P, 3, CT, DIM], F32R) for i in (HI, LO)]
        wh_bias = sb("wh_bias", [P, HEADS * DIM], F32)
        s_weights = sb("s_weights", [P, CT, HEADS], F32)
        g_bias = sb("g_bias", [P, CT, HEADS], F32)
        s_bias = sb("s_bias", [P, HEADS], F32)
        half_gate_bias = sb("half_gate_bias", [P, CT], F32)
        ident = sb("ident", [P, P], F32)
        minus_half = sb("minus_half", [P, RT], F32)

        with ExitStack() as pre:
            w_stage = sb("w_stage", [P, CT * HEADS * DIM], F32, pre)
            mix_stage = sb("mix_stage", [P, HEADS * CT * DIM], F32, pre)
            small_stage = sb("small_stage", [P, 3 * CT * DIM], F32, pre)
            wb = sb("wb", [P, CT, HEADS, GR], F32, pre)
            attn_sb = sb("attn_sb", [P, CT, HEADS, DIM], F32, pre)
            aw = sb("aw", [P, CT, HEADS, GR], F32, pre)
            b_attn_b = sb("b_attn_b", [P, CT, HEADS], F32, pre)
            gate_bias_sb = sb("gate_bias_sb", [P, CT], F32, pre)
            ones = sb("ones", [P, P], F32, pre)
            banks = pre.enter_context(nc.psum_tensor(f"{layer}_banks", [P, 2 * HEADS, ROWS], F32))

            staged_in = [sem(f"staged_in{n}") for n in range(3)]
            rows_in = sem("rows_in")
            biases_in = sem("biases_in")
            weights_hi = sem("weights_hi")
            weights_lo = sem("weights_lo")
            ident_made = sem("ident_made")
            ones_made = sem("ones_made")
            aw_done = sem("aw_done")
            aw_kept = sem("aw_kept")
            gw_done = sem("gw_done")
            gw_hi = sem("gw_hi")
            gw_lo = sem("gw_lo")
            b_attn_b_made = sem("b_attn_b_made")
            vectors_done = sem("vectors_done")
            vectors_kept = sem("vectors_kept")

            with nc.Block() as block:
                @block.sync
                def _(sync):
                    with nc.allow_non_contiguous_dma(reason="columns of biases"):
                        for t in range(CT):
                            sync.dma_start(wb[:, t, :, 0:DIM], w_rows[t * P:(t + 1) * P]).then_inc(rows_in, 16)
                            sync.dma_start(wb[:, t, :, DIM], b_heads[:, t * P:(t + 1) * P].rearrange("h p -> p h")).then_inc(rows_in, 16)
                        sync.dma_start(attn_sb[:], attn_t.rearrange("(t p) h o -> p t h o", p=P)).then_inc(rows_in, 16)
                        sync.dma_start(gate_bias_sb[:], gate_bias.rearrange("(t p) -> p t", p=P)).then_inc(biases_in, 16)
                    sync.dma_start(wh_bias[:], b_heads.rearrange("h o -> (h o)").rearrange("(a n) -> a n", a=1).to_broadcast([P, HEADS * DIM])).then_inc(biases_in, 16)

                stage, make_hi, make_lo = split_weights(nc, [
                    ([(w_stage[:].rearrange("p (t n) -> p t n", t=CT), w_cols.rearrange("(t p) n -> p t n", p=P))],
                     w_stage[:], *(w[:].rearrange("p t n -> p (t n)") for w in w_sb)),
                    ([(mix_stage[:].rearrange("p (t n) -> p t n", t=HEADS * CT), mix.rearrange("(t p) n -> p t n", p=P))],
                     mix_stage[:], *(w[:].rearrange("p t n -> p (t n)") for w in mix_sb)),
                    ([(small_stage[:].rearrange("p (a t n) -> p a t n", a=3, t=CT)[:, a], w.rearrange("(t p) n -> p t n", p=P))
                      for a, w in enumerate(small)],
                     small_stage[:], *(w[:].rearrange("p a t n -> p (a t n)") for w in small_sb)),
                ], (staged_in, weights_hi, weights_lo))
                block.sync(stage)
                block.scalar(make_hi)
                block.vector(make_lo)
                identity_matrix(nc, block, ident[:], ident_made)

                @block.gpsimd
                def _(pool):
                    nc.gpsimd.memset(ones[:], 1.0).then_inc(ones_made, 1)
                    nc.gpsimd.memset(minus_half[:], -0.5).then_inc(ones_made, 1)

                @block.tensor
                def _(pe):
                    pe.wait_ge(rows_in, 80)
                    for h in range(HEADS):
                        for o in range(CT):
                            for t in range(CT):
                                mm = nc.tensor.matmul(banks[:, h * CT + o, 0:GR], attn_sb[:, t, h, o * P:(o + 1) * P],
                                                      wb[:, t, h], start=(t == 0), stop=(t == CT - 1))
                            mm.then_inc(aw_done, 1)
                    for h in range(HEADS):
                        pe.wait_ge(aw_kept, CT * (h + 1))
                        for i in range(CT):
                            for t in range(CT):
                                mm = nc.tensor.matmul(banks[:, h * CT + i, 0:GR], aw[:, t, h, i * P:(i + 1) * P],
                                                      wb[:, t, h], start=(t == 0), stop=(t == CT - 1))
                            mm.then_inc(gw_done, 1)
                    pe.wait_ge(gw_lo, CT)
                    for i in range(CT):
                        for h in range(HEADS):
                            for t in range(CT):
                                nc.tensor.matmul(banks[:, 0, i * HEADS + h:i * HEADS + h + 1], wb[:, t, h, i * P:(i + 1) * P],
                                                 aw[:, t, h, DIM:GR], start=(t == 0), stop=(t == CT - 1))
                    pe.wait_ge(b_attn_b_made, 1)
                    pe.wait_ge(ones_made, 1)
                    for t in range(CT):
                        mm = nc.tensor.matmul(banks[:, 1, 0:HEADS], ones[:], b_attn_b[:, t], start=(t == 0), stop=(t == CT - 1))
                    mm.then_inc(vectors_done, 1)

                @block.scalar
                def _(act):
                    for h in range(HEADS):
                        for i in range(CT):
                            act.wait_ge(gw_done, h * CT + i + 1)
                            nc.scalar.activation(gw_sb[HI][:, i, h], banks[:, h * CT + i, 0:DIM], ACT.Copy).then_inc(gw_hi, 1)
                    act.wait_ge(biases_in, 32)
                    nc.scalar.activation(half_gate_bias[:], gate_bias_sb[:], ACT.Copy, scale=0.5)

                @block.vector
                def _(dve):
                    for h in range(HEADS):
                        for o in range(CT):
                            dve.wait_ge(aw_done, h * CT + o + 1)
                            nc.vector.tensor_copy(aw[:, o, h], banks[:, h * CT + o, 0:GR]).then_inc(aw_kept, 1)
                    dve.wait_ge(rows_in, 80)
                    dve.wait_ge(aw_kept, HEADS * CT)
                    nc.vector.tensor_tensor(b_attn_b[:], wb[:, :, :, DIM], aw[:, :, :, DIM], ALU.mult).then_inc(b_attn_b_made, 1)
                    for h in range(HEADS):
                        for i in range(CT):
                            bank = banks[:, h * CT + i]
                            dve.wait_ge(gw_hi, h * CT + i + 1)
                            nc.vector.tensor_copy(s_weights[:, i, h:h + 1], bank[:, DIM:GR])
                            nc.vector.tensor_tensor(gw_sb[LO][:, i, h], bank[:, 0:DIM], exact(gw_sb[HI][:, i, h]), ALU.subtract).then_inc(gw_lo, 1)
                    dve.wait_ge(vectors_done, 1)
                    nc.vector.tensor_copy(g_bias[:].rearrange("p i h -> p (i h)"), banks[:, 0, 0:CT * HEADS])
                    nc.vector.tensor_copy(s_bias[:], banks[:, 1, 0:HEADS]).then_inc(vectors_kept, 1)
                    dve.wait_ge(vectors_kept, 1)

        x_sb = sb("x_sb", [P, PER_LOOP, RT, DIM], F32)
        res = sb("res", [P, PER_LOOP, RT, DIM], F32)
        adj_sb = sb("adj_sb", [P, PER_LOOP, RT, ROWS], U8)
        stats = sb("stats", [P, RT, 6], F32)
        mean_var = sb("mean_var", [P, RT, 2], F32)
        var_eps = sb("var_eps", [P, RT], F32)
        rstd = sb("rstd", [P, RT], F32)
        normed_x = sb("normed_x", [P, RT, DIM], F32)
        hT_full = sb("hT_full", [P, CT, ROWS], F32)
        hT = [sb(f"hT{i}", [P, PER_LOOP, CT, ROWS], F32R) for i in (HI, LO)]
        s_sb = sb("s_sb", [P, PER_LOOP, RT, HEADS], F32)
        gT = [sb(f"gT{i}", [P, 2, CT, ROWS], F32R) for i in (HI, LO)]
        wh_full = sb("wh_full", [P, RT, DIM], F32)
        wh = [sb(f"wh{i}", [P, 2, RT, DIM], F32R) for i in (HI, LO)]
        a_full = sb("a_full", [P, RT, ROWS], F32)
        a_sb = [sb(f"a{i}", [P, RT, ROWS], F32R) for i in (HI, LO)]
        hpT = [sb(f"hpT{i}", [P, CT, ROWS], F32R) for i in (HI, LO)]
        ha_full = sb("ha_full", [P, CT, ROWS], F32)
        ha = [sb(f"ha{i}", [P, CT, ROWS], F32R) for i in (HI, LO)]
        hf_full = sb("hf_full", [P, CT, ROWS], F32)
        hf = [sb(f"hf{i}", [P, CT, ROWS], F32R) for i in (HI, LO)]
        gate = sb("gate", [P, CT, ROWS], F32)

        def psum(name, shape):
            return ctx.enter_context(nc.psum_tensor(f"{layer}_{name}", shape, F32))

        scores_ps = psum("scores_ps", [P, 2, ROWS])
        front_ps = psum("front_ps", [P, 2, ROWS])
        hp_ps = psum("hp_ps", [P, CT, ROWS])
        ha_ps = psum("ha_ps", [P, CT, ROWS])

        x_loaded = [sem(f"x_loaded{i}") for i in range(PER_LOOP)]
        adj_loaded = [sem(f"adj_loaded{i}") for i in range(PER_LOOP)]
        res_loaded = [sem(f"res_loaded{i}") for i in range(PER_LOOP)]
        stored = [sem(f"stored{i}") for i in range(PER_LOOP)]
        passed = sem("passed")
        stats_done = sem("stats_done")
        mean_var_done = sem("mean_var_done")
        var_eps_done = sem("var_eps_done")
        rstd_done = sem("rstd_done")
        normed_done = sem("normed_done")
        front_done = sem("front_done")
        front_read = sem("front_read")
        front_full = sem("front_full")
        front_act = sem("front_act")
        wh_ready = sem("wh_ready")
        difference_done = sem("difference_done")
        opened = sem("opened")
        mixed = sem("mixed")
        added = sem("added")
        scores_done = sem("scores_done")
        masked = sem("masked")
        tanh_hi = sem("tanh_hi")
        tanh_full = sem("tanh_full")
        tanh_lo = sem("tanh_lo")
        hp_done = sem("hp_done")
        hp_hi = sem("hp_hi")
        hp_lo = sem("hp_lo")
        ha_done = sem("ha_done")
        ha_hi = sem("ha_hi")
        ha_lo = sem("ha_lo")

        def side_work(n):
            b, s = n // HEADS, n % HEADS
            if n == -1:
                at = [[("h", 0, 0), ("h", 1, 0), ("s", 0, 0), ("g", 0, 0), ("g", 1, 0), ("g", 0, 1), ("g", 1, 1),
                       ("w", 0, 0), ("w", 1, 0)], [], [], []]
            else:
                at = [[("g", 0, n + 2), ("g", 1, n + 2)], [("w", 0, n + 1)], [("w", 1, n + 1)], []]
                if s == 0:
                    at[1] += [("gate", 0, b - 1)]
                    at[2] += [("gate", 1, b - 1)]
                elif s == 1:
                    at[1] += [("h", 0, b + 1)]
                    at[2] += [("h", 1, b + 1)]
                    at[3] += [("s", 0, b + 1), ("back", 0, b - 1)]
                elif s == 2:
                    at[1] += [("back", 1, b - 1)]
                    at[2] += [("hf", 0, b)]
                elif s == 3:
                    at[2] += [("hf", 1, b)]

            def there(chunk):
                kind, _, to = chunk
                return 0 <= to < (HEADS_ALL if kind in "gw" else BATCHES)

            return [[c for c in point if there(c)] for point in at]

        LAST = HEADS_ALL + HEADS
        chunks = [(n, c) for n in range(-1, LAST) for point in side_work(n) for c in point]

        def before(kinds, n, c):
            at = chunks.index((n, c))
            return sum(x[0] in kinds for _, x in chunks[:at])

        def through(kinds, n, kind, part):
            at = next(i for i, (_, c) in enumerate(chunks) if c == (kind, part, n))
            return sum(x[0] in kinds for _, x in chunks[:at + 1])

        ALL = ("h", "s", "g", "w", "gate", "back", "hf")
        BY_ACT = ("h", "g", "w", "gate", "hf")

        def per_loop(kinds):
            return sum(c[0] in kinds for n, c in chunks if FIRST <= n < FIRST + SLOTS)

        def times(it, each, value):
            return it * each + value

        def exists(n):
            return n < HEADS_ALL

        def parity(n):
            return n // HEADS % PER_LOOP

        def slots(engine, slot):
            for n in range(FIRST):
                slot(0, n)
            with engine.Fori(0, LOOPS - 1) as it:
                for n in range(FIRST, FIRST + SLOTS):
                    slot(it, n)
            for n in range(FIRST + SLOTS * (LOOPS - 1), LAST):
                slot(0, n)

        rows = "b (t p) c -> b p t c"
        x_src = x_in.rearrange(rows, p=P)
        x_dst = x_out.rearrange(rows, p=P)
        adj_src = adj_t.rearrange(rows, p=P)

        with nc.Block() as block:
            @block.sync
            def _(sync):
                def load(b, source):
                    sync.dma_start(x_sb[:, b], x_src[source]).then_inc(x_loaded[b], 16)
                    sync.dma_start(adj_sb[:, b], adj_src[source]).then_inc(adj_loaded[b], 16)

                for b in range(PER_LOOP):
                    load(b, b)
                    sync.dma_start(res[:, b], x_src[b]).then_inc(res_loaded[b], 16)
                with sync.Fori(0, LOOPS - 1) as it:
                    for b in range(PER_LOOP):
                        own_wait(sync, normed_done, times(it, PER_LOOP, b + 1), passed)
                        own_wait(sync, masked, times(it, PER_LOOP * HEADS * RT, (b + 1) * HEADS * RT), passed)
                        load(b, it * PER_LOOP + (b + PER_LOOP))
                        own_wait(sync, added, times(it, PER_LOOP * 2, 2 * b + 2), passed)
                        sync.dma_start(x_dst[it * PER_LOOP + b], res[:, b]).then_inc(stored[b], 16)
                        own_wait(sync, stored[b], times(it, 16, 16), passed)
                        sync.dma_start(res[:, b], x_src[it * PER_LOOP + (b + PER_LOOP)]).then_inc(res_loaded[b], 16)
                for b in range(PER_LOOP):
                    sync.wait_ge(added, 2 * (BATCHES - PER_LOOP + b + 1))
                    sync.dma_start(x_dst[BATCHES - PER_LOOP + b], res[:, b]).then_inc(stored[b], 16)
                for b in range(PER_LOOP):
                    sync.wait_ge(stored[b], 16 * LOOPS)

            @block.gpsimd
            def _(pool):
                def rstd_step(it, b):
                    own_wait(pool, mean_var_done, times(it, PER_LOOP, b + 1), passed)
                    nc.gpsimd.tensor_scalar(var_eps[:], mean_var[:, :, 1], EPS, 1.0, ALU.add, ALU.mult).then_inc(var_eps_done, 1)
                    pool.wait_ge(var_eps_done, times(it, PER_LOOP, b + 1))
                    nc.gpsimd.tensor_tensor(rstd[:], var_eps[:], minus_half[:], ALU.pow).then_inc(rstd_done, 1)

                def side(it, n, c):
                    kind, part, to = c
                    acted = times(it, per_loop(BY_ACT), before(BY_ACT, n, c) + 1)
                    if kind == "w":
                        pool.wait_ge(front_act, acted)
                        at = slice(2 * part, 2 * part + 2)
                        nc.gpsimd.tensor_tensor(wh[LO][:, to % 2, at], wh_full[:, at], exact(wh[HI][:, to % 2, at]),
                                                ALU.subtract).then_inc(wh_ready, 1)
                    elif kind == "gate":
                        pool.wait_ge(front_act, acted)
                        nc.gpsimd.tensor_tensor(hf_full[:, part], hf_full[:, part], ha_full[:, part],
                                                ALU.subtract).then_inc(difference_done, 1)

                def tanh_rest(it, n, t):
                    pool.wait_ge(tanh_full, times(it, SLOTS * RT, n * RT + t + 1))
                    nc.gpsimd.tensor_tensor(a_sb[LO][:, t], a_full[:, t], exact(a_sb[HI][:, t]), ALU.subtract).then_inc(tanh_lo, 1)

                def slot(it, n):
                    if n % HEADS == 0 and exists(n + HEADS):
                        rstd_step(it, n // HEADS + 1)
                    work = side_work(n)
                    for t in range(RT):
                        if exists(n + 1):
                            tanh_rest(it, n + 1, t)
                        for c in work[t] if t else []:
                            side(it, n, c)

                rstd_step(0, 0)
                for c in side_work(-1)[0]:
                    side(0, -1, c)
                for t in range(RT):
                    tanh_rest(0, 0, t)
                slots(pool, slot)

            @block.scalar
            def _(act):
                def side(it, n, c):
                    kind, part, to = c
                    bank = front_ps[:, before(ALL, n, c) % 2]
                    done = times(it, per_loop(ALL), before(ALL, n, c) + 1)
                    if kind == "h":
                        act.wait_ge(front_done, done)
                        nc.scalar.activation(hT[HI][:, to % PER_LOOP, part], bank, ACT.Relu).then_inc(front_act, 1)
                    elif kind == "g":
                        act.wait_ge(front_done, done)
                        nc.scalar.activation(gT[HI][:, to % 2, part], bank, ACT.Identity,
                                             bias=g_bias[:, part, to % HEADS:to % HEADS + 1]).then_inc(front_act, 1)
                    elif kind == "w":
                        at = slice(2 * part, 2 * part + 2)
                        act.wait_ge(front_read, done)
                        nc.scalar.activation(wh[HI][:, to % 2, at], wh_full[:, at], ACT.Copy).then_inc(front_act, 1)
                    elif kind == "gate":
                        act.wait_ge(front_done, done)
                        nc.scalar.activation(gate[:, part], bank, ACT.Tanh, scale=0.5,
                                             bias=half_gate_bias[:, part:part + 1]).then_inc(front_act, 1)
                    elif kind == "hf":
                        act.wait_ge(front_done, done)
                        nc.scalar.activation(hf[HI][:, part], bank, ACT.Copy).then_inc(front_act, 1)

                def tanhs(it, n, t):
                    act.wait_ge(masked, times(it, SLOTS * RT, n * RT + t + 1))
                    nc.scalar.activation(a_sb[HI][:, t], a_full[:, t], ACT.Tanh).then_inc(tanh_hi, 1)
                    act.wait_ge(tanh_hi, times(it, SLOTS * RT, n * RT + t + 1))
                    nc.scalar.activation(a_full[:, t], a_full[:, t], ACT.Tanh).then_inc(tanh_full, 1)

                def slot(it, n):
                    work = side_work(n)
                    for c in work[0]:
                        side(it, n, c)
                    for t in range(RT):
                        if t == RT - 1 and exists(n):
                            act.wait_ge(hp_done, times(it, SLOTS, n + 1))
                            for i in range(CT):
                                nc.scalar.activation(hpT[HI][:, i], hp_ps[:, i], ACT.Relu).then_inc(hp_hi, 1)
                        if exists(n + 1):
                            tanhs(it, n + 1, t)
                        if t == 0 and n % HEADS == 0 and 0 < n <= HEADS_ALL:
                            act.wait_ge(ha_done, times(it, PER_LOOP, n // HEADS))
                            for i in range(CT):
                                nc.scalar.activation(ha_full[:, i], ha_ps[:, i], ACT.Copy)
                                nc.scalar.activation(ha[HI][:, i], ha_ps[:, i], ACT.Copy).then_inc(ha_hi, 1)
                        for c in work[t] if t else []:
                            side(it, n, c)

                for c in side_work(-1)[0]:
                    side(0, -1, c)
                for t in range(RT):
                    tanhs(0, 0, t)
                slots(act, slot)

            @block.vector
            def _(dve):
                def norm_first(it, b):
                    p = b % PER_LOOP
                    dve.wait_ge(x_loaded[p], times(it, 16, b // PER_LOOP * 16 + 16))
                    for q in range(RT):
                        step = nc.vector.bn_stats(stats[:, q], x_sb[:, p, q])
                    step.then_inc(stats_done, 1)
                    own_wait(dve, stats_done, times(it, PER_LOOP, b + 1), passed)
                    for q in range(RT):
                        step = nc.vector.bn_aggr(mean_var[:, q], stats[:, q])
                    step.then_inc(mean_var_done, 1)

                def norm_last(it, b):
                    dve.wait_ge(rstd_done, times(it, PER_LOOP, b + 1))
                    for q in range(RT):
                        step = nc.vector.tensor_scalar(normed_x[:, q], x_sb[:, b % PER_LOOP, q], mean_var[:, q, 0:1],
                                                       rstd[:, q:q + 1], ALU.subtract, ALU.mult)
                    step.then_inc(normed_done, 1)

                def side(it, n, c):
                    kind, part, to = c
                    bank = front_ps[:, before(ALL, n, c) % 2]
                    done = times(it, per_loop(ALL), before(ALL, n, c) + 1)
                    acted = times(it, per_loop(BY_ACT), before(BY_ACT, n, c) + 1)
                    if kind == "h":
                        dve.wait_ge(front_act, acted)
                        nc.vector.tensor_scalar(hT_full[:, part], bank, 0.0, None, ALU.max)
                        nc.vector.scalar_tensor_tensor(hT[LO][:, to % PER_LOOP, part], bank, 0.0,
                                                       exact(hT[HI][:, to % PER_LOOP, part]),
                                                       ALU.max, ALU.subtract).then_inc(front_read, 1)
                    elif kind == "s":
                        dve.wait_ge(front_done, done)
                        nc.vector.tensor_tensor(
                            s_sb[:, to % PER_LOOP], bank[:, 0:RT * HEADS].rearrange("p (t h) -> p t h", t=RT),
                            s_bias[:].unsqueeze(1).to_broadcast([P, RT, HEADS]), ALU.add).then_inc(front_read, 1)
                    elif kind == "g":
                        dve.wait_ge(front_act, acted)
                        nc.vector.scalar_tensor_tensor(
                            gT[LO][:, to % 2, part], bank, g_bias[:, part, to % HEADS:to % HEADS + 1],
                            exact(gT[HI][:, to % 2, part]), ALU.add, ALU.subtract).then_inc(front_read, 1)
                    elif kind == "w":
                        if to > 0:
                            dve.wait_ge(wh_ready, times(it, SLOTS * 2, 2 * to))
                        dve.wait_ge(front_done, done)
                        h = to % HEADS
                        bias = wh_bias[:, h * DIM:(h + 1) * DIM].unsqueeze(1).to_broadcast([P, 2, DIM])
                        nc.vector.tensor_tensor(wh_full[:, 2 * part:2 * part + 2], bank.rearrange("p (t o) -> p t o", t=2),
                                                bias, ALU.add).then_inc(front_read, 1)
                    elif kind == "gate":
                        dve.wait_ge(front_act, acted)
                        dve.sem_inc(front_read, 1)
                    elif kind == "back":
                        p, at = to % PER_LOOP, slice(2 * part, 2 * part + 2)
                        dve.wait_ge(front_done, done)
                        dve.wait_ge(res_loaded[p], times(it, 16, to // PER_LOOP * 16 + 16))
                        nc.vector.tensor_tensor(res[:, p, at], bank.rearrange("p (t o) -> p t o", t=2), res[:, p, at],
                                                ALU.add).then_inc(added, 1)
                        dve.wait_ge(added, times(it, PER_LOOP * 2, to * 2 + part + 1))
                        dve.sem_inc(front_read, 1)
                    elif kind == "hf":
                        dve.wait_ge(front_act, acted)
                        nc.vector.tensor_tensor(hf[LO][:, part], bank, exact(hf[HI][:, part]), ALU.subtract)
                        nc.vector.tensor_copy(hf_full[:, part], bank).then_inc(front_read, 1)

                def mix_gate(it, b):
                    for part in range(CT):
                        dve.wait_ge(difference_done, times(it, PER_LOOP * CT, b * CT + part + 1))
                        nc.vector.scalar_tensor_tensor(gate[:, part], gate[:, part], 1.0, hf_full[:, part],
                                                       ALU.add, ALU.mult).then_inc(opened, 1)
                    for part in range(CT):
                        dve.wait_ge(opened, times(it, PER_LOOP * CT, b * CT + part + 1))
                        nc.vector.scalar_tensor_tensor(gate[:, part], gate[:, part], 0.5, ha_full[:, part],
                                                       ALU.mult, ALU.add).then_inc(mixed, 1)

                def mask_scores(it, n, t):
                    p, h = parity(n), n % HEADS
                    if h == 0 and t == 0:
                        dve.wait_ge(adj_loaded[p], times(it, 16, n // HEADS // PER_LOOP * 16 + 16))
                    if n > 0:
                        dve.wait_ge(tanh_lo, times(it, SLOTS * RT, (n - 1) * RT + t + 1))
                    dve.wait_ge(scores_done, times(it, SLOTS * RT, n * RT + t + 1))
                    nc.vector.scalar_tensor_tensor(a_full[:, t], scores_ps[:, t % 2], s_sb[:, p, t, h:h + 1], adj_sb[:, p, t],
                                                   ALU.add, ALU.mult).then_inc(masked, 1)

                def slot(it, n):
                    ahead = n % HEADS == 0 and exists(n + HEADS)
                    work = side_work(n)
                    for c in work[0]:
                        side(it, n, c)
                    if ahead:
                        norm_first(it, n // HEADS + 1)
                    for t in range(RT):
                        if t == RT - 1 and exists(n):
                            for i in range(CT):
                                dve.wait_ge(hp_hi, times(it, SLOTS * CT, n * CT + i + 1))
                                nc.vector.scalar_tensor_tensor(hpT[LO][:, i], hp_ps[:, i], 0.0, exact(hpT[HI][:, i]),
                                                               ALU.max, ALU.subtract).then_inc(hp_lo, 1)
                        if exists(n + 1):
                            mask_scores(it, n + 1, t)
                        if t == 1 and ahead:
                            norm_last(it, n // HEADS + 1)
                        if t == 0 and n % HEADS == 0 and 0 < n <= HEADS_ALL:
                            for i in range(CT):
                                dve.wait_ge(ha_hi, times(it, PER_LOOP * CT, (n // HEADS - 1) * CT + i + 1))
                                nc.vector.tensor_tensor(ha[LO][:, i], ha_ps[:, i], exact(ha[HI][:, i]), ALU.subtract).then_inc(ha_lo, 1)
                        if t == 0 and n % HEADS == 1 and n > HEADS:
                            mix_gate(it, n // HEADS - 1)
                        for c in work[t] if t else []:
                            side(it, n, c)

                norm_first(0, 0)
                norm_last(0, 0)
                for c in side_work(-1)[0]:
                    side(0, -1, c)
                for t in range(RT):
                    mask_scores(0, 0, t)
                slots(dve, slot)

            @block.tensor
            def _(pe):
                def three_passes(out, pairs):
                    for n, (i, j) in enumerate(PASSES):
                        for m, (left, right) in enumerate(pairs):
                            mm = nc.tensor.matmul(out, left[i], right[j], start=(n + m == 0),
                                                  stop=(n == 2 and m == len(pairs) - 1))
                    return mm

                def halves(pair, *at):
                    return [x[(slice(None), *at)] for x in pair]

                def side(it, n, c):
                    kind, part, to = c
                    number = before(ALL, n, c)
                    bank = front_ps[:, number % 2]
                    if number >= 2:
                        pe.wait_ge(front_read, times(it, per_loop(ALL), number - 1))
                    at = slice(part * P, (part + 1) * P)
                    b = to % PER_LOOP if kind not in "gw" else parity(to)
                    if kind == "h":
                        if part == 0:
                            pe.wait_ge(normed_done, times(it, PER_LOOP, to + 1))
                        for q in range(RT):
                            mm = nc.tensor.transpose(bank[:, q * P:(q + 1) * P], normed_x[:, q, at], ident[:])
                    elif kind == "s":
                        pe.wait_ge(front_read, times(it, per_loop(ALL), through(ALL, to, "h", 1)))
                        for q in range(RT):
                            for t in range(CT):
                                mm = nc.tensor.matmul(bank[:, q * HEADS:(q + 1) * HEADS], hT_full[:, t, q * P:(q + 1) * P],
                                                      s_weights[:, t], start=(t == 0), stop=(t == CT - 1))
                    elif kind == "g":
                        if to % HEADS == 0 and part == 0:
                            pe.wait_ge(front_read, times(it, per_loop(ALL), through(ALL, to // HEADS, "h", 1)))
                        mm = three_passes(bank, [(halves(gw_sb, t, to % HEADS, at), halves(hT, b, t)) for t in range(CT)])
                    elif kind == "w":
                        h = to % HEADS
                        for m in range(2):
                            q = 2 * part + m
                            mm = three_passes(bank[:, m * DIM:(m + 1) * DIM], [
                                (halves(hT, b, t, slice(q * P, (q + 1) * P)), halves(w_sb, t, slice(h * DIM, (h + 1) * DIM)))
                                for t in range(CT)])
                    elif kind == "hf":
                        mm = three_passes(bank, [(halves(small_sb, FC, t, at), halves(hT, b, t)) for t in range(CT)])
                    elif kind == "gate":
                        if part == 0:
                            pe.wait_ge(ha_lo, times(it, PER_LOOP * CT, (to + 1) * CT))
                            pe.wait_ge(front_read, times(it, per_loop(ALL), through(ALL, to, "hf", 1)))
                        mm = three_passes(bank, [(halves(small_sb, G1, t, at), halves(hf, t)) for t in range(CT)]
                                          + [(halves(small_sb, G2, t, at), halves(ha, t)) for t in range(CT)])
                    elif kind == "back":
                        pe.wait_ge(mixed, times(it, PER_LOOP * CT, (to + 1) * CT))
                        for m in range(2):
                            q = 2 * part + m
                            for t in range(CT):
                                mm = nc.tensor.transpose(bank[:, m * DIM + t * P:m * DIM + (t + 1) * P],
                                                         gate[:, t, q * P:(q + 1) * P], ident[:])
                    mm.then_inc(front_done, 1)

                def scores(it, n, t):
                    if t == 0:
                        pe.wait_ge(front_read, times(it, per_loop(ALL), through(ALL, n, "g", 1)))
                    tile = n * RT + t
                    if tile >= 2:
                        pe.wait_ge(masked, times(it, SLOTS * RT, tile - 1))
                    three_passes(scores_ps[:, t % 2], [
                        (halves(gT, n % 2, i, slice(t * P, (t + 1) * P)), halves(hT, parity(n), i)) for i in range(CT)
                    ]).then_inc(scores_done, 1)

                def times_wh(it, n, t):
                    if t == 0:
                        pe.wait_ge(wh_ready, times(it, SLOTS * 2, 2 * n + 2))
                        if n > 0:
                            pe.wait_ge(hp_lo, times(it, SLOTS * CT, n * CT))
                    pe.wait_ge(tanh_lo, times(it, SLOTS * RT, n * RT + t + 1))
                    for o in range(CT):
                        for m, (i, j) in enumerate(PASSES):
                            mm = nc.tensor.matmul(hp_ps[:, o], wh[i][:, n % 2, t, o * P:(o + 1) * P], a_sb[j][:, t],
                                                  start=(t == 0 and m == 0), stop=(t == RT - 1 and m == 2))
                    if t == RT - 1:
                        mm.then_inc(hp_done, 1)

                def mix_head(it, n):
                    h = n % HEADS
                    pe.wait_ge(hp_lo, times(it, SLOTS * CT, (n + 1) * CT))
                    if h == 0 and n > 0:
                        pe.wait_ge(ha_lo, times(it, PER_LOOP * CT, n // HEADS * CT))
                    for o in range(CT):
                        for m, (i, j) in enumerate(PASSES):
                            for t in range(CT):
                                mm = nc.tensor.matmul(
                                    ha_ps[:, o], mix_sb[i][:, h * CT + t, o * P:(o + 1) * P], hpT[j][:, t],
                                    start=(h == 0 and m + t == 0), stop=(h == HEADS - 1 and m == 2 and t == CT - 1))
                    if h == HEADS - 1:
                        mm.then_inc(ha_done, 1)

                def slot(it, n):
                    work = side_work(n)
                    for c in work[0]:
                        side(it, n, c)
                    for t in range(RT):
                        if exists(n):
                            times_wh(it, n, t)
                        if exists(n + 1):
                            scores(it, n + 1, t)
                        if t == 0 and n > 0 and exists(n - 1):
                            mix_head(it, n - 1)
                        for c in work[t] if t else []:
                            side(it, n, c)

                for c in side_work(-1)[0]:
                    side(0, -1, c)
                for t in range(RT):
                    scores(0, 0, t)
                slots(pe, slot)


def network(nc, x, adj, adj_t, l0, l1, l2, l3, out):
    x1, x2, x3 = (nc.dram_tensor(f"x{n}", x.shape, F32).ap() for n in (1, 2, 3))
    attention_layer(nc, "L0", x, x1, adj, *l0, heads=4)
    attention_layer(nc, "L1", x1, x2, adj, *l1[:3], heads=8, gamma=l1[3], beta=l1[4])
    gated_layer(nc, "L2", x2, x3, adj_t, *l2)
    attention_layer(nc, "L3", x3, out, adj, *l3, heads=4)


def kernel(**inputs):
    import numpy as _np
    import concourse.bacc as _bacc
    from concourse import mybir as _mybir
    from concourse.bass_utils import run_bass_kernel_spmd as _run

    nc = _bacc.Bacc("TRN2", target_bir_lowering=False, num_devices=1)
    arrays = {}
    inputs = {name: _np.asarray(a) for name, a in inputs.items()}

    def given(name, array):
        arrays[name] = _np.ascontiguousarray(array)
        dtype = _mybir.dt.from_np(arrays[name].dtype)
        return nc.dram_tensor(name, arrays[name].shape, dtype, kind="ExternalInput").ap()

    x = given("x", inputs["x"])
    adj = given("adj", inputs["adj"])
    adj_t = given("adj_t", inputs["adj"].transpose(0, 2, 1))

    def square_layer(n):
        w = _np.stack([inputs[f"L{n}_gnn_W{c}"] for c in "qkv"], axis=1)
        return given(f"L{n}_qkv", w), given(f"L{n}_Wo", inputs[f"L{n}_gnn_Wo"]), given(f"L{n}_bo", inputs[f"L{n}_gnn_bo"])

    w_qkv = inputs["L1_gnn_w_qkv"]
    l1 = (
        given("L1_qkv", w_qkv.reshape(3, -1, w_qkv.shape[1]).transpose(2, 0, 1)),
        given("L1_w_out", inputs["L1_gnn_w_out"].T), given("L1_b_out", inputs["L1_gnn_b_out"]),
        given("L1_gamma", inputs["L1_gnn_gamma"]), given("L1_beta", inputs["L1_gnn_beta"]),
    )
    w = inputs["L2_gnn_W"]
    l2 = (
        given("L2_W_rows", w.transpose(1, 0, 2)), given("L2_W_cols", w.transpose(2, 0, 1).reshape(w.shape[2], -1)),
        given("L2_attn_t", inputs["L2_gnn_attn"].transpose(2, 0, 1)), given("L2_bW", inputs["L2_gnn_bW"]),
        given("L2_A_w_t", inputs["L2_gnn_A_w"].T),
        tuple(given(f"L2_{c}_t", inputs[f"L2_gnn_{c}_w"].T) for c in ("fc", "g1", "g2")),
        given("L2_gbias", inputs["L2_gnn_gbias"]),
    )
    out = nc.dram_tensor("out", x.shape, _mybir.dt.float32, kind="ExternalOutput").ap()
    network(nc, x, adj, adj_t, square_layer(0), l1, l2, square_layer(3), out)
    r = _run(nc, [arrays], core_ids=[0])
    return r.results[0]["out"]
```
